# Optimizing a Trainium2 kernel written in Bass

```python
import numpy as np
import jax
import jax.numpy as jnp

def _softmax(x, axis=-1):
    return jax.nn.softmax(x, axis=axis)

def _gelu(x):
    return jax.nn.gelu(x, approximate=True)

def _silu(x):
    return jax.nn.silu(x)

def _sigmoid(x):
    return jax.nn.sigmoid(x)

def _layernorm(x, axis=-1, eps=1e-05):
    m = jnp.mean(x, axis=axis, keepdims=True)
    v = jnp.var(x, axis=axis, keepdims=True)
    return (x - m) / jnp.sqrt(v + eps)

def _scatter_add(tgt, idx, src, axis=0):
    return tgt.at[idx].add(src)

def _segment_sum(src, seg, n):
    return jax.ops.segment_sum(src, seg, n)
kernel_name = 'mk_flamingo_gated_d4_seqx_r8_630668'

def setup_inputs(seed: int=0):
    np.random.seed(seed)
    _w = jnp.asarray

    def _rec_inputs():
        import jax
        import jax.numpy as jnp
        _rk = jax.random.key(seed)
        x = -0.0002928 + 1 * jax.random.normal(jax.random.fold_in(_rk, 1), (16, 64, 128), jnp.float32)
        _lenS = 64 - jax.random.randint(jax.random.fold_in(_rk, 7), (16,), 0, max(1, 64 // 4) + 1, jnp.int32)
        _lenS2 = 64 - jax.random.randint(jax.random.fold_in(_rk, 8), (16,), 0, max(1, 64 // 4) + 1, jnp.int32)
        _ctx_1024P = jax.random.normal(jax.random.fold_in(_rk, 11), (16, 16, 128), jnp.float32)
        _ctx_1024c = jax.random.dirichlet(jax.random.fold_in(_rk, 511), 0.3 * jnp.ones((16,), jnp.float32), (16, 64))
        _ctx_1024t = jnp.einsum('bsk,bkd->bsd', _ctx_1024c, _ctx_1024P)
        _ctx_1024t = _ctx_1024t * jax.lax.rsqrt(jnp.mean(jnp.square(_ctx_1024t)) + 1e-12) * 0.953939
        ctx_1024 = -1.39393e-06 + 0.999914 * (_ctx_1024t + 0.3 * jax.random.normal(jax.random.fold_in(_rk, 611), (16, 64, 128), jnp.float32))
        _validS = jnp.arange(64)[None, :] < _lenS[:, None]
        _validS2 = jnp.arange(64)[None, :] < _lenS2[:, None]
        _causal = jnp.tril(jnp.ones((64, 64), dtype=bool))
        mask_SxS2_if1 = jnp.where(jnp.ones((64, 64), dtype=bool), 1, 0).astype(jnp.int32)
        mask_BxSxS2_ik1 = jnp.where(jnp.broadcast_to(_validS2[:, None, :], (16, 64, 64)), 1, 0).astype(jnp.int32)
        _g = jax.random.normal(jax.random.fold_in(_rk, 9001), (2, 4), jnp.float32)
        _g = jnp.sign(_g) * jnp.maximum(jnp.abs(_g), 1.0) + (_g == 0) * 1.0
        g_xattn = _g[0]
        g_ffn = _g[1]
        return (x, ctx_1024, mask_SxS2_if1, mask_BxSxS2_ik1, g_xattn, g_ffn)
    x, ctx_1024, mask_SxS2_if1, mask_BxSxS2_ik1, g_xattn, g_ffn = _rec_inputs()

    def _L0_xattn_setup():
        import jax, jax.numpy as jnp
        import numpy as np
        B, S, D = (2, 256, 128)
        H = 16
        DK = D // H
        SCALE = 1.0 / np.sqrt(DK)
        key = jax.random.key(seed)
        ks = jax.random.split(key, 11)
        std = 1.0 / np.sqrt(D)
        return {'query': jax.random.normal(ks[0], (B, S, D), jnp.float32), 'key': jax.random.normal(ks[1], (B, S, D), jnp.float32), 'value': jax.random.normal(ks[2], (B, S, D), jnp.float32), 'Wq': jax.random.normal(ks[3], (D, H * DK), jnp.float32) * std, 'bq': jnp.zeros((H * DK,), jnp.float32), 'Wk': jax.random.normal(ks[4], (D, H * DK), jnp.float32) * std, 'bk': jnp.zeros((H * DK,), jnp.float32), 'Wv': jax.random.normal(ks[5], (D, H * DK), jnp.float32) * std, 'bv': jnp.zeros((H * DK,), jnp.float32), 'Wo': jax.random.normal(ks[6], (D, D), jnp.float32) * std, 'bo': jnp.zeros((D,), jnp.float32)}
    _L0_xattn_all = _L0_xattn_setup()
    _L0_xattn_in = {k: v for k, v in _L0_xattn_all.items() if k in ('Wq', 'bq', 'Wk', 'bk', 'Wv', 'bv', 'Wo', 'bo')}
    del _L0_xattn_all

    def _L0_ffn_setup():
        import jax, jax.numpy as jnp
        import numpy as np
        B, S, D, E, F = (2, 256, 128, 14, 256)
        key = jax.random.key(seed)
        k = jax.random.split(key, 4)
        h = jax.random.normal(k[0], (B, S, D), dtype=jnp.float32)
        router_w = jax.random.normal(k[1], (D, E), dtype=jnp.float32) * 0.02
        w1 = jax.random.uniform(k[2], (E, D, F), dtype=jnp.float32, minval=-1.0, maxval=1.0) * float(np.sqrt(6.0 / D))
        w2 = jax.random.uniform(k[3], (E, F, D), dtype=jnp.float32, minval=-1.0, maxval=1.0) * float(np.sqrt(6.0 / F))
        b1 = jnp.zeros((E, F), dtype=jnp.float32)
        b2 = jnp.zeros((E, D), dtype=jnp.float32)
        return {'h': h, 'router_w': router_w, 'w1': w1, 'b1': b1, 'w2': w2, 'b2': b2}
    _L0_ffn_all = _L0_ffn_setup()
    _L0_ffn_in = {k: v for k, v in _L0_ffn_all.items() if k in ('router_w', 'w1', 'b1', 'w2', 'b2')}
    del _L0_ffn_all

    def _L1_xattn_setup():
        import jax, jax.numpy as jnp
        import numpy as np
        E = 128
        H = 16
        D = E // H
        key = jax.random.key(seed)
        ks = jax.random.split(key, 12)
        N, S, T = (4, 256, 256)
        inp = {'query': jax.random.normal(ks[0], (N, S, E), jnp.float32), 'key': jax.random.normal(ks[1], (N, T, E), jnp.float32), 'value': jax.random.normal(ks[2], (N, T, E), jnp.float32), 'attn_mask': jnp.ones((S, T), jnp.int32), 'Wq': jax.random.normal(ks[3], (E, E), jnp.float32) / np.sqrt(E), 'bq': jax.random.normal(ks[4], (E,), jnp.float32) * 0.01, 'Wk': jax.random.normal(ks[5], (E, E), jnp.float32) / np.sqrt(E), 'bk': jax.random.normal(ks[6], (E,), jnp.float32) * 0.01, 'Wv': jax.random.normal(ks[7], (E, E), jnp.float32) / np.sqrt(E), 'bv': jax.random.normal(ks[8], (E,), jnp.float32) * 0.01, 'Wo': jax.random.normal(ks[9], (E, E), jnp.float32) / np.sqrt(E), 'bo': jax.random.normal(ks[10], (E,), jnp.float32) * 0.01}
        return inp
    _L1_xattn_all = _L1_xattn_setup()
    _L1_xattn_in = {k: v for k, v in _L1_xattn_all.items() if k in ('Wq', 'bq', 'Wk', 'bk', 'Wv', 'bv', 'Wo', 'bo')}
    del _L1_xattn_all

    def _L1_ffn_setup():
        import jax, jax.numpy as jnp
        import numpy as np
        DIM = 128

        def _reference_tuple_inner(x, W_r, W_k, W_v, mu_r, mu_k):
            B, T, C = x.shape
            x_prev = jnp.concatenate([jnp.zeros((B, 1, C), x.dtype), x[:, :-1, :]], axis=1)
            xr = mu_r * x + (1.0 - mu_r) * x_prev
            xk = mu_k * x + (1.0 - mu_k) * x_prev
            r = jax.nn.sigmoid(jnp.einsum('btc,dc->btd', xr, W_r))
            k = jnp.einsum('btc,dc->btd', xk, W_k)
            k_act = jnp.square(jax.nn.relu(k))
            out = r * jnp.einsum('btc,dc->btd', k_act, W_v)
            new_state = x[:, -1, :]
            return (out, new_state)
        key = jax.random.key(seed)
        ks = jax.random.split(key, 6)
        B, T, C = (8, 256, DIM)
        x = jax.random.normal(ks[0], (B, T, C), dtype=jnp.float32)
        s = 1.0 / np.sqrt(C)
        W_r = jax.random.uniform(ks[1], (C, C), jnp.float32, -s, s)
        W_k = jax.random.uniform(ks[2], (C, C), jnp.float32, -s, s)
        W_v = jax.random.uniform(ks[3], (C, C), jnp.float32, -s, s)
        mu_r = jax.random.uniform(ks[4], (C,), jnp.float32)
        mu_k = jax.random.uniform(ks[5], (C,), jnp.float32)
        return {'x': x, 'W_r': W_r, 'W_k': W_k, 'W_v': W_v, 'mu_r': mu_r, 'mu_k': mu_k}
    _L1_ffn_all = _L1_ffn_setup()
    _L1_ffn_in = {k: v for k, v in _L1_ffn_all.items() if k in ('W_r', 'W_k', 'W_v', 'mu_r', 'mu_k')}
    del _L1_ffn_all

    def _L2_xattn_setup():
        import jax, jax.numpy as jnp
        import numpy as np
        D_MODEL = 128
        N_HEAD = 16
        B, S = (2, 256)
        key = jax.random.key(seed)
        ks = jax.random.split(key, 12)
        scale = 1.0 / np.sqrt(D_MODEL)
        inp = {'q': jax.random.normal(ks[0], (B, S, D_MODEL), jnp.float32), 'k': jax.random.normal(ks[1], (B, S, D_MODEL), jnp.float32), 'v': jax.random.normal(ks[2], (B, S, D_MODEL), jnp.float32), 'mask': jax.random.randint(ks[3], (B, S, S), 0, 2, jnp.int32), 'Wq': jax.random.normal(ks[4], (D_MODEL, D_MODEL), jnp.float32) * scale, 'bq': jnp.zeros((D_MODEL,), jnp.float32), 'Wk': jax.random.normal(ks[5], (D_MODEL, D_MODEL), jnp.float32) * scale, 'bk': jnp.zeros((D_MODEL,), jnp.float32), 'Wv': jax.random.normal(ks[6], (D_MODEL, D_MODEL), jnp.float32) * scale, 'bv': jnp.zeros((D_MODEL,), jnp.float32), 'Wo': jax.random.normal(ks[7], (D_MODEL, D_MODEL), jnp.float32) * scale, 'bo': jnp.zeros((D_MODEL,), jnp.float32)}
        return inp
    _L2_xattn_all = _L2_xattn_setup()
    _L2_xattn_in = {k: v for k, v in _L2_xattn_all.items() if k in ('Wq', 'bq', 'Wk', 'bk', 'Wv', 'bv', 'Wo', 'bo')}
    del _L2_xattn_all

    def _L2_ffn_setup():
        import jax, jax.numpy as jnp
        import numpy as np
        DIM = 128
        HIDDEN = 512
        E = 8
        B, S = (2, 512)
        key = jax.random.key(seed)
        ks = jax.random.split(key, 8)
        sd = 1.0 / np.sqrt(DIM)
        sh = 1.0 / np.sqrt(HIDDEN)
        return {'x': jax.random.normal(ks[0], (B, S, DIM), dtype=jnp.float32), 'router_w': jax.random.uniform(ks[1], (DIM, E), jnp.float32, -sd, sd), 'router_b': jax.random.uniform(ks[2], (E,), jnp.float32, -sd, sd), 'w1': jax.random.uniform(ks[3], (E, DIM, 2 * HIDDEN), jnp.float32, -sd, sd), 'b1': jax.random.uniform(ks[4], (E, 2 * HIDDEN), jnp.float32, -sd, sd), 'w2': jax.random.uniform(ks[5], (E, HIDDEN, DIM), jnp.float32, -sh, sh), 'b2': jax.random.uniform(ks[6], (E, DIM), jnp.float32, -sh, sh)}
    _L2_ffn_all = _L2_ffn_setup()
    _L2_ffn_in = {k: v for k, v in _L2_ffn_all.items() if k in ('router_w', 'router_b', 'w1', 'b1', 'w2', 'b2')}
    del _L2_ffn_all

    def _L3_xattn_setup():
        import jax, jax.numpy as jnp
        import numpy as np
        N_HEAD = 16
        key = jax.random.key(seed)
        ks = jax.random.split(key, 5)
        b, l, d = (4, 256, 128)
        dh = d // N_HEAD
        return {'q': jax.random.normal(ks[0], (b, l, d), dtype=jnp.float32), 'kv': jax.random.normal(ks[1], (b, l, d), dtype=jnp.float32), 'Wq': jax.random.normal(ks[2], (d, d), dtype=jnp.float32) * 0.02, 'Wkv': jax.random.normal(ks[3], (2 * dh, d), dtype=jnp.float32) * 0.02, 'Wc': jax.random.normal(ks[4], (d, d), dtype=jnp.float32) * 0.02}
    _L3_xattn_all = _L3_xattn_setup()
    _L3_xattn_in = {k: v for k, v in _L3_xattn_all.items() if k in ('Wq', 'Wkv', 'Wc')}
    del _L3_xattn_all

    def _L3_ffn_setup():
        import jax, jax.numpy as jnp
        import numpy as np
        from jax import lax
        DIM = 128
        N_EXPERTS = 16
        TOPK = 4
        N_GROUPS = 4
        TOPK_GROUPS = 2
        ROUTE_SCALE = 1.0
        INTER = 64
        SHARED_INTER = 2 * INTER

        def _gate(x, gate_w):
            T = x.shape[0]
            logits = x @ gate_w.T
            scores = jax.nn.softmax(logits.astype(jnp.float32), axis=-1)
            original_scores = scores
            g = scores.reshape(T, N_GROUPS, N_EXPERTS // N_GROUPS)
            group_scores = g.max(axis=-1)
            _, gidx = lax.top_k(group_scores, TOPK_GROUPS)
            gmask = jnp.zeros_like(group_scores).at[jnp.arange(T)[:, None], gidx].set(1.0)
            masked = (g * gmask[..., None]).reshape(T, N_EXPERTS)
            _, indices = lax.top_k(masked, TOPK)
            weights = jnp.take_along_axis(original_scores, indices, axis=1)
            weights = weights * ROUTE_SCALE
            return (weights.astype(x.dtype), indices)
        key = jax.random.key(seed)
        ks = jax.random.split(key, 8)
        s = lambda fan_in: 1.0 / np.sqrt(fan_in)
        return {'x': jax.random.normal(ks[0], (2, 128, DIM), dtype=jnp.float32), 'gate_w': jax.random.normal(ks[1], (N_EXPERTS, DIM), dtype=jnp.float32) * s(DIM), 'w1': jax.random.normal(ks[2], (N_EXPERTS, DIM, INTER), dtype=jnp.float32) * s(DIM), 'w2': jax.random.normal(ks[3], (N_EXPERTS, INTER, DIM), dtype=jnp.float32) * s(INTER), 'w3': jax.random.normal(ks[4], (N_EXPERTS, DIM, INTER), dtype=jnp.float32) * s(DIM), 'ws1': jax.random.normal(ks[5], (DIM, SHARED_INTER), dtype=jnp.float32) * s(DIM), 'ws2': jax.random.normal(ks[6], (SHARED_INTER, DIM), dtype=jnp.float32) * s(SHARED_INTER), 'ws3': jax.random.normal(ks[7], (DIM, SHARED_INTER), dtype=jnp.float32) * s(DIM)}
    _L3_ffn_all = _L3_ffn_setup()
    _L3_ffn_in = {k: v for k, v in _L3_ffn_all.items() if k in ('gate_w', 'w1', 'w2', 'w3', 'ws1', 'ws2', 'ws3')}
    del _L3_ffn_all
    return {'x': x, 'ctx_1024': ctx_1024, 'mask_SxS2_if1': mask_SxS2_if1, 'mask_BxSxS2_ik1': mask_BxSxS2_ik1, 'g_xattn': g_xattn, 'g_ffn': g_ffn, 'L0_xattn_Wq': _L0_xattn_in['Wq'], 'L0_xattn_bq': _L0_xattn_in['bq'], 'L0_xattn_Wk': _L0_xattn_in['Wk'], 'L0_xattn_bk': _L0_xattn_in['bk'], 'L0_xattn_Wv': _L0_xattn_in['Wv'], 'L0_xattn_bv': _L0_xattn_in['bv'], 'L0_xattn_Wo': _L0_xattn_in['Wo'], 'L0_xattn_bo': _L0_xattn_in['bo'], 'L0_ffn_router_w': _L0_ffn_in['router_w'], 'L0_ffn_w1': _L0_ffn_in['w1'], 'L0_ffn_b1': _L0_ffn_in['b1'], 'L0_ffn_w2': _L0_ffn_in['w2'], 'L0_ffn_b2': _L0_ffn_in['b2'], 'L1_xattn_Wq': _L1_xattn_in['Wq'], 'L1_xattn_bq': _L1_xattn_in['bq'], 'L1_xattn_Wk': _L1_xattn_in['Wk'], 'L1_xattn_bk': _L1_xattn_in['bk'], 'L1_xattn_Wv': _L1_xattn_in['Wv'], 'L1_xattn_bv': _L1_xattn_in['bv'], 'L1_xattn_Wo': _L1_xattn_in['Wo'], 'L1_xattn_bo': _L1_xattn_in['bo'], 'L1_ffn_W_r': _L1_ffn_in['W_r'], 'L1_ffn_W_k': _L1_ffn_in['W_k'], 'L1_ffn_W_v': _L1_ffn_in['W_v'], 'L1_ffn_mu_r': _L1_ffn_in['mu_r'], 'L1_ffn_mu_k': _L1_ffn_in['mu_k'], 'L2_xattn_Wq': _L2_xattn_in['Wq'], 'L2_xattn_bq': _L2_xattn_in['bq'], 'L2_xattn_Wk': _L2_xattn_in['Wk'], 'L2_xattn_bk': _L2_xattn_in['bk'], 'L2_xattn_Wv': _L2_xattn_in['Wv'], 'L2_xattn_bv': _L2_xattn_in['bv'], 'L2_xattn_Wo': _L2_xattn_in['Wo'], 'L2_xattn_bo': _L2_xattn_in['bo'], 'L2_ffn_router_w': _L2_ffn_in['router_w'], 'L2_ffn_router_b': _L2_ffn_in['router_b'], 'L2_ffn_w1': _L2_ffn_in['w1'], 'L2_ffn_b1': _L2_ffn_in['b1'], 'L2_ffn_w2': _L2_ffn_in['w2'], 'L2_ffn_b2': _L2_ffn_in['b2'], 'L3_xattn_Wq': _L3_xattn_in['Wq'], 'L3_xattn_Wkv': _L3_xattn_in['Wkv'], 'L3_xattn_Wc': _L3_xattn_in['Wc'], 'L3_ffn_gate_w': _L3_ffn_in['gate_w'], 'L3_ffn_w1': _L3_ffn_in['w1'], 'L3_ffn_w2': _L3_ffn_in['w2'], 'L3_ffn_w3': _L3_ffn_in['w3'], 'L3_ffn_ws1': _L3_ffn_in['ws1'], 'L3_ffn_ws2': _L3_ffn_in['ws2'], 'L3_ffn_ws3': _L3_ffn_in['ws3']}

def reference(x, ctx_1024, mask_SxS2_if1, mask_BxSxS2_ik1, g_xattn, g_ffn, L0_xattn_Wq, L0_xattn_bq, L0_xattn_Wk, L0_xattn_bk, L0_xattn_Wv, L0_xattn_bv, L0_xattn_Wo, L0_xattn_bo, L0_ffn_router_w, L0_ffn_w1, L0_ffn_b1, L0_ffn_w2, L0_ffn_b2, L1_xattn_Wq, L1_xattn_bq, L1_xattn_Wk, L1_xattn_bk, L1_xattn_Wv, L1_xattn_bv, L1_xattn_Wo, L1_xattn_bo, L1_ffn_W_r, L1_ffn_W_k, L1_ffn_W_v, L1_ffn_mu_r, L1_ffn_mu_k, L2_xattn_Wq, L2_xattn_bq, L2_xattn_Wk, L2_xattn_bk, L2_xattn_Wv, L2_xattn_bv, L2_xattn_Wo, L2_xattn_bo, L2_ffn_router_w, L2_ffn_router_b, L2_ffn_w1, L2_ffn_b1, L2_ffn_w2, L2_ffn_b2, L3_xattn_Wq, L3_xattn_Wkv, L3_xattn_Wc, L3_ffn_gate_w, L3_ffn_w1, L3_ffn_w2, L3_ffn_w3, L3_ffn_ws1, L3_ffn_ws2, L3_ffn_ws3):
    import jax
    import jax.numpy as jnp

    def _L0_xattn_ref(query, key, value, Wq, bq, Wk, bk, Wv, bv, Wo, bo):
        import jax, jax.numpy as jnp
        import numpy as np
        B, S, D = (2, 256, 128)
        H = 16
        DK = D // H
        SCALE = 1.0 / np.sqrt(DK)
        b, s, _ = query.shape
        q = (query @ Wq + bq).reshape(b, s, H, DK)
        k = (key @ Wk + bk).reshape(b, s, H, DK)
        v = (value @ Wv + bv).reshape(b, s, H, DK)
        scores = jnp.einsum('bihd,bjhd->bijh', q, k) * SCALE
        attn = jax.nn.softmax(scores, axis=2)
        x = jnp.einsum('bijh,bjhd->bihd', attn, v).reshape(b, s, H * DK)
        return x @ Wo + bo

    def _L0_ffn_ref(h, router_w, w1, b1, w2, b2):
        import jax, jax.numpy as jnp
        import numpy as np
        B, S, D, E, F = (2, 256, 128, 14, 256)
        Bb, Ss, Dd = h.shape
        x = h.reshape(-1, Dd)
        logits = x @ router_w
        assignments = jnp.argmax(logits, axis=-1)
        probs = jax.nn.softmax(logits, axis=-1)
        weights = jnp.take_along_axis(probs, assignments[:, None], axis=1)[:, 0]
        hid = jnp.einsum('nd,edf->nef', x, w1) + b1
        hid = jax.nn.gelu(hid, approximate=False)
        all_out = jnp.einsum('nef,efd->ned', hid, w2) + b2
        sel = jnp.take_along_axis(all_out, assignments[:, None, None], axis=1)[:, 0, :]
        moe_out = (sel * weights[:, None]).reshape(Bb, Ss, Dd)
        return moe_out

    def _L1_xattn_ref(query, key, value, attn_mask, Wq, bq, Wk, bk, Wv, bv, Wo, bo):
        import jax, jax.numpy as jnp
        import numpy as np
        E = 128
        H = 16
        D = E // H
        N, S, _ = query.shape
        T = key.shape[1]
        q = (query @ Wq.T + bq).reshape(N, S, H, D).transpose(0, 2, 1, 3)
        k = (key @ Wk.T + bk).reshape(N, T, H, D).transpose(0, 2, 1, 3)
        v = (value @ Wv.T + bv).reshape(N, T, H, D).transpose(0, 2, 1, 3)
        scores = jnp.einsum('nhsd,nhtd->nhst', q, k) / np.sqrt(D).astype(np.float32)
        scores = jnp.where(attn_mask == 0, jnp.float32(-jnp.inf), scores)
        attn = jax.nn.softmax(scores, axis=-1)
        out = jnp.einsum('nhst,nhtd->nhsd', attn, v)
        out = out.transpose(0, 2, 1, 3).reshape(N, S, E)
        return out @ Wo.T + bo

    def _L1_ffn_ref(x, W_r, W_k, W_v, mu_r, mu_k):
        import jax, jax.numpy as jnp
        import numpy as np
        DIM = 128

        def _reference_tuple_inner(x, W_r, W_k, W_v, mu_r, mu_k):
            B, T, C = x.shape
            x_prev = jnp.concatenate([jnp.zeros((B, 1, C), x.dtype), x[:, :-1, :]], axis=1)
            xr = mu_r * x + (1.0 - mu_r) * x_prev
            xk = mu_k * x + (1.0 - mu_k) * x_prev
            r = jax.nn.sigmoid(jnp.einsum('btc,dc->btd', xr, W_r))
            k = jnp.einsum('btc,dc->btd', xk, W_k)
            k_act = jnp.square(jax.nn.relu(k))
            out = r * jnp.einsum('btc,dc->btd', k_act, W_v)
            new_state = x[:, -1, :]
            return (out, new_state)
        return _reference_tuple_inner(x, W_r, W_k, W_v, mu_r, mu_k)[0]

    def _L2_xattn_ref(q, k, v, mask, Wq, bq, Wk, bk, Wv, bv, Wo, bo):
        import jax, jax.numpy as jnp
        import numpy as np
        D_MODEL = 128
        N_HEAD = 16
        B, S = (2, 256)
        b, s, d = q.shape
        dh = d // N_HEAD

        def proj_split(x, W, bias):
            y = x @ W.T + bias
            return y.reshape(b, s, N_HEAD, dh).transpose(0, 2, 1, 3)
        qh = proj_split(q, Wq, bq)
        kh = proj_split(k, Wk, bk)
        vh = proj_split(v, Wv, bv)
        score = jnp.einsum('bhqd,bhkd->bhqk', qh, kh) / jnp.sqrt(jnp.float32(dh))
        score = jnp.where(mask[:, None, :, :] == 0, jnp.float32(-10000.0), score)
        attn = jax.nn.softmax(score, axis=-1)
        out = jnp.einsum('bhqk,bhkd->bhqd', attn, vh)
        out = out.transpose(0, 2, 1, 3).reshape(b, s, d)
        return out @ Wo.T + bo

    def _L2_ffn_ref(x, router_w, router_b, w1, b1, w2, b2):
        import jax, jax.numpy as jnp
        import numpy as np
        DIM = 128
        HIDDEN = 512
        E = 8
        B, S = (2, 512)
        logits = jnp.einsum('bsd,de->bse', x, router_w) + router_b
        probs = jax.nn.softmax(logits, axis=-1)
        top1 = jnp.argmax(probs, axis=-1)
        out = jnp.zeros_like(x)
        for i in range(E):
            h = jnp.einsum('bsd,df->bsf', x, w1[i]) + b1[i]
            a, g = jnp.split(h, 2, axis=-1)
            y = jnp.einsum('bsh,hd->bsd', a * jax.nn.sigmoid(g), w2[i]) + b2[i]
            out = out + jnp.where((top1 == i)[..., None], y, 0.0)
        return out

    def _L3_xattn_ref(q, kv, Wq, Wkv, Wc):
        import jax, jax.numpy as jnp
        import numpy as np
        N_HEAD = 16
        b, l, d = q.shape
        h = N_HEAD
        dh = d // h
        qp = jnp.einsum('bld,ed->ble', q, Wq)
        scores = jnp.einsum('bld,bmd->blm', qp, kv)
        idx = jnp.argmax(scores, axis=-1)
        mem = jnp.take_along_axis(kv, idx[..., None], axis=1)
        mkv = jnp.einsum('bld,ed->ble', mem, Wkv)
        mk, mv = jnp.split(mkv, 2, axis=-1)
        qh = qp.reshape(b, l, h, dh).transpose(0, 2, 1, 3)
        scale = 1.0 / np.sqrt(dh).astype(np.float32)
        logits = jnp.einsum('bhld,bmd->bhlm', qh, mk) * scale
        attn = jax.nn.softmax(logits, axis=-1)
        out = jnp.einsum('bhlm,bmd->bhld', attn, mv)
        out = out.transpose(0, 2, 1, 3).reshape(b, l, d)
        return jnp.einsum('bld,ed->ble', out, Wc)

    def _L3_ffn_ref(x, gate_w, w1, w2, w3, ws1, ws2, ws3):
        import jax, jax.numpy as jnp
        import numpy as np
        from jax import lax
        DIM = 128
        N_EXPERTS = 16
        TOPK = 4
        N_GROUPS = 4
        TOPK_GROUPS = 2
        ROUTE_SCALE = 1.0
        INTER = 64
        SHARED_INTER = 2 * INTER

        def _gate(x, gate_w):
            T = x.shape[0]
            logits = x @ gate_w.T
            scores = jax.nn.softmax(logits.astype(jnp.float32), axis=-1)
            original_scores = scores
            g = scores.reshape(T, N_GROUPS, N_EXPERTS // N_GROUPS)
            group_scores = g.max(axis=-1)
            _, gidx = lax.top_k(group_scores, TOPK_GROUPS)
            gmask = jnp.zeros_like(group_scores).at[jnp.arange(T)[:, None], gidx].set(1.0)
            masked = (g * gmask[..., None]).reshape(T, N_EXPERTS)
            _, indices = lax.top_k(masked, TOPK)
            weights = jnp.take_along_axis(original_scores, indices, axis=1)
            weights = weights * ROUTE_SCALE
            return (weights.astype(x.dtype), indices)
        shape = x.shape
        xt = x.reshape(-1, DIM)
        T = xt.shape[0]
        weights, indices = _gate(xt, gate_w)
        c = jnp.zeros((T, N_EXPERTS), dtype=xt.dtype)
        c = c.at[jnp.arange(T)[:, None], indices].add(weights)
        h1 = jnp.einsum('td,edi->tei', xt, w1)
        h3 = jnp.einsum('td,edi->tei', xt, w3)
        a = jax.nn.silu(h1) * h3
        y = jnp.einsum('tei,eid,te->td', a, w2, c)
        z = jax.nn.silu(xt @ ws1) * (xt @ ws3) @ ws2
        return (y + z).reshape(shape)
    x = x + jnp.tanh(g_xattn[0]) * _L0_xattn_ref(_layernorm(x, axis=-1), ctx_1024, ctx_1024, L0_xattn_Wq, L0_xattn_bq, L0_xattn_Wk, L0_xattn_bk, L0_xattn_Wv, L0_xattn_bv, L0_xattn_Wo, L0_xattn_bo)
    x = x + jnp.tanh(g_ffn[0]) * _L0_ffn_ref(_layernorm(x, axis=-1), L0_ffn_router_w, L0_ffn_w1, L0_ffn_b1, L0_ffn_w2, L0_ffn_b2)
    x = x + jnp.tanh(g_xattn[1]) * _L1_xattn_ref(_layernorm(x, axis=-1), ctx_1024, ctx_1024, mask_SxS2_if1, L1_xattn_Wq, L1_xattn_bq, L1_xattn_Wk, L1_xattn_bk, L1_xattn_Wv, L1_xattn_bv, L1_xattn_Wo, L1_xattn_bo)
    x = x + jnp.tanh(g_ffn[1]) * _L1_ffn_ref(_layernorm(x, axis=-1), L1_ffn_W_r, L1_ffn_W_k, L1_ffn_W_v, L1_ffn_mu_r, L1_ffn_mu_k)
    x = x + jnp.tanh(g_xattn[2]) * _L2_xattn_ref(_layernorm(x, axis=-1), ctx_1024, ctx_1024, mask_BxSxS2_ik1, L2_xattn_Wq, L2_xattn_bq, L2_xattn_Wk, L2_xattn_bk, L2_xattn_Wv, L2_xattn_bv, L2_xattn_Wo, L2_xattn_bo)
    x = x + jnp.tanh(g_ffn[2]) * _L2_ffn_ref(_layernorm(x, axis=-1), L2_ffn_router_w, L2_ffn_router_b, L2_ffn_w1, L2_ffn_b1, L2_ffn_w2, L2_ffn_b2)
    x = x + jnp.tanh(g_xattn[3]) * _L3_xattn_ref(_layernorm(x, axis=-1), ctx_1024, L3_xattn_Wq, L3_xattn_Wkv, L3_xattn_Wc)
    x = x + jnp.tanh(g_ffn[3]) * _L3_ffn_ref(_layernorm(x, axis=-1), L3_ffn_gate_w, L3_ffn_w1, L3_ffn_w2, L3_ffn_w3, L3_ffn_ws1, L3_ffn_ws2, L3_ffn_ws3)
    return x

_drawn_inputs = setup_inputs


def setup_inputs(seed=0):
    import zlib

    import numpy as np

    out = dict(_drawn_inputs(seed))
    spreads = {'L0_xattn_bq': (0.0, 0.1),
     'L0_xattn_bk': (0.0, 2.0),
     'L0_xattn_bv': (0.0, 0.1),
     'L0_xattn_bo': (0.0, 0.1),
     'L0_ffn_b1': (0.0, 0.515),
     'L0_ffn_b2': (0.0, 0.407),
     'L2_xattn_bq': (0.0, 0.307),
     'L2_xattn_bk': (0.0, 2.0),
     'L2_xattn_bv': (0.0, 0.1),
     'L2_xattn_bo': (0.0, 0.1)}
    factors = {'g_ffn': 22.88,
     'L1_xattn_bq': 7.119,
     'L1_xattn_bk': 200.0,
     'L1_xattn_bv': 3.563,
     'L1_xattn_bo': 3.606,
     'L1_ffn_mu_r': 4.604,
     'L2_ffn_b1': 5.002,
     'L2_ffn_b2': 3.177,
     'L3_xattn_Wq': 53.128}
    for name, (base, spread) in spreads.items():
        noise = np.random.default_rng([zlib.crc32(name.encode()), seed]).standard_normal(out[name].shape)
        drawn = base * np.exp(spread * noise) if base else spread * noise
        out[name] = jnp.asarray(drawn.astype(out[name].dtype))
    for name, factor in factors.items():
        out[name] = (out[name] * factor).astype(out[name].dtype)
    return out
```

```python
from contextlib import ExitStack

import concourse.bass as bass
from concourse import mybir

F32 = mybir.dt.float32
BF16 = mybir.dt.bfloat16
I32 = mybir.dt.int32
ALU = mybir.AluOpType
ACT = mybir.ActivationFunctionType
AX = mybir.AxisListType.X

P = 128
B, S, D = 16, 64, 128
H, DH = 16, 8
LAYERS = 4
HALVES = 2
HB = B // HALVES
TOK = HB * S
PAIRS = HB // 2
HG = 8
HP = H // 2
SCALE = 1.0 / float(DH) ** 0.5
EPS = 1e-5
E0, F0 = 14, 256
E2, F2 = 8, 512
E3, F3 = 16, 64
C0 = E0 * F0 // P
C2 = E2 * F2 // P
C3 = E3 * F3 // P + 1
NH = 4
LAG = 2
STAGES = LAYERS * HALVES

COL = {}
for _n, _k in (("bq0", 1), ("bk0", 1), ("bv0", 1), ("bq1", 1), ("bk1", 1), ("bv1", 1), ("bq2", 1), ("bk2", 1),
               ("bv2", 1), ("mu_r", 1), ("mu_k", 1), ("b1_0", C0), ("b1_2", 2 * C2)):
    COL[_n] = (sum(v[1] for v in COL.values()), _k)
NCOL = sum(v[1] for v in COL.values())

W_DIRECT = ["Wq0", "Wk0", "Wv0", "Wo0"]
W_TURNED = ["Wq1", "Wk1", "Wv1", "Wo1", "W_r", "W_k", "W_v", "Wq2", "Wk2", "Wv2", "Wo2", "Wq3", "Wk3", "Wv3", "Wo3",
            "gate"]
SLOT = {n: i for i, n in enumerate(W_DIRECT + W_TURNED)}
TURN_GROUPS = [list(range(g, min(g + 4, len(W_TURNED)))) for g in range(0, len(W_TURNED), 4)]


def make_plan():

    def early_kv(n):
        return n < STAGES and n // HALVES < 3

    def attention(n):
        steps = [("attn_norm", n), ("queries", n)]
        if n // HALVES == 3:
            steps += [("retrieve", n), ("keys_values", n)]
        steps.append(("scores", n, 0))
        for p in range(PAIRS):
            steps.append(("turn_probs", n, p, 0))
            if p + 1 < PAIRS:
                steps.append(("scores", n, p + 1))
            steps += [("turn_probs", n, p, 1), ("attend", n, p)]
        if early_kv(n + 1):
            steps.append(("keys_values", n + 1))
        return steps + [("attn_out", n)]

    def feed_forward(n):
        layer = n // HALVES
        steps = [("ffn_norm", n)]
        if layer == 1:
            return steps + [("channel_mix", n), ("ffn_out", n)]
        steps.append(("route", n))
        chunks = {0: C0, 2: C2, 3: C3}[layer]
        for i in range(chunks + LAG):
            steps.append(("chunk", n, i))
        return steps + [("ffn_out", n)]

    def beside(a, b):
        out, j = [], 0
        for i, step in enumerate(a):
            out.append(step)
            while j < len(b) and (j + 1) * len(a) <= (i + 1) * len(b):
                out.append(b[j])
                j += 1
        return out + b[j:]

    plan = [("setup",), ("keys_values", 0)]
    plan += beside(attention(0), [("turn_weights", g) for g in range(len(TURN_GROUPS))])
    for n in range(STAGES):
        nxt = attention(n + 1) if n + 1 < STAGES else []
        cur = feed_forward(n)
        plan += beside(nxt, cur) if nxt else cur
    return plan


def flamingo_kernel(nc: bass.Bass, A: dict, out: bass.AP):
    PLAN = make_plan()
    with ExitStack() as ctx:
        def sb(name, shape, dt=F32):
            return ctx.enter_context(nc.sbuf_tensor(name, shape, dt))

        def sem(name):
            return ctx.enter_context(nc.semaphore(name))

        score = ctx.enter_context(nc.psum_tensor("score", [P, 2, 512], F32))
        turn = ctx.enter_context(nc.psum_tensor("turn", [P, 512], F32))
        amisc = ctx.enter_context(nc.psum_tensor("amisc", [P, 512], F32))
        up = [ctx.enter_context(nc.psum_tensor(f"up{i}", [P, 512], F32)) for i in range(3)]
        yacc = ctx.enter_context(nc.psum_tensor("yacc", [P, 512], F32))

        x = sb("x", [P, 2 * PAIRS, D])
        cx = sb("cx", [P, 2 * PAIRS, D])
        ctxT = sb("ctxT", [P, B * S])
        vecs = sb("vecs", [NCOL, P])
        col = sb("col", [P, NCOL])
        half_bg = sb("half_bg", [P, C2])
        anti_mu = sb("anti_mu", [P, 2])
        wT = sb("wT", [P, len(SLOT), P])
        w_nat = sb("w_nat", [P, len(W_TURNED), P])
        bo_b = sb("bo_b", [P, 3, D])
        gbo = sb("gbo", [P, 3, D])
        rb_b = sb("rb_b", [P, E2])
        gates = sb("gates", [P, 2 * LAYERS])
        gx = sb("gx", [P, LAYERS])
        gf = sb("gf", [P, LAYERS])
        mask1 = sb("mask1", [P, S], I32)
        mask2 = sb("mask2", [P, 2 * PAIRS, S], I32)
        add1 = sb("add1", [P, S])
        hide2 = sb("hide2", [P, 2 * PAIRS, S], I32)
        hidden_score = sb("hidden_score", [P, 1])
        ident = sb("ident", [P, P])
        head_of = sb("head_of", [P, HG])
        desc = sb("desc", [P, S])
        pick = sb("pick", [E0, E0, P], BF16)
        pick3 = sb("pick3", [80, C3 - 1, P], BF16)
        regA = sb("regA", [P, E0 * F0 * 2])
        w1_0 = regA[:, 0:E0 * F0].rearrange("p (e f) -> p e f", e=E0)
        w2_0 = regA[:, E0 * F0:2 * E0 * F0].rearrange("p (c d) -> p c d", d=D)
        w2_2 = regA[:, 0:C2 * D].rearrange("p (c d) -> p c d", d=D)
        o3 = C2 * D
        w1_3 = regA[:, o3:o3 + E3 * F3].rearrange("p (e f) -> p e f", e=E3)
        w3_3 = regA[:, o3 + E3 * F3:o3 + 2 * E3 * F3].rearrange("p (e f) -> p e f", e=E3)
        w2_3 = regA[:, o3 + 2 * E3 * F3:o3 + 3 * E3 * F3].rearrange("p (c d) -> p c d", d=D)
        ws = sb("ws", [P, 3, P])
        w1_2 = sb("w1_2", [P, E2, 2 * F2])
        rw0 = sb("rw0", [P, E0])
        rw2 = sb("rw2", [P, E2])
        b2_0 = sb("b2_0", [E0, D])
        b2_2 = sb("b2_2", [E2, D])
        b2_2x = sb("b2_2x", [E2, D])
        xn_a = sb("xn_a", [P, PAIRS, D])
        xT_a = sb("xT_a", [P, TOK])
        stat_a = sb("stat_a", [P, PAIRS, 6])
        mv_a = sb("mv_a", [P, PAIRS, 2])
        rs_a = sb("rs_a", [P, PAIRS])
        xg = sb("xg", [P, PAIRS, D])
        qT = sb("qT", [P, TOK])
        kT = sb("kT", [P, TOK])
        kblk = sb("kblk", [P, HG, TOK])
        vblk = sb("vblk", [P, 2, HB, HP, 2, DH + 1])
        mx = sb("mx", [P, 2, H])
        prob = sb("prob", [P, 2, H, S])
        probT = sb("probT", [P, HP, P])
        rsum = sb("rsum", [P, H])
        attn_o = sb("attn_o", [P, PAIRS, D])
        oT = sb("oT", [P, TOK])
        found = sb("found", [P, PAIRS, 4])
        eqm = sb("eqm", [P, PAIRS, S])
        hit = sb("hit", [P, PAIRS, P])
        hitT = sb("hitT", [P, TOK])
        memT = sb("memT", [P, TOK])
        xn_f = sb("xn_f", [P, PAIRS, D])
        xT_f = sb("xT_f", [P, TOK])
        stat_f = sb("stat_f", [P, PAIRS, 6])
        mv_f = sb("mv_f", [P, PAIRS, 2])
        rs_f = sb("rs_f", [P, PAIRS])
        half_pow = sb("half_pow", [P, PAIRS])
        logit = sb("logit", [P, PAIRS, E3])
        expo = sb("expo", [P, PAIRS, E3])
        tmp_r = sb("tmp_r", [P, PAIRS, E3])
        onehot = sb("onehot", [P, PAIRS, E3])
        red = sb("red", [P, 4, PAIRS])
        wg = sb("wg", [P, PAIRS])
        grp = sb("grp", [P, PAIRS, 8])
        grp2 = sb("grp2", [P, PAIRS, 8])
        top = sb("top", [P, PAIRS, 8])
        keep_g = sb("keep_g", [P, PAIRS, 4])
        maskT = sb("maskT", [E3, TOK])
        maskTb = sb("maskTb", [E3, TOK], BF16)
        cparts = sb("cparts", [80, TOK], BF16)
        cleft = sb("cleft", [E3, 2, TOK])
        hid = sb("hid", [P, NH, TOK])
        am = sb("am", [P, 2, TOK])
        th = sb("th", [P, 2, TOK])
        mB = sb("mB", [P, 2, TOK])
        yT = sb("yT", [P, TOK])
        xprev = hid[:, 0, :].rearrange("p (b s) -> p b s", s=S)

        ld = {n: sem("ld_" + n) for n in ("x", "ctx", "vec", "w0", "misc", "f0", "f0b", "wn", "mask", "f2", "f2b", "f3")}
        LD = {}
        stored = sem("stored")
        ident_set = sem("ident_set"); const_set = sem("const_set"); pool_seq = sem("pool_seq")
        vec_ps = sem("vec_ps"); vec_sb = sem("vec_sb"); ctx_ps = sem("ctx_ps")
        ctx_sb_act = sem("ctx_sb_act"); ctx_sb_dve = sem("ctx_sb_dve")
        wturn_ps = sem("wturn_ps"); wturn_sb = sem("wturn_sb")
        gates_sb = sem("gates_sb"); gf_sb = sem("gf_sb"); gbo_sb = sem("gbo_sb"); mask_sb = sem("mask_sb")
        zeros_set = sem("zeros_set"); dve_seq = sem("dve_seq"); b2x_sb = sem("b2x_sb")
        a_var = sem("a_var"); a_rstd = sem("a_rstd"); a_xn = sem("a_xn"); a_xT_ps = sem("a_xT_ps"); a_xT = sem("a_xT")
        xg_sb = sem("xg_sb"); q_ps = sem("q_ps"); q_sb = sem("q_sb"); k_ps = sem("k_ps"); k_sb = sem("k_sb")
        kblk_sb = sem("kblk_sb"); v_ps = sem("v_ps"); v_sb = sem("v_sb")
        r_ps = sem("r_ps"); hit_sb = sem("hit_sb"); hitT_ps = sem("hitT_ps"); hitT_sb = sem("hitT_sb")
        mem_ps = sem("mem_ps"); mem_sb = sem("mem_sb")
        s_ps = sem("s_ps"); d_sb = sem("d_sb"); p_sb = sem("p_sb"); pt_ps = sem("pt_ps"); pt_sb = sem("pt_sb")
        av_ps = sem("av_ps"); on_sb = sem("on_sb"); ot_ps = sem("ot_ps"); ot_sb = sem("ot_sb"); o_ps = sem("o_ps")
        x_attn = sem("x_attn")
        f_var = sem("f_var"); f_rstd = sem("f_rstd"); f_xn = sem("f_xn"); f_xT_ps = sem("f_xT_ps"); f_xT = sem("f_xT")
        lg_ps = sem("lg_ps"); lg_max = sem("lg_max"); lg_exp = sem("lg_exp"); hot_sb = sem("hot_sb"); hotT_ps = sem("hotT_ps")
        hotT_sb = sem("hotT_sb"); parts_sb = sem("parts_sb")
        m0_ps = sem("m0_ps"); h0_ps = sem("h0_ps"); h0_sb = sem("h0_sb"); hm0_sb = sem("hm0_sb"); dn0_ps = sem("dn0_ps")
        m2_ps = sem("m2_ps"); m2_sb = sem("m2_sb"); a2_ps = sem("a2_ps"); g2_ps = sem("g2_ps"); am2_sb = sem("am2_sb")
        t2_sb = sem("t2_sb"); h2_sb = sem("h2_sb"); dn2_ps = sem("dn2_ps")
        h3_ps = sem("h3_ps"); g3_ps = sem("g3_ps"); c3_ps = sem("c3_ps"); t3_sb = sem("t3_sb"); u3_sb = sem("u3_sb")
        v3_sb = sem("v3_sb"); hm3_sb = sem("hm3_sb"); dn3_ps = sem("dn3_ps")
        mix_sb = sem("mix_sb"); mr_ps = sem("mr_ps"); mk_ps = sem("mk_ps"); mt_sb = sem("mt_sb"); mrelu_sb = sem("mrelu_sb")
        mka_sb = sem("mka_sb"); mv_ps = sem("mv_ps"); my_sb = sem("my_sb")
        y_ps = sem("y_ps"); y_sb = sem("y_sb"); yb_ps = sem("yb_ps"); x_ffn = sem("x_ffn")

        def half(t, n):
            h = n % HALVES
            return t[:, h * PAIRS:(h + 1) * PAIRS]

        def flat(ap):
            return ap.rearrange("p a b -> p (a b)")

        def cols(name, i=0):
            o = COL[name][0] + i
            return col[:, o:o + 1]

        def W(name):
            return wT[:, SLOT[name], :]

        def y_index(n):
            return n if n < 2 else n - 2

        loads = []

        def load(group, dst, src):
            LD[group] = LD.get(group, 0) + 1
            loads.append((group, dst, src))

        xf = A["x"].rearrange("b s d -> (b s) d").rearrange("(t p) d -> p t d", p=P)
        cf = A["ctx_1024"].rearrange("b s d -> (b s) d").rearrange("(t p) d -> p t d", p=P)
        load("ctx", cx[:], cf)
        load("x", x[:], xf)

        def row(v):
            return v.rearrange("(a n) -> a n", a=1)

        for nm, src in (("bq0", "L0_xattn_bq"), ("bk0", "L0_xattn_bk"), ("bv0", "L0_xattn_bv"),
                        ("bq1", "L1_xattn_bq"), ("bk1", "L1_xattn_bk"), ("bv1", "L1_xattn_bv"),
                        ("bq2", "L2_xattn_bq"), ("bk2", "L2_xattn_bk"), ("bv2", "L2_xattn_bv"),
                        ("mu_r", "L1_ffn_mu_r"), ("mu_k", "L1_ffn_mu_k")):
            o = COL[nm][0]
            load("vec", vecs[o:o + 1, :], row(A[src]))
        for nm, src, k in (("b1_0", "L0_ffn_b1", C0), ("b1_2", "L2_ffn_b1", 2 * C2)):
            o = COL[nm][0]
            load("vec", vecs[o:o + k, :], A[src].rearrange("e (c p) -> (e c) p", p=P))
        for nm, src in (("Wk0", "L0_xattn_Wk"), ("Wv0", "L0_xattn_Wv"), ("Wq0", "L0_xattn_Wq"), ("Wo0", "L0_xattn_Wo")):
            load("w0", wT[:, SLOT[nm], :], A[src])
        load("misc", gates[:, 0:LAYERS], A["g_xattn"].partition_broadcast(P))
        load("misc", gates[:, LAYERS:], A["g_ffn"].partition_broadcast(P))
        for l in range(3):
            load("misc", bo_b[:, l, :], A[f"L{l}_xattn_bo"].partition_broadcast(P))
        load("misc", rb_b[:], A["L2_ffn_router_b"].partition_broadcast(P))
        load("f0", rw0[:], A["L0_ffn_router_w"])
        load("f0", b2_0[:], A["L0_ffn_b2"])
        load("f0", w1_0, A["L0_ffn_w1"].rearrange("e d f -> d e f"))
        for nm, src in (("Wq1", "L1_xattn_Wq"), ("Wk1", "L1_xattn_Wk"), ("Wv1", "L1_xattn_Wv"), ("Wo1", "L1_xattn_Wo"),
                        ("W_r", "L1_ffn_W_r"), ("W_k", "L1_ffn_W_k"), ("W_v", "L1_ffn_W_v"),
                        ("Wq2", "L2_xattn_Wq"), ("Wk2", "L2_xattn_Wk"), ("Wv2", "L2_xattn_Wv"), ("Wo2", "L2_xattn_Wo"),
                        ("Wq3", "L3_xattn_Wq"), ("Wo3", "L3_xattn_Wc")):
            load("wn", w_nat[:, W_TURNED.index(nm), :], A[src])
        for j, nm in enumerate(("Wk3", "Wv3")):
            for h in range(H):
                load("wn", w_nat[h * DH:(h + 1) * DH, W_TURNED.index(nm), :], A["L3_xattn_Wkv"][j * DH:(j + 1) * DH, :])
        load("wn", w_nat[0:E3, W_TURNED.index("gate"), :], A["L3_ffn_gate_w"])
        load("f0b", w2_0, A["L0_ffn_w2"].rearrange("e (c p) d -> p (e c) d", p=P))
        for j in range(2):
            load("mask", mask1[j * S:(j + 1) * S, :], A["mask_SxS2_if1"])
        load("mask", mask2[:], A["mask_BxSxS2_ik1"].rearrange("b q k -> (b q) k").rearrange("(t p) k -> p t k", p=P))
        load("f2", rw2[:], A["L2_ffn_router_w"])
        load("f2", b2_2[:], A["L2_ffn_b2"])
        load("f2", w1_2[:], A["L2_ffn_w1"].rearrange("e d f -> d e f"))
        for j, nm in enumerate(("L3_ffn_ws1", "L3_ffn_ws3", "L3_ffn_ws2")):
            load("f2", ws[:, j, :], A[nm])
        early = len(loads)
        load("f2b", w2_2, A["L2_ffn_w2"].rearrange("e (c p) d -> p (e c) d", p=P))
        load("f3", w1_3, A["L3_ffn_w1"].rearrange("e d f -> d e f"))
        load("f3", w3_3, A["L3_ffn_w3"].rearrange("e d f -> d e f"))
        load("f3", w2_3, A["L3_ffn_w2"].rearrange("(c two) f d -> (two f) c d", two=2))
        out_t = out.rearrange("b s d -> (b s) d").rearrange("(t p) d -> p t d", p=P)

        def loaded(eng, group):
            eng.wait_ge(ld[group], 16 * LD[group])

        block = ctx.enter_context(nc.Block())

        @block.sync
        def _(sync):
            for i, (group, dst, src) in enumerate(loads):
                if i == early:
                    sync.wait_ge(dn0_ps, 2 * C0)
                sync.dma_start(dst, src).then_inc(ld[group], 16)
            for h in range(HALVES):
                sync.wait_ge(x_ffn, STAGES - HALVES + h + 1)
                sync.dma_start(out_t[:, h * PAIRS:(h + 1) * PAIRS, :], half(x, h)).then_inc(stored, 16)
            sync.wait_ge(stored, 16 * HALVES)

        @block.gpsimd
        def _(pool):
            seq = [0]

            def done(ins):
                seq[0] += 1
                ins.then_inc(pool_seq, 1)
                pool.wait_ge(pool_seq, seq[0])

            def setup():
                done(pool.memset(ident[:], 0.0))
                pool.affine_select(out=ident[:], in_=ident[:], compare_op=ALU.not_equal, fill=1.0, base=0,
                                   pattern=[[-1, P]], channel_multiplier=1).then_inc(ident_set, 1)
                done(pool.memset(head_of[:], 1.0))
                for r in range(2):
                    part = head_of[64 * r:64 * r + 64, :]
                    done(pool.affine_select(out=part, in_=part, compare_op=ALU.is_ge, fill=0.0, base=0,
                                            pattern=[[-DH, HG]], channel_multiplier=1))
                    done(pool.affine_select(out=part, in_=part, compare_op=ALU.is_ge, fill=0.0, base=DH - 1,
                                            pattern=[[DH, HG]], channel_multiplier=-1))
                pool.memset(half_pow[:], -0.5)
                pool.memset(hidden_score[:], -10000.0 / SCALE)
                done(pool.memset(grp[:, :, :], -1.0))
                done(pool.iota(desc[:], pattern=[[-1, S]], base=S, channel_multiplier=0,
                               allow_small_or_imprecise_dtypes=True))
                done(pool.memset(pick[:], 0.0))
                done(pool.affine_select(out=pick[:], in_=pick[:], compare_op=ALU.not_equal, fill=1.0, base=0,
                                        pattern=[[-1, E0], [0, P]], channel_multiplier=1))
                done(pool.memset(pick3[:], 0.0))
                for k in range(3):
                    part = pick3[32 * k:32 * k + E3, :, :].rearrange("p c (two f) -> p c two f", two=2)
                    done(pool.affine_select(out=part, in_=part, compare_op=ALU.not_equal, fill=1.0, base=0,
                                            pattern=[[-2, C3 - 1], [-1, 2], [0, F3]], channel_multiplier=1))
                done(pool.memset(cparts[:], 0.0))
                pool.memset(hit[:], 0.0).then_inc(const_set, 1)
                for k in range(2):
                    done(pool.memset(vblk[:, k], 0.0))
                    for j in range(2):
                        done(pool.memset(vblk[64 * j:64 * j + 64, k, :, :, j, DH:DH + 1], 1.0))
                pool.memset(stat_a[:], 0.0).then_inc(zeros_set, 1)
                pool.wait_ge(zeros_set, 1)

            def keys_values(n):
                pool.wait_ge(k_sb, n + 1)
                if n > 0:
                    pool.wait_ge(s_ps, PAIRS * n)
                pool.tensor_tensor(kblk[:], kT[:].unsqueeze(1).to_broadcast([P, HG, TOK]),
                                   head_of[:].unsqueeze(2).to_broadcast([P, HG, TOK]), ALU.mult).then_inc(kblk_sb, 1)

            def rstd(var_sem, count, mv, rs, rstd_sem):
                pool.wait_ge(var_sem, count)
                pool.tensor_tensor(rs[:], mv[:, :, 1], half_pow[:], ALU.pow).then_inc(rstd_sem, 1)

            def attn_norm(n):
                rstd(a_var, n + 1, mv_a, rs_a, a_rstd)
                if n // HALVES < 3:
                    if n == 0:
                        loaded(pool, "misc")
                        pool.wait_ge(gates_sb, 1)
                        for l in range(3):
                            done(pool.tensor_scalar(gbo[:, l, :], bo_b[:, l, :], gx[:, l:l + 1], None, ALU.mult))
                    if n > 0:
                        pool.wait_ge(x_attn, n)
                    pool.tensor_tensor(xg[:], half(x, n),
                                       gbo[:, n // HALVES, :].unsqueeze(1).to_broadcast([P, PAIRS, D]),
                                       ALU.add).then_inc(xg_sb, 1)

            def ffn_norm(n):
                rstd(f_var, n + 1, mv_f, rs_f, f_rstd)

            parts = {"setup": setup, "keys_values": keys_values, "attn_norm": attn_norm, "ffn_norm": ffn_norm}
            for step, *at in PLAN:
                if step in parts:
                    parts[step](*at)

        @block.scalar
        def _(act):
            def setup():
                loaded(act, "misc")
                act.activation(gx[:], gates[:, 0:LAYERS], ACT.Tanh).then_inc(gates_sb, 1)
                act.activation(gf[:], gates[:, LAYERS:], ACT.Tanh).then_inc(gates_sb, 1)
                act.wait_ge(ctx_ps, 1)
                act.activation(ctxT[:, 0:512], up[1][:], ACT.Copy).then_inc(ctx_sb_act, 1)

            def turn_weights(g):
                act.wait_ge(wturn_ps, g + 1)
                lo = len(W_DIRECT) + TURN_GROUPS[g][0]
                k = len(TURN_GROUPS[g])
                act.activation(wT[:, lo:lo + k, :], up[g % 3][:, 0:k * P].rearrange("p (k m) -> p k m", k=k),
                               ACT.Copy).then_inc(wturn_sb, 1)

            def keys_values(n):
                l = n // HALVES
                if n == 0:
                    act.wait_ge(vec_sb, 1)
                act.wait_ge(k_ps, n + 1)
                if n > 0:
                    act.wait_ge(kblk_sb, n)
                if l < 3:
                    act.activation(kT[:], amisc[:], ACT.Identity, bias=cols(f"bk{l}")).then_inc(k_sb, 1)
                else:
                    act.activation(kT[:], amisc[:], ACT.Copy).then_inc(k_sb, 1)
                act.wait_ge(v_ps, n + 1)
                if n == 0:
                    act.wait_ge(zeros_set, 1)
                for j in range(2):
                    o = vblk[64 * j:64 * j + 64, n % 2, :, :, j, 0:DH]
                    last = act.activation(o, amisc[64 * j:64 * j + 64, :].rearrange("p (b h d) -> p b h d", b=HB, h=HP),
                                          ACT.Copy)
                    last.then_inc(v_sb, 1)

            def attn_norm(n):
                act.wait_ge(a_xT_ps, n + 1)
                act.activation(xT_a[:], amisc[:], ACT.Copy).then_inc(a_xT, 1)

            def queries(n):
                l = n // HALVES
                act.wait_ge(q_ps, n + 1)
                if l < 3:
                    act.activation(qT[:], amisc[:], ACT.Identity, bias=cols(f"bq{l}")).then_inc(q_sb, 1)
                else:
                    act.activation(qT[:], amisc[:], ACT.Copy).then_inc(q_sb, 1)

            def retrieve(n):
                r = n - 3 * HALVES
                act.wait_ge(hitT_ps, r + 1)
                act.activation(hitT[:], amisc[:], ACT.Copy).then_inc(hitT_sb, 1)
                act.wait_ge(mem_ps, r + 1)
                act.activation(memT[:], amisc[:], ACT.Copy).then_inc(mem_sb, 1)

            def scores(n, p):
                i = n * PAIRS + p
                act.wait_ge(d_sb, i + 1)
                act.activation(prob[:, i % 2], prob[:, i % 2], ACT.Exp, scale=SCALE).then_inc(p_sb, 1)

            def turn_probs(n, p, r):
                i = n * PAIRS + p
                act.wait_ge(pt_ps, 2 * i + r + 1)
                if i > 0:
                    act.wait_ge(av_ps, i)
                act.activation(flat(probT[:, 4 * r:4 * r + 4, :]), turn[:], ACT.Copy).then_inc(pt_sb, 1)

            def attn_out(n):
                l = n // HALVES
                act.wait_ge(ot_ps, n + 1)
                if l < 3:
                    act.activation(oT[:], amisc[:], ACT.Identity, bias=cols(f"bv{l}")).then_inc(ot_sb, 1)
                else:
                    act.activation(oT[:], amisc[:], ACT.Copy).then_inc(ot_sb, 1)

            def ffn_norm(n):
                act.wait_ge(f_xT_ps, n + 1)
                act.activation(xT_f[:], up[0][:], ACT.Copy).then_inc(f_xT, 1)

            def route(n):
                l = n // HALVES
                r = n if l == 0 else n - 2
                ne = {0: E0, 2: E2, 3: E3}[l]
                if l != 2:
                    k = r if l == 0 else r - 2
                    act.wait_ge(lg_max, k + 1)
                    act.activation(expo[:, :, 0:ne], logit[:, :, 0:ne], ACT.Exp).then_inc(lg_exp, 1)
                if l != 3:
                    act.wait_ge(hotT_ps, r + 1)
                    act.activation(maskT[0:ne, :], up[2][0:ne, :], ACT.Copy).then_inc(hotT_sb, 1)
                    act.activation(maskTb[0:ne, :], up[2][0:ne, :], ACT.Copy).then_inc(hotT_sb, 1)

            def chunk(n, i):
                l, h = n // HALVES, n % HALVES
                if l == 0 and i < C0:
                    g = h * C0 + i
                    act.wait_ge(h0_ps, g + 1)
                    if g >= NH:
                        act.wait_ge(dn0_ps, g - NH + 1)
                    act.activation(hid[:, i % NH, :], up[i % 2][:], ACT.Gelu, bias=cols("b1_0", i)).then_inc(h0_sb, 1)
                if l == 2 and i < C2:
                    g = h * C2 + i
                    e = i // 4
                    if i % 4 == 0:
                        ge = h * E2 + e
                        act.wait_ge(m2_ps, ge + 1)
                        if ge >= 2:
                            act.wait_ge(am2_sb, 4 * (ge - 1))
                        act.activation(mB[:, ge % 2, :], up[0][:], ACT.Copy).then_inc(m2_sb, 1)
                    act.wait_ge(g2_ps, g + 1)
                    if g >= 2:
                        act.wait_ge(h2_sb, g - 1)
                    act.activation(th[:, g % 2, :], up[0][:], ACT.Tanh, bias=half_bg[:, i:i + 1],
                                   scale=0.5).then_inc(t2_sb, 1)
                if l == 3 and i < C3:
                    g = h * C3 + i
                    act.wait_ge(h3_ps, g + 1)
                    if g >= 2:
                        act.wait_ge(u3_sb, g - 1)
                    act.activation(th[:, g % 2, :], up[0][:], ACT.Tanh, scale=0.5).then_inc(t3_sb, 1)

            def channel_mix(n):
                h = n % HALVES
                act.wait_ge(mr_ps, h + 1)
                act.activation(th[:, 0, :], up[0][:], ACT.Tanh, scale=0.5).then_inc(mt_sb, 1)
                act.wait_ge(mk_ps, h + 1)
                act.activation(th[:, 1, :], up[1][:], ACT.Relu).then_inc(mrelu_sb, 1)

            def ffn_out(n):
                if n // HALVES != 1:
                    if n // HALVES == 3:
                        act.wait_ge(dn3_ps, C3 * (n % HALVES + 1))
                    else:
                        act.wait_ge(y_ps, y_index(n) + 1)
                    if n > 0:
                        act.wait_ge(yb_ps, n)
                    act.activation(yT[:], yacc[:], ACT.Copy).then_inc(y_sb, 1)

            parts = {"setup": setup, "turn_weights": turn_weights, "keys_values": keys_values, "attn_norm": attn_norm,
                     "queries": queries, "retrieve": retrieve, "scores": scores, "turn_probs": turn_probs,
                     "attn_out": attn_out, "ffn_norm": ffn_norm, "route": route, "chunk": chunk,
                     "channel_mix": channel_mix, "ffn_out": ffn_out}
            for step, *at in PLAN:
                if step in parts:
                    parts[step](*at)

        @block.tensor
        def _(pe):
            def turn4(dst, src, n_in=P):
                for t in range(4):
                    last = pe.transpose(dst[0:n_in, t * P:(t + 1) * P], src(t), ident[:])
                return last

            def setup():
                pe.wait_ge(ident_set, 1)
                loaded(pe, "ctx")
                turn4(up[1], lambda t: cx[:, t, :]).then_inc(ctx_ps, 1)
                turn4(up[2], lambda t: cx[:, 4 + t, :]).then_inc(ctx_ps, 1)
                loaded(pe, "vec")
                pe.transpose(up[0][:, 0:NCOL], vecs[:], ident[0:NCOL, 0:NCOL]).then_inc(vec_ps, 1)

            def turn_weights(g):
                if g == 0:
                    loaded(pe, "wn")
                    pe.wait_ge(vec_sb, 1)
                if g == 1:
                    pe.wait_ge(ctx_sb_act, 1)
                if g == 2:
                    pe.wait_ge(ctx_sb_dve, 1)
                if g >= 3:
                    pe.wait_ge(wturn_sb, g - 2)
                for j, s in enumerate(TURN_GROUPS[g]):
                    rows = E3 if W_TURNED[s] == "gate" else P
                    last = pe.transpose(up[g % 3][:, j * P:j * P + rows], w_nat[0:rows, s, :], ident[0:rows, 0:rows])
                last.then_inc(wturn_ps, 1)

            def keys_values(n):
                l, h = n // HALVES, n % HALVES
                if n == 0:
                    loaded(pe, "w0")
                    pe.wait_ge(ctx_sb_act, 1)
                    pe.wait_ge(ctx_sb_dve, 1)
                if l > 0:
                    pe.wait_ge(wturn_sb, len(TURN_GROUPS))
                if l < 3:
                    src = ctxT[:, h * TOK:(h + 1) * TOK]
                    if n > 0:
                        pe.wait_ge(on_sb, PAIRS * n)
                else:
                    src = memT[:]
                    pe.wait_ge(mem_sb, n - 3 * HALVES + 1)
                pe.matmul(amisc[:], W(f"Wk{l}"), src, start=True, stop=True).then_inc(k_ps, 1)
                pe.wait_ge(k_sb, n + 1)
                w = W(f"Wv{l}").rearrange("p (h j d) -> p j h d", j=2, d=DH)
                for b in range(HB):
                    for j in range(2):
                        last = pe.matmul(amisc[64 * j:64 * j + 64, b * 64:(b + 1) * 64], src[:, b * S:(b + 1) * S],
                                         w[:, j], start=True, stop=True)
                last.then_inc(v_ps, 1)

            def attn_norm(n):
                pe.wait_ge(a_xn, n + 1)
                if n == 0:
                    pe.wait_ge(v_sb, 2)
                else:
                    pe.wait_ge(x_attn, n)
                turn4(amisc, lambda t: xn_a[:, t, :]).then_inc(a_xT_ps, 1)

            def queries(n):
                pe.wait_ge(a_xT, n + 1)
                pe.matmul(amisc[:], W(f"Wq{n // HALVES}"), xT_a[:], start=True, stop=True).then_inc(q_ps, 1)

            def retrieve(n):
                h, r = n % HALVES, n - 3 * HALVES
                pe.wait_ge(q_sb, n + 1)
                for b in range(HB):
                    t = slice(b * S, (b + 1) * S)
                    last = pe.matmul(amisc[64 * (b % 2):64 * (b % 2) + 64, (b // 2) * S:(b // 2 + 1) * S], qT[:, t],
                                     ctxT[:, h * TOK + b * S:h * TOK + (b + 1) * S], start=True, stop=True)
                last.then_inc(r_ps, 1)
                pe.wait_ge(hit_sb, r + 1)
                turn4(amisc, lambda t: hit[:, t, :]).then_inc(hitT_ps, 1)
                pe.wait_ge(hitT_sb, r + 1)
                for t in range(PAIRS):
                    last = pe.matmul(amisc[:, t * P:(t + 1) * P], cx[:, h * PAIRS + t, :], hitT[:, t * P:(t + 1) * P],
                                     start=True, stop=True)
                last.then_inc(mem_ps, 1)

            def scores(n, p):
                i = n * PAIRS + p
                if p == 0:
                    pe.wait_ge(kblk_sb, n + 1)
                    pe.wait_ge(q_sb, n + 1)
                if i > 0:
                    pe.wait_ge(d_sb, i)
                for b in range(2):
                    t = slice((2 * p + b) * S, (2 * p + b + 1) * S)
                    for r in range(2):
                        rows = slice(64 * r, 64 * r + 64)
                        last = pe.matmul(score[64 * b:64 * b + 64, r, :], qT[rows, t], kblk[rows, :, t],
                                         start=True, stop=True)
                last.then_inc(s_ps, 1)

            def turn_probs(n, p, r):
                i = n * PAIRS + p
                pe.wait_ge(p_sb, i + 1)
                if i + r > 0:
                    pe.wait_ge(pt_sb, 2 * i + r)
                for t in range(4):
                    hp = 4 * r + t
                    last = pe.transpose(turn[:, t * P:(t + 1) * P],
                                        prob[:, i % 2, 2 * hp:2 * hp + 2, :].rearrange("p a b -> p (a b)"), ident[:])
                last.then_inc(pt_ps, 1)

            def attend(n, p):
                i = n * PAIRS + p
                pe.wait_ge(v_sb, 2 * (n + 1))
                pe.wait_ge(pt_sb, 2 * i + 2)
                if i > 0:
                    pe.wait_ge(on_sb, i)
                for hp in range(HP):
                    for b in range(2):
                        v = vblk[:, n % 2, 2 * p + b, hp].rearrange("p j d -> p (j d)")
                        last = pe.matmul(amisc[64 * b:64 * b + 64, hp * 2 * (DH + 1):(hp + 1) * 2 * (DH + 1)],
                                         probT[:, hp, 64 * b:64 * b + 64], v, start=True, stop=True)
                last.then_inc(av_ps, 1)

            def attn_out(n):
                pe.wait_ge(on_sb, PAIRS * (n + 1))
                if n + 1 < STAGES and (n + 1) // HALVES < 3:
                    pe.wait_ge(v_sb, 2 * (n + 2))
                turn4(amisc, lambda t: attn_o[:, t, :]).then_inc(ot_ps, 1)
                pe.wait_ge(ot_sb, n + 1)
                for t in range(PAIRS):
                    last = pe.matmul(amisc[:, t * P:(t + 1) * P], oT[:, t * P:(t + 1) * P], W(f"Wo{n // HALVES}"),
                                     start=True, stop=True)
                last.then_inc(o_ps, 1)

            def ffn_norm(n):
                pe.wait_ge(f_xn, n + 1)
                if n == 0:
                    pe.wait_ge(wturn_sb, len(TURN_GROUPS))
                else:
                    pe.wait_ge(x_ffn, n)
                turn4(up[0], lambda t: xn_f[:, t, :]).then_inc(f_xT_ps, 1)

            def route(n):
                l = n // HALVES
                r = n if l == 0 else n - 2
                ne = {0: E0, 2: E2, 3: E3}[l]
                w = {0: rw0[:], 2: rw2[:], 3: W("gate")[:, 0:E3]}[l]
                loaded(pe, {0: "f0", 2: "f2", 3: "wn"}[l])
                pe.wait_ge(f_xT, n + 1)
                for t in range(PAIRS):
                    last = pe.matmul(up[1][:, t * ne:(t + 1) * ne], xT_f[:, t * P:(t + 1) * P], w, start=True, stop=True)
                last.then_inc(lg_ps, 1)
                pe.wait_ge(hot_sb, r + 1)
                turn4(up[2], lambda t: onehot[:, t, 0:ne], ne).then_inc(hotT_ps, 1)

            def chunk(n, i):
                l, h = n // HALVES, n % HALVES
                if l == 0:
                    g = h * C0 + i
                    if i < C0:
                        e, f = i // 2, i % 2
                        if f == 0:
                            if i == 0:
                                pe.wait_ge(hotT_sb, 2 * (n + 1))
                            if g > 0:
                                pe.wait_ge(hm0_sb, g)
                            pe.matmul(up[2][:], pick[:, e, :], maskTb[0:E0, :], start=True, stop=True).then_inc(m0_ps, 1)
                        if i >= 2:
                            pe.wait_ge(h0_sb, g - 1)
                        pe.matmul(up[i % 2][:], w1_0[:, e, f * P:(f + 1) * P], xT_f[:], start=True,
                                  stop=True).then_inc(h0_ps, 1)
                    if i >= LAG:
                        j, gj = i - LAG, g - LAG
                        if j == 0:
                            loaded(pe, "f0b")
                            if n > 0:
                                pe.wait_ge(y_sb, y_index(n))
                        pe.wait_ge(hm0_sb, gj + 1)
                        pe.matmul(yacc[:], w2_0[:, j, :], hid[:, j % NH, :], start=(j == 0), stop=False).then_inc(dn0_ps, 1)
                        if j == C0 - 1:
                            pe.matmul(yacc[:], b2_0[:], maskT[0:E0, :], start=False, stop=True).then_inc(y_ps, 1)
                if l == 2:
                    g = h * C2 + i
                    if i < C2:
                        e, c = i // 4, i % 4
                        if c == 0:
                            ge = h * E2 + e
                            if i == 0:
                                r = n - 2
                                pe.wait_ge(hotT_sb, 2 * (r + 1))
                            if g > 0:
                                pe.wait_ge(t2_sb, g)
                            pe.matmul(up[0][:], pick[0:E2, e, :], maskTb[0:E2, :], start=True, stop=True).then_inc(m2_ps, 1)
                        if g >= 2:
                            pe.wait_ge(am2_sb, g - 1)
                        pe.matmul(up[1 + i % 2][:], w1_2[:, e, c * P:(c + 1) * P], xT_f[:], start=True,
                                  stop=True).then_inc(a2_ps, 1)
                        if c == 0:
                            pe.wait_ge(m2_sb, ge + 1)
                        else:
                            pe.wait_ge(t2_sb, g)
                        pe.matmul(up[0][:], w1_2[:, e, F2 + c * P:F2 + (c + 1) * P], xT_f[:], start=True,
                                  stop=True).then_inc(g2_ps, 1)
                    if i >= LAG:
                        j, gj = i - LAG, g - LAG
                        if j == 0:
                            loaded(pe, "f2b")
                            pe.wait_ge(y_sb, y_index(n))
                        pe.wait_ge(h2_sb, gj + 1)
                        pe.matmul(yacc[:], w2_2[:, j, :], hid[:, j % NH, :], start=(j == 0), stop=False).then_inc(dn2_ps, 1)
                        if j == C2 - 1:
                            if h == 0:
                                pe.wait_ge(b2x_sb, 1)
                            pe.matmul(yacc[:], b2_2x[:], maskT[0:E2, :], start=False, stop=True).then_inc(y_ps, 1)
                if l == 3:
                    g = h * C3 + i
                    if i < C3:
                        if i == 0:
                            loaded(pe, "f3")
                        if g > 0:
                            pe.wait_ge(u3_sb, g)
                        w = w1_3[:, 2 * i:2 * i + 2, :].rearrange("p a b -> p (a b)") if i < C3 - 1 else ws[:, 0, :]
                        pe.matmul(up[0][:], w, xT_f[:], start=True, stop=True).then_inc(h3_ps, 1)
                        if g > 0:
                            pe.wait_ge(v3_sb, g)
                        w = w3_3[:, 2 * i:2 * i + 2, :].rearrange("p a b -> p (a b)") if i < C3 - 1 else ws[:, 1, :]
                        pe.matmul(up[1][:], w, xT_f[:], start=True, stop=True).then_inc(g3_ps, 1)
                        if i < C3 - 1:
                            gc = h * (C3 - 1) + i
                            if i == 0:
                                pe.wait_ge(parts_sb, h + 1)
                            if gc > 0:
                                pe.wait_ge(hm3_sb, gc)
                            pe.matmul(up[2][:], pick3[:, i, :], cparts[:], start=True, stop=True).then_inc(c3_ps, 1)
                    if i >= LAG:
                        j, gj = i - LAG, g - LAG
                        if j == 0:
                            pe.wait_ge(y_sb, y_index(n))
                        if j < C3 - 1:
                            pe.wait_ge(hm3_sb, h * (C3 - 1) + j + 1)
                            w = w2_3[:, j, :]
                        else:
                            pe.wait_ge(v3_sb, gj + 1)
                            w = ws[:, 2, :]
                        last = pe.matmul(yacc[:], w, hid[:, j % NH, :], start=(j == 0), stop=(j == C3 - 1))
                        last.then_inc(dn3_ps, 1)

            def channel_mix(n):
                h = n % HALVES
                pe.wait_ge(mix_sb, 2 * h + 1)
                pe.matmul(up[0][:], W("W_r"), am[:, 0, :], start=True, stop=True).then_inc(mr_ps, 1)
                pe.wait_ge(mix_sb, 2 * h + 2)
                pe.matmul(up[1][:], W("W_k"), am[:, 1, :], start=True, stop=True).then_inc(mk_ps, 1)
                pe.wait_ge(mka_sb, h + 1)
                pe.matmul(up[2][:], W("W_v"), hid[:, 1, :], start=True, stop=True).then_inc(mv_ps, 1)

            def ffn_out(n):
                if n // HALVES == 1:
                    pe.wait_ge(my_sb, n % HALVES + 1)
                else:
                    pe.wait_ge(y_sb, y_index(n) + 1)
                turn4(up[0], lambda t: yT[:, t * P:(t + 1) * P]).then_inc(yb_ps, 1)

            parts = {"setup": setup, "turn_weights": turn_weights, "keys_values": keys_values, "attn_norm": attn_norm,
                     "queries": queries, "retrieve": retrieve, "scores": scores, "turn_probs": turn_probs,
                     "attend": attend, "attn_out": attn_out, "ffn_norm": ffn_norm, "route": route, "chunk": chunk,
                     "channel_mix": channel_mix, "ffn_out": ffn_out}
            for step, *at in PLAN:
                if step in parts:
                    parts[step](*at)

        @block.vector
        def _(dve):
            seq = [0]

            def done(ins):
                seq[0] += 1
                ins.then_inc(dve_seq, 1)
                dve.wait_ge(dve_seq, seq[0])

            def setup():
                dve.wait_ge(ctx_ps, 2)
                dve.tensor_copy(ctxT[:, 512:1024], up[2][:]).then_inc(ctx_sb_dve, 1)
                dve.wait_ge(vec_ps, 1)
                dve.tensor_copy(col[:], up[0][:, 0:NCOL]).then_inc(vec_sb, 1)
                dve.wait_ge(vec_sb, 1)
                b1 = col[:, COL["b1_2"][0]:COL["b1_2"][0] + 2 * C2].rearrange("p (e two c) -> p e two c", e=E2, two=2)
                done(dve.tensor_scalar(half_bg[:].rearrange("p (e c) -> p e c", e=E2), b1[:, :, 1, :], 0.5, None, ALU.mult))
                o = COL["mu_r"][0]
                done(dve.tensor_scalar(anti_mu[:], col[:, o:o + 2], -1.0, 1.0, ALU.mult, ALU.add))
                dve.wait_ge(gates_sb, 2)
                dve.tensor_scalar(gf[:, 1:LAYERS], gf[:, 1:LAYERS], 0.5, None, ALU.mult).then_inc(gf_sb, 1)

            def late_setup():
                loaded(dve, "mask")
                done(dve.tensor_scalar(add1[:], mask1[:], 0.0, None, ALU.is_equal))
                done(dve.tensor_scalar(add1[:], add1[:], -3.0e38, None, ALU.mult))
                dve.tensor_scalar(hide2[:], mask2[:], 0.0, None, ALU.is_equal).then_inc(mask_sb, 1)
                loaded(dve, "f2")
                dve.tensor_scalar(b2_2x[:], b2_2[:], 2.0, None, ALU.mult).then_inc(b2x_sb, 1)

            def norm(n, xt, stat, mv, rs, xn, var_sem, rstd_sem, xn_sem):
                for t in range(PAIRS):
                    last = dve.bn_stats(stat[:, t, :], xt[:, t, :])
                done(last)
                for t in range(PAIRS):
                    last = dve.bn_aggr(mv[:, t, :], stat[:, t, :])
                done(last)
                dve.tensor_scalar(mv[:, :, 1], mv[:, :, 1], EPS, None, ALU.add).then_inc(var_sem, 1)
                dve.wait_ge(rstd_sem, n + 1)
                for t in range(PAIRS):
                    last = dve.tensor_scalar(xn[:, t, :], xt[:, t, :], mv[:, t, 0:1], rs[:, t:t + 1],
                                             ALU.subtract, ALU.mult)
                last.then_inc(xn_sem, 1)

            def attn_norm(n):
                if n == 0:
                    loaded(dve, "x")
                    dve.wait_ge(zeros_set, 1)
                if n >= HALVES:
                    dve.wait_ge(x_ffn, n - 1)
                if n > 0:
                    dve.wait_ge(a_xT_ps, n)
                    if (n - 1) // HALVES < 3:
                        dve.wait_ge(a_rstd, n)
                norm(n, half(x, n), stat_a, mv_a, rs_a, xn_a, a_var, a_rstd, a_xn)

            def retrieve(n):
                r = n - 3 * HALVES
                dve.wait_ge(r_ps, r + 1)
                sc = amisc[:, 0:PAIRS * S].rearrange("p (t m) -> p t m", t=PAIRS)
                done(dve.tensor_reduce(found[:, :, 0], sc, AX, ALU.max))
                done(dve.tensor_tensor(eqm[:], sc, found[:, :, 0:1].to_broadcast([P, PAIRS, S]), ALU.is_equal))
                done(dve.tensor_tensor(eqm[:], eqm[:], desc[:].unsqueeze(1).to_broadcast([P, PAIRS, S]), ALU.mult))
                done(dve.tensor_reduce(found[:, :, 1], eqm[:], AX, ALU.max))
                if r == 0:
                    dve.wait_ge(const_set, 1)
                for j in range(2):
                    rows = slice(64 * j, 64 * j + 64)
                    last = dve.tensor_tensor(hit[rows, :, 64 * j:64 * j + 64],
                                             desc[rows, :].unsqueeze(1).to_broadcast([64, PAIRS, S]),
                                             found[rows, :, 1:2].to_broadcast([64, PAIRS, S]), ALU.is_equal)
                    if j == 0:
                        done(last)
                last.then_inc(hit_sb, 1)

            def scores(n, p):
                i, l, h = n * PAIRS + p, n // HALVES, n % HALVES
                if i == 0:
                    late_setup()
                dve.wait_ge(s_ps, i + 1)
                sc = score[:].rearrange("p r (h k) -> p (r h) k", k=S)
                if l == 1:
                    done(dve.tensor_tensor(sc, sc, add1[:].unsqueeze(1).to_broadcast([P, H, S]), ALU.add))
                if l == 2:
                    done(dve.copy_predicated(sc, hide2[:, h * PAIRS + p, :].unsqueeze(1).to_broadcast([P, H, S]),
                                             hidden_score[:].unsqueeze(2).to_broadcast([P, H, S])))
                done(dve.tensor_reduce(mx[:, i % 2, :], sc, AX, ALU.max))
                if i >= 2:
                    dve.wait_ge(pt_ps, 2 * (i - 1))
                dve.tensor_tensor(prob[:, i % 2], sc, mx[:, i % 2, :].unsqueeze(2).to_broadcast([P, H, S]),
                                  ALU.subtract).then_inc(d_sb, 1)

            def attend(n, p):
                i = n * PAIRS + p
                dve.wait_ge(av_ps, i + 1)
                o = amisc[:, 0:H * (DH + 1)].rearrange("p (h d) -> p h d", d=DH + 1)
                done(dve.reciprocal(rsum[:], o[:, :, DH]))
                if p == 0 and n > 0:
                    dve.wait_ge(ot_ps, n)
                dve.tensor_tensor(attn_o[:, p, :].rearrange("p (h d) -> p h d", d=DH), o[:, :, 0:DH],
                                  rsum[:].unsqueeze(2).to_broadcast([P, H, DH]), ALU.mult).then_inc(on_sb, 1)

            def attn_out(n):
                l = n // HALVES
                dve.wait_ge(o_ps, n + 1)
                if l < 3:
                    dve.wait_ge(xg_sb, n + 1)
                src = xg[:] if l < 3 else half(x, n)
                dve.scalar_tensor_tensor(out=flat(half(x, n)), in0=amisc[:], scalar=gx[:, l:l + 1], in1=flat(src),
                                         op0=ALU.mult, op1=ALU.add).then_inc(x_attn, 1)

            def ffn_norm(n):
                dve.wait_ge(x_attn, n + 1)
                if n > 0:
                    dve.wait_ge(f_xT_ps, n)
                norm(n, half(x, n), stat_f, mv_f, rs_f, xn_f, f_var, f_rstd, f_xn)

            def first_of(ne, value, limit):
                d3 = desc[:, 0:ne].unsqueeze(1).to_broadcast([P, PAIRS, ne])
                done(dve.scalar_tensor_tensor(out=tmp_r[:, :, 0:ne], in0=value, scalar=limit, in1=d3,
                                              op0=ALU.is_equal, op1=ALU.mult))
                done(dve.tensor_reduce(red[:, 3, :], tmp_r[:, :, 0:ne], AX, ALU.max))
                dve.tensor_tensor(onehot[:, :, 0:ne], d3, red[:, 3, :].unsqueeze(2).to_broadcast([P, PAIRS, ne]),
                                  ALU.is_equal).then_inc(hot_sb, 1)

            def route(n):
                l, h = n // HALVES, n % HALVES
                r = n if l == 0 else n - 2
                ne = {0: E0, 2: E2, 3: E3}[l]
                dve.wait_ge(lg_ps, r + 1)
                if r > 0:
                    dve.wait_ge(hotT_ps, r)
                lg = up[1][:, 0:PAIRS * ne].rearrange("p (t e) -> p t e", e=ne)
                lo = logit[:, :, 0:ne]
                if l == 2:
                    done(dve.tensor_tensor(lo, lg, rb_b[:].unsqueeze(1).to_broadcast([P, PAIRS, ne]), ALU.add))
                    lg = lo
                done(dve.tensor_reduce(red[:, 0, :], lg, AX, ALU.max))
                if l == 3 and h == 0 or l == 0:
                    dve.wait_ge(gf_sb, 1)
                ins = dve.tensor_tensor(lo, lg, red[:, 0, :].unsqueeze(2).to_broadcast([P, PAIRS, ne]), ALU.subtract)
                if l == 2:
                    done(ins)
                    first_of(ne, lo, 0.0)
                    return
                k = r if l == 0 else r - 2
                ins.then_inc(lg_max, 1)
                dve.wait_ge(lg_exp, k + 1)
                ex = expo[:, :, 0:ne]
                done(dve.tensor_reduce(red[:, 1, :], ex, AX, ALU.add))
                done(dve.reciprocal(red[:, 2, :], red[:, 1, :]))
                if l == 0:
                    done(dve.tensor_scalar(wg[:], red[:, 2, :], gf[:, 0:1], None, ALU.mult))
                    first_of(ne, lo, 0.0)
                    return
                done(dve.tensor_tensor(ex, ex, red[:, 2, :].unsqueeze(2).to_broadcast([P, PAIRS, ne]), ALU.mult))
                done(dve.tensor_reduce(grp[:, :, 0:4], ex.rearrange("p t (g e) -> p t g e", e=4), AX, ALU.max))

                def top_of(width, k, src, dst):
                    for t in range(PAIRS):
                        last = dve.max(top[:, t, :], src[:, t, 0:width])
                    done(last)
                    done(dve.memset(top[:, :, k:8], -3.0))
                    for t in range(PAIRS):
                        last = dve.match_replace(dst[:, t, 0:width], top[:, t, :], src[:, t, 0:width], -2.0)
                    done(last)

                top_of(8, 2, grp, grp2)
                done(dve.tensor_scalar(keep_g[:], grp2[:, :, 0:4], -2.0, None, ALU.is_equal))
                done(dve.tensor_tensor(tmp_r[:].rearrange("p t (g e) -> p t g e", e=4),
                                       ex.rearrange("p t (g e) -> p t g e", e=4),
                                       keep_g[:].unsqueeze(3).to_broadcast([P, PAIRS, 4, 4]), ALU.mult))
                top_of(E3, 4, tmp_r, logit)
                dve.scalar_tensor_tensor(out=onehot[:], in0=logit[:], scalar=-2.0, in1=ex, op0=ALU.is_equal,
                                         op1=ALU.mult).then_inc(hot_sb, 1)
                dve.wait_ge(hotT_ps, r + 1)
                c = up[2][0:E3, :]
                if h == 0:
                    dve.wait_ge(const_set, 1)
                else:
                    dve.wait_ge(c3_ps, C3 - 1)
                done(dve.tensor_copy(cparts[0:E3, :], c))
                done(dve.tensor_tensor(cleft[:, 0, :], c, cparts[0:E3, :], ALU.subtract))
                done(dve.tensor_copy(cparts[32:32 + E3, :], cleft[:, 0, :]))
                done(dve.tensor_copy(maskTb[:], cleft[:, 0, :]))
                done(dve.tensor_tensor(cleft[:, 1, :], cleft[:, 0, :], maskTb[:], ALU.subtract))
                dve.tensor_copy(cparts[64:64 + E3, :], cleft[:, 1, :]).then_inc(parts_sb, 1)

            def chunk(n, i):
                l, h = n // HALVES, n % HALVES
                if l == 0 and i < C0:
                    g = h * C0 + i
                    dve.wait_ge(m0_ps, h * E0 + i // 2 + 1)
                    dve.wait_ge(h0_sb, g + 1)
                    hb = hid[:, i % NH, :]
                    dve.tensor_tensor(hb, hb, up[2][:], ALU.mult).then_inc(hm0_sb, 1)
                if l == 2 and i < C2:
                    g = h * C2 + i
                    e, c = i // 4, i % 4
                    ge = h * E2 + e
                    dve.wait_ge(a2_ps, g + 1)
                    dve.wait_ge(m2_sb, ge + 1)
                    dve.scalar_tensor_tensor(out=am[:, g % 2, :], in0=up[1 + i % 2][:], scalar=cols("b1_2", 8 * e + c),
                                             in1=mB[:, ge % 2, :], op0=ALU.add, op1=ALU.mult).then_inc(am2_sb, 1)
                    dve.wait_ge(am2_sb, g + 1)
                    dve.wait_ge(t2_sb, g + 1)
                    if g >= NH:
                        dve.wait_ge(dn2_ps, g - NH + 1)
                    dve.scalar_tensor_tensor(out=hid[:, i % NH, :], in0=th[:, g % 2, :], scalar=1.0, in1=am[:, g % 2, :],
                                             op0=ALU.add, op1=ALU.mult).then_inc(h2_sb, 1)
                if l == 3 and i < C3:
                    g = h * C3 + i
                    dve.wait_ge(t3_sb, g + 1)
                    dve.scalar_tensor_tensor(out=am[:, g % 2, :], in0=th[:, g % 2, :], scalar=1.0, in1=up[0][:],
                                             op0=ALU.add, op1=ALU.mult).then_inc(u3_sb, 1)
                    dve.wait_ge(u3_sb, g + 1)
                    dve.wait_ge(g3_ps, g + 1)
                    hb = hid[:, i % NH, :]
                    if g >= NH:
                        dve.wait_ge(dn3_ps, g - NH + 1)
                    dve.tensor_tensor(hb, am[:, g % 2, :], up[1][:], ALU.mult).then_inc(v3_sb, 1)
                    if i < C3 - 1:
                        gc = h * (C3 - 1) + i
                        dve.wait_ge(v3_sb, g + 1)
                        dve.wait_ge(c3_ps, gc + 1)
                        dve.tensor_tensor(hb, hb, up[2][:], ALU.mult).then_inc(hm3_sb, 1)

            def channel_mix(n):
                h = n % HALVES
                dve.wait_ge(f_xT, n + 1)
                x3 = xT_f[:].rearrange("p (b s) -> p b s", s=S)
                done(dve.memset(xprev[:, :, 0:1], 0.0))
                done(dve.tensor_copy(xprev[:, :, 1:S], x3[:, :, 0:S - 1]))
                for j, mu in enumerate(("mu_r", "mu_k")):
                    done(dve.tensor_scalar(hid[:, 2 + j, :], hid[:, 0, :], anti_mu[:, j:j + 1], None, ALU.mult))
                    dve.scalar_tensor_tensor(out=am[:, j, :], in0=xT_f[:], scalar=cols(mu), in1=hid[:, 2 + j, :],
                                             op0=ALU.mult, op1=ALU.add).then_inc(mix_sb, 1)
                dve.wait_ge(mrelu_sb, h + 1)
                dve.tensor_tensor(hid[:, 1, :], th[:, 1, :], up[1][:], ALU.mult).then_inc(mka_sb, 1)
                dve.wait_ge(mv_ps, h + 1)
                dve.wait_ge(mt_sb, h + 1)
                if n > 0:
                    dve.wait_ge(yb_ps, n)
                dve.scalar_tensor_tensor(out=yT[:], in0=th[:, 0, :], scalar=1.0, in1=up[2][:],
                                         op0=ALU.add, op1=ALU.mult).then_inc(my_sb, 1)

            def ffn_out(n):
                l = n // HALVES
                dve.wait_ge(yb_ps, n + 1)
                dve.wait_ge(x_attn, n + 1)
                xh = half(x, n)
                if l == 0:
                    for t in range(PAIRS):
                        last = dve.scalar_tensor_tensor(out=xh[:, t, :], in0=up[0][:, t * P:(t + 1) * P],
                                                        scalar=wg[:, t:t + 1], in1=xh[:, t, :],
                                                        op0=ALU.mult, op1=ALU.add)
                else:
                    last = dve.scalar_tensor_tensor(out=flat(xh), in0=up[0][:], scalar=gf[:, l:l + 1], in1=flat(xh),
                                                    op0=ALU.mult, op1=ALU.add)
                last.then_inc(x_ffn, 1)

            parts = {"setup": setup, "attn_norm": attn_norm, "retrieve": retrieve, "scores": scores, "attend": attend,
                     "attn_out": attn_out, "ffn_norm": ffn_norm, "route": route, "chunk": chunk,
                     "channel_mix": channel_mix, "ffn_out": ffn_out}
            for step, *at in PLAN:
                if step in parts:
                    parts[step](*at)


def kernel(**inputs):
    import numpy as _np
    import concourse.bacc as _bacc
    from concourse import mybir as _mybir
    from concourse.bass_utils import run_bass_kernel_spmd as _run

    nc = _bacc.Bacc("TRN2", target_bir_lowering=False, num_devices=1)
    arrays, aps = {}, {}
    for name in inputs:
        a = _np.ascontiguousarray(inputs[name])
        arrays[f"in_{name}_dram"] = a
        aps[name] = nc.dram_tensor(f"in_{name}_dram", a.shape, _mybir.dt.from_np(a.dtype), kind="ExternalInput").ap()
    out = nc.dram_tensor("out_0_dram", (B, S, D), F32, kind="ExternalOutput").ap()
    flamingo_kernel(nc, aps, out)
    r = _run(nc, [arrays], core_ids=[0])
    return r.results[0]["out_0_dram"]
```

```python
from contextlib import ExitStack

import concourse.bass as bass
from concourse import mybir

F32 = mybir.dt.float32
BF16 = mybir.dt.bfloat16
I32 = mybir.dt.int32
ALU = mybir.AluOpType
ACT = mybir.ActivationFunctionType
AX = mybir.AxisListType.X

P = 128
B, S, D = 16, 64, 128
H, DH = 16, 8
LAYERS = 4
HALVES = 2
HB = B // HALVES
TOK = HB * S
PAIRS = HB // 2
HG = 8
HP = H // 2
SCALE = 1.0 / float(DH) ** 0.5
EPS = 1e-5
E0, F0 = 14, 256
E2, F2 = 8, 512
E3, F3 = 16, 64
C0 = E0 * F0 // P
C2 = E2 * F2 // P
C3 = E3 * F3 // P + 1
NH = 4
LAG = 2
LEAST = -3.0e38

COL = {}
for _n, _k in (("bq0", 1), ("bk0", 1), ("bv0", 1), ("bq1", 1), ("bk1", 1), ("bv1", 1), ("bq2", 1), ("bk2", 1),
               ("bv2", 1), ("mu_r", 1), ("mu_k", 1), ("b1_0", C0), ("b1_2", 2 * C2)):
    COL[_n] = (sum(v[1] for v in COL.values()), _k)
NCOL = sum(v[1] for v in COL.values())

W_DIRECT = ["Wq0", "Wk0", "Wv0", "Wo0"]
W_TURNED = ["Wq1", "Wk1", "Wv1", "Wo1", "W_r", "W_k", "W_v", "Wq2", "Wk2", "Wv2", "Wo2", "Wq3", "Wk3", "Wv3", "Wo3",
            "gate"]
SLOT = {n: i for i, n in enumerate(W_DIRECT + W_TURNED)}
TURN_GROUPS = [list(range(g, min(g + 4, len(W_TURNED)))) for g in range(0, len(W_TURNED), 4)]


COST = {"keys": (0.9, 0.9), "values": (1.3, 0.9), "attn_stats": (0.0, 0.0), "attn_norm": (0.4, 5.0), "queries": (0.9, 0.9),
        "find": (0.9, 0.9), "turn_hit": (0.4, 3.5), "fetch": (0.9, 0.9), "scores": (1.8, 0.9), "turn_probs": (0.4, 0.9),
        "attend": (1.3, 0.9), "turn_attn": (0.4, 1.2), "attn_out": (1.0, 0.9), "ffn_stats": (0.0, 0.0),
        "ffn_norm": (0.4, 5.0), "logits": (1.2, 0.9), "turn_route": (0.4, 3.0), "chunk": (1.9, 0.0), "ffn_y": (0.0, 0.0),
        "ffn_out": (0.4, 1.5), "mix": (1.8, 3.0), "mix_out": (0.9, 1.6), "turn_weights": (0.5, 0.3)}


def stream_steps(h):
    steps = []
    for l in range(LAYERS):
        if l == 0:
            steps += [("keys", h, l), ("values", h, l)]
        steps += [("attn_stats", h, l), ("attn_norm", h, l), ("queries", h, l)]
        if l == 3:
            steps += [("find", h, l), ("turn_hit", h, l), ("fetch", h, l), ("keys", h, l), ("values", h, l)]
        steps.append(("scores", h, l, 0))
        for p in range(PAIRS):
            if p + 1 < PAIRS:
                steps.append(("scores", h, l, p + 1))
            steps += [("turn_probs", h, l, p, 0), ("turn_probs", h, l, p, 1), ("attend", h, l, p)]
        steps += [("turn_attn", h, l), ("attn_out", h, l), ("ffn_stats", h, l)]
        if h == 1 and l == 0:
            steps += [("turn_weights", g) for g in range(len(TURN_GROUPS))]
        steps.append(("ffn_norm", h, l))
        if l == 1:
            steps += [("mix", h, l), ("mix_out", h, l)]
        else:
            steps += [("logits", h, l), ("turn_route", h, l)]
            steps += [("chunk", h, l, i) for i in range({0: C0, 2: C2, 3: C3}[l] + LAG)]
        steps.append(("ffn_y", h, l))
        if l + 1 < 3:
            steps += [("keys", h, l + 1), ("values", h, l + 1)]
        steps.append(("ffn_out", h, l))
    return steps


def make_plan():

    def cost(step):
        pe, lat = COST[step[0]]
        if step[0] == "chunk":
            pe = {0: 1.9, 2: 2.6, 3: 2.8}[step[2]]
            lat = {0: 1.5, 2: 1.5, 3: 4.0}[step[2]] if step[3] == 0 else 0.0
        if step[0] == "turn_route" and step[2] == 3:
            lat = 8.0
        if step[0] == "scores" and step[3] > 0:
            lat = 2.8
        if step[0] == "turn_probs":
            lat = 0.9 if step[4] else (4.2 if step[3] == PAIRS - 1 else 0.0)
        return pe, lat

    todo = [stream_steps(h) for h in range(HALVES)]
    at = [0] * HALVES
    end = [0.0] * HALVES
    now, plan = 0.0, [("setup",)]
    while any(at[h] < len(todo[h]) for h in range(HALVES)):
        best = None
        for h in range(HALVES):
            if at[h] < len(todo[h]):
                step = todo[h][at[h]]
                pe, lat = cost(step)
                start = max(now, end[h] + lat)
                key = (start, step[0] == "chunk", -at[h] / len(todo[h]))
                if best is None or key < best[0]:
                    best = (key, h, start + pe, step)
        _, h, now, step = best
        end[h] = now
        at[h] += 1
        plan.append(step)
    return plan


class Half:

    def __init__(self, h, sb, bank, sem):
        def s(name):
            return sem(f"{name}{h}")

        two = bank(f"two{h}", 2)
        self.score = two[:].rearrange("p r (h k) -> p (r h) k", k=S)
        self.score_r = two
        third = bank(f"third{h}", 1)
        self.turn = third[:, 0, :]
        self.misc = self.y = bank(f"fourth{h}", 1)[:, 0, :]
        self.up = [two[:, 0, :], two[:, 1, :], third[:, 0, :]]
        big = sb(f"big{h}", [P, 5 * 1024])
        self.kblk = big[:, 0:2048].rearrange("p (k h t) -> p k h t", k=2, h=HG)
        self.am = big[:, 0:1024].rearrange("p (k t) -> p k t", k=2)
        self.th = big[:, 1024:2048].rearrange("p (k t) -> p k t", k=2)
        self.prob = big[:, 2048:4096].rearrange("p (k h s) -> p k h s", k=2, h=H)
        self.hid = big[:, 2048:4096].rearrange("p (k t) -> p k t", k=NH)
        self.xprev = self.hid[:, 0, :].rearrange("p (b s) -> p b s", s=S)
        self.probT = big[:, 4096:5120].rearrange("p (h t) -> p h t", h=HP)
        self.mB = big[:, 4096:5120].rearrange("p (k t) -> p k t", k=2)
        mid = sb(f"mid{h}", [P, 5, TOK])
        self.qT, self.kT, self.xg, self.attn_o, self.oT = (mid[:, i, :] for i in range(5))
        self.xg = self.xg.rearrange("p (t d) -> p t d", d=D)
        self.attn_o = self.attn_o.rearrange("p (t d) -> p t d", d=D)
        self.yT, self.maskT, self.cleft = mid[:, 4, :], mid[0:E3, 0, :], mid[0:E3, 2:4, :]
        self.hit = self.attn_o
        self.eqm = mid[:, 2, 0:PAIRS * S].rearrange("p (t s) -> p t s", s=S)
        self.memT = self.oT
        self.xn = sb(f"xn{h}", [P, PAIRS, D])
        self.hitT = self.xn[:].rearrange("p t d -> p (t d)")
        self.xT = sb(f"xT{h}", [P, TOK])
        self.vblk = sb(f"vblk{h}", [P, HB, HP, 2, DH + 1])
        self.stat = sb(f"stat{h}", [P, PAIRS, 6])
        self.mv = sb(f"mv{h}", [P, PAIRS, 2])
        self.rs = sb(f"rs{h}", [P, PAIRS])
        self.mx = sb(f"mx{h}", [P, 2, H])
        self.rsum = sb(f"rsum{h}", [P, H])
        self.found = sb(f"found{h}", [P, PAIRS, 2])
        self.logit = sb(f"logit{h}", [P, PAIRS, E3])
        self.expo = sb(f"expo{h}", [P, PAIRS, E3])
        self.marks = sb(f"marks{h}", [P, PAIRS, E3])
        self.onehot = sb(f"onehot{h}", [P, PAIRS, E3])
        self.red = sb(f"red{h}", [P, 4, PAIRS])
        self.wg = sb(f"wg{h}", [P, PAIRS])
        self.grp = sb(f"grp{h}", [P, PAIRS, 8])
        self.grp2 = sb(f"grp2{h}", [P, PAIRS, 8])
        self.top = sb(f"top{h}", [P, PAIRS, 8])
        self.keep_g = sb(f"keep_g{h}", [P, PAIRS, 4])
        self.maskTb = sb(f"maskTb{h}", [E3, TOK], BF16)
        self.cparts = sb(f"cparts{h}", [80, TOK], BF16)
        self.var_sb, self.rstd_sb, self.xn_sb, self.xT_ps, self.xT_sb = map(s, ("var", "rstd", "xn", "xT_ps", "xT_sb"))
        self.x_attn, self.x_ffn = s("x_attn"), s("x_ffn")
        self.xg_sb, self.q_ps, self.q_sb, self.k_ps, self.k_sb = map(s, ("xg_sb", "q_ps", "q_sb", "k_ps", "k_sb"))
        self.kblk_sb, self.v_ps, self.v_sb = map(s, ("kblk_sb", "v_ps", "v_sb"))
        self.find_ps, self.hit_sb, self.hitT_ps, self.hitT_sb = map(s, ("find_ps", "hit_sb", "hitT_ps", "hitT_sb"))
        self.mem_ps, self.mem_sb = map(s, ("mem_ps", "mem_sb"))
        self.score_ps, self.diff_sb, self.prob_sb = map(s, ("score_ps", "diff_sb", "prob_sb"))
        self.probT_ps, self.probT_sb, self.av_ps, self.av_sb = map(s, ("probT_ps", "probT_sb", "av_ps", "av_sb"))
        self.oT_ps, self.oT_sb, self.o_ps = map(s, ("oT_ps", "oT_sb", "o_ps"))
        self.logit_ps, self.logit_sb, self.expo_sb, self.hot_sb = map(s, ("logit_ps", "logit_sb", "expo_sb", "hot_sb"))
        self.hotT_ps, self.hotT_sb, self.parts_sb = map(s, ("hotT_ps", "hotT_sb", "parts_sb"))
        self.mask_ps, self.mask_sb, self.up_ps, self.gate_ps = map(s, ("mask_ps", "mask_sb", "up_ps", "gate_ps"))
        self.act_sb, self.am_sb, self.hid_sb, self.down_ps = map(s, ("act_sb", "am_sb", "hid_sb", "down_ps"))
        self.u3_sb, self.v3_sb, self.c3_ps = map(s, ("u3_sb", "v3_sb", "c3_ps"))
        self.mix_sb, self.mk_ps, self.relu_sb, self.ka_sb, self.mv_ps = map(s, ("mix_sb", "mk_ps", "relu_sb", "ka_sb", "mv_ps"))
        self.y_ps, self.y_sb, self.yb_ps = map(s, ("y_ps", "y_sb", "yb_ps"))


CHUNKS = {0: C0, 2: C2, 3: C3}
CHUNK0 = {0: 0, 2: C0, 3: C0 + C2}
MASK0 = {0: 0, 2: E0}
ROUTE0 = {0: 0, 2: 1, 3: 2}


def flamingo_kernel(nc: bass.Bass, A: dict, out: bass.AP):
    PLAN = make_plan()
    with ExitStack() as ctx:
        def sb(name, shape, dt=F32):
            return ctx.enter_context(nc.sbuf_tensor(name, shape, dt))

        def bank(name, k):
            return ctx.enter_context(nc.psum_tensor(name, [P, k, 512], F32))

        def sem(name):
            return ctx.enter_context(nc.semaphore(name))

        halves = [Half(h, sb, bank, sem) for h in range(HALVES)]

        x = sb("x", [P, 2 * PAIRS, D])
        cx = sb("cx", [P, 2 * PAIRS, D])
        ctxT = sb("ctxT", [P, B * S])
        vecs = sb("vecs", [NCOL, P])
        col = sb("col", [P, NCOL])
        half_bg = sb("half_bg", [P, C2])
        anti_mu = sb("anti_mu", [P, 2])
        wT = sb("wT", [P, len(SLOT), P])
        bo_b = sb("bo_b", [P, 3, D])
        gbo = sb("gbo", [P, 3, D])
        rb_b = sb("rb_b", [P, E2])
        gates = sb("gates", [P, 2 * LAYERS])
        gx = sb("gx", [P, LAYERS])
        gf = sb("gf", [P, LAYERS])
        mask1 = sb("mask1", [P, S], I32)
        mask2 = sb("mask2", [P, 2 * PAIRS, S], I32)
        add1 = sb("add1", [P, S])
        hide2 = sb("hide2", [P, 2 * PAIRS, S], I32)
        hidden_score = sb("hidden_score", [P, 1])
        ident = sb("ident", [P, P])
        head_of = sb("head_of", [P, HG])
        desc = sb("desc", [P, S])
        pick = sb("pick", [E0, E0, P], BF16)
        pick3 = sb("pick3", [80, C3 - 1, P], BF16)
        half_pow = sb("half_pow", [P, PAIRS])
        regA = sb("regA", [P, E0 * F0 * 2])
        w1_0 = regA[:, 0:E0 * F0].rearrange("p (e f) -> p e f", e=E0)
        w2_0 = regA[:, E0 * F0:2 * E0 * F0].rearrange("p (c d) -> p c d", d=D)
        w2_2 = regA[:, 0:C2 * D].rearrange("p (c d) -> p c d", d=D)
        o3 = C2 * D
        w1_3 = regA[:, o3:o3 + E3 * F3].rearrange("p (e f) -> p e f", e=E3)
        w3_3 = regA[:, o3 + E3 * F3:o3 + 2 * E3 * F3].rearrange("p (e f) -> p e f", e=E3)
        w2_3 = regA[:, o3 + 2 * E3 * F3:o3 + 3 * E3 * F3].rearrange("p (c d) -> p c d", d=D)
        ws = sb("ws", [P, 3, P])
        regB = sb("regB", [P, E2 * 2 * F2])
        w_nat = regB[:, 0:len(W_TURNED) * P].rearrange("p (k m) -> p k m", m=P)
        w1_2 = regB[:].rearrange("p (e f) -> p e f", e=E2)
        rw0 = sb("rw0", [P, E0])
        rw2 = sb("rw2", [P, E2])
        b2_0 = sb("b2_0", [E0, D])
        b2_2 = sb("b2_2", [E2, D])
        b2_2x = sb("b2_2x", [E2, D])

        ld = {n: sem("ld_" + n) for n in ("x", "ctx", "vec", "w0", "misc", "f0", "f0b", "wn", "mask", "f2", "w12", "f2b",
                                          "f3")}
        stored = sem("stored")
        ident_set, const_set, zeros_set, pool_seq = map(sem, ("ident_set", "const_set", "zeros_set", "pool_seq"))
        vec_ps, vec_sb, ctx_ps, ctx_sb_act, ctx_sb_dve = map(sem, ("vec_ps", "vec_sb", "ctx_ps", "ctx_sb_act", "ctx_sb_dve"))
        wturn_ps, wturn_sb = sem("wturn_ps"), sem("wturn_sb")
        gates_sb, gf_sb, dve_seq, b2x_sb = map(sem, ("gates_sb", "gf_sb", "dve_seq", "b2x_sb"))

        def part(t, h):
            return t[:, h * PAIRS:(h + 1) * PAIRS]

        def flat(ap):
            return ap.rearrange("p a b -> p (a b)")

        def cols(name, i=0):
            o = COL[name][0] + i
            return col[:, o:o + 1]

        def W(name):
            return wT[:, SLOT[name], :]

        loads, group_size = [], {}

        def load(group, dst, src):
            group_size[group] = group_size.get(group, 0) + 1
            loads.append((group, dst, src))

        def row(v):
            return v.rearrange("(a n) -> a n", a=1)

        xf = A["x"].rearrange("b s d -> (b s) d").rearrange("(t p) d -> p t d", p=P)
        cf = A["ctx_1024"].rearrange("b s d -> (b s) d").rearrange("(t p) d -> p t d", p=P)
        load("ctx", cx[:], cf)
        for nm, src in (("bq0", "L0_xattn_bq"), ("bk0", "L0_xattn_bk"), ("bv0", "L0_xattn_bv"),
                        ("bq1", "L1_xattn_bq"), ("bk1", "L1_xattn_bk"), ("bv1", "L1_xattn_bv"),
                        ("bq2", "L2_xattn_bq"), ("bk2", "L2_xattn_bk"), ("bv2", "L2_xattn_bv"),
                        ("mu_r", "L1_ffn_mu_r"), ("mu_k", "L1_ffn_mu_k")):
            o = COL[nm][0]
            load("vec", vecs[o:o + 1, :], row(A[src]))
        for nm, src, k in (("b1_0", "L0_ffn_b1", C0), ("b1_2", "L2_ffn_b1", 2 * C2)):
            o = COL[nm][0]
            load("vec", vecs[o:o + k, :], A[src].rearrange("e (c p) -> (e c) p", p=P))
        for nm, src in (("Wk0", "L0_xattn_Wk"), ("Wv0", "L0_xattn_Wv"), ("Wq0", "L0_xattn_Wq"), ("Wo0", "L0_xattn_Wo")):
            load("w0", wT[:, SLOT[nm], :], A[src])
        load("x", x[:], xf)
        load("misc", gates[:, 0:LAYERS], A["g_xattn"].partition_broadcast(P))
        load("misc", gates[:, LAYERS:], A["g_ffn"].partition_broadcast(P))
        for l in range(3):
            load("misc", bo_b[:, l, :], A[f"L{l}_xattn_bo"].partition_broadcast(P))
        load("misc", rb_b[:], A["L2_ffn_router_b"].partition_broadcast(P))
        for nm, src in (("Wq1", "L1_xattn_Wq"), ("Wk1", "L1_xattn_Wk"), ("Wv1", "L1_xattn_Wv"), ("Wo1", "L1_xattn_Wo"),
                        ("W_r", "L1_ffn_W_r"), ("W_k", "L1_ffn_W_k"), ("W_v", "L1_ffn_W_v"),
                        ("Wq2", "L2_xattn_Wq"), ("Wk2", "L2_xattn_Wk"), ("Wv2", "L2_xattn_Wv"), ("Wo2", "L2_xattn_Wo"),
                        ("Wq3", "L3_xattn_Wq"), ("Wo3", "L3_xattn_Wc")):
            load("wn", w_nat[:, W_TURNED.index(nm), :], A[src])
        for j, nm in enumerate(("Wk3", "Wv3")):
            for hd in range(H):
                load("wn", w_nat[hd * DH:(hd + 1) * DH, W_TURNED.index(nm), :],
                     A["L3_xattn_Wkv"][j * DH:(j + 1) * DH, :])
        load("wn", w_nat[0:E3, W_TURNED.index("gate"), :], A["L3_ffn_gate_w"])
        load("f0", rw0[:], A["L0_ffn_router_w"])
        load("f0", b2_0[:], A["L0_ffn_b2"])
        load("f0", w1_0, A["L0_ffn_w1"].rearrange("e d f -> d e f"))
        load("f0b", w2_0, A["L0_ffn_w2"].rearrange("e (c p) d -> p (e c) d", p=P))
        for j in range(2):
            load("mask", mask1[j * S:(j + 1) * S, :], A["mask_SxS2_if1"])
        load("mask", mask2[:], A["mask_BxSxS2_ik1"].rearrange("b q k -> (b q) k").rearrange("(t p) k -> p t k", p=P))
        load("f2", rw2[:], A["L2_ffn_router_w"])
        load("f2", b2_2[:], A["L2_ffn_b2"])
        for j, nm in enumerate(("L3_ffn_ws1", "L3_ffn_ws3", "L3_ffn_ws2")):
            load("f2", ws[:, j, :], A[nm])
        load("w12", w1_2, A["L2_ffn_w1"].rearrange("e d f -> d e f"))
        load("f2b", w2_2, A["L2_ffn_w2"].rearrange("e (c p) d -> p (e c) d", p=P))
        load("f3", w1_3, A["L3_ffn_w1"].rearrange("e d f -> d e f"))
        load("f3", w3_3, A["L3_ffn_w3"].rearrange("e d f -> d e f"))
        load("f3", w2_3, A["L3_ffn_w2"].rearrange("(c two) f d -> (two f) c d", two=2))
        out_t = out.rearrange("b s d -> (b s) d").rearrange("(t p) d -> p t d", p=P)

        def loaded(eng, group):
            eng.wait_ge(ld[group], 16 * group_size[group])

        block = ctx.enter_context(nc.Block())

        @block.sync
        def _(sync):
            waited = set()
            for group, dst, src in loads:
                if group == "w12":
                    sync.wait_ge(wturn_ps, len(TURN_GROUPS))
                if group == "f2b":
                    for s in halves:
                        sync.wait_ge(s.down_ps, C0)
                sync.dma_start(dst, src).then_inc(ld[group], 16)
            for h, s in enumerate(halves):
                sync.wait_ge(s.x_ffn, LAYERS)
                sync.dma_start(out_t[:, h * PAIRS:(h + 1) * PAIRS, :], part(x, h)).then_inc(stored, 16)
            sync.wait_ge(stored, 16 * HALVES)

        @block.gpsimd
        def _(pool):
            seq = [0]

            def done(ins):
                seq[0] += 1
                ins.then_inc(pool_seq, 1)
                pool.wait_ge(pool_seq, seq[0])

            def setup():
                done(pool.memset(ident[:], 0.0))
                pool.affine_select(out=ident[:], in_=ident[:], compare_op=ALU.not_equal, fill=1.0, base=0,
                                   pattern=[[-1, P]], channel_multiplier=1).then_inc(ident_set, 1)
                done(pool.memset(head_of[:], 1.0))
                for r in range(2):
                    rows = head_of[64 * r:64 * r + 64, :]
                    done(pool.affine_select(out=rows, in_=rows, compare_op=ALU.is_ge, fill=0.0, base=0,
                                            pattern=[[-DH, HG]], channel_multiplier=1))
                    done(pool.affine_select(out=rows, in_=rows, compare_op=ALU.is_ge, fill=0.0, base=DH - 1,
                                            pattern=[[DH, HG]], channel_multiplier=-1))
                pool.memset(half_pow[:], -0.5)
                done(pool.memset(hidden_score[:], -10000.0 / SCALE))
                for h, s in enumerate(halves):
                    done(pool.memset(s.vblk[:], 0.0))
                    done(pool.memset(s.vblk[0:64, :, :, 0, DH:DH + 1], 1.0))
                    pool.memset(s.vblk[64:P, :, :, 1, DH:DH + 1], 1.0).then_inc(zeros_set, 1)
                    pool.wait_ge(zeros_set, h + 1)

            def setup_routing():
                for s in halves:
                    done(pool.memset(s.cparts[:], 0.0))
                done(pool.memset(pick[:], 0.0))
                done(pool.affine_select(out=pick[:], in_=pick[:], compare_op=ALU.not_equal, fill=1.0, base=0,
                                        pattern=[[-1, E0], [0, P]], channel_multiplier=1))
                done(pool.memset(pick3[:], 0.0))
                for k in range(3):
                    rows = pick3[32 * k:32 * k + E3, :, :].rearrange("p c (two f) -> p c two f", two=2)
                    done(pool.affine_select(out=rows, in_=rows, compare_op=ALU.not_equal, fill=1.0, base=0,
                                            pattern=[[-2, C3 - 1], [-1, 2], [0, F3]], channel_multiplier=1))
                done(pool.iota(desc[:], pattern=[[-1, S]], base=S, channel_multiplier=0,
                               allow_small_or_imprecise_dtypes=True))
                done(pool.memset(halves[0].grp[:], -1.0))
                pool.memset(halves[1].grp[:], -1.0).then_inc(const_set, 1)
                pool.wait_ge(const_set, 1)

            def key_block(s, l, p):
                i = l * PAIRS + p
                if i >= 2:
                    pool.wait_ge(s.score_ps, i - 1)
                pool.tensor_tensor(s.kblk[:, i % 2], s.kT[:, p * P:(p + 1) * P].unsqueeze(1).to_broadcast([P, HG, P]),
                                   head_of[:].unsqueeze(2).to_broadcast([P, HG, P]), ALU.mult).then_inc(s.kblk_sb, 1)

            def keys(h, l):
                s = halves[h]
                pool.wait_ge(s.k_sb, l + 1)
                for p in range(2):
                    key_block(s, l, p)

            def scores(h, l, p):
                if p + 2 < PAIRS:
                    key_block(halves[h], l, p + 2)
                if h == 0 and l == 0 and p == 0:
                    setup_routing()

            def rstd(s, count):
                pool.wait_ge(s.var_sb, count)
                pool.tensor_tensor(s.rs[:], s.mv[:, :, 1], half_pow[:], ALU.pow).then_inc(s.rstd_sb, 1)

            def attn_stats(h, l):
                s = halves[h]
                rstd(s, 2 * l + 1)
                if l < 3:
                    if h == 0 and l == 0:
                        loaded(pool, "misc")
                        pool.wait_ge(gates_sb, 1)
                        for m in range(3):
                            done(pool.tensor_scalar(gbo[:, m, :], bo_b[:, m, :], gx[:, m:m + 1], None, ALU.mult))
                    pool.tensor_tensor(s.xg, part(x, h), gbo[:, l, :].unsqueeze(1).to_broadcast([P, PAIRS, D]),
                                       ALU.add).then_inc(s.xg_sb, 1)

            def ffn_stats(h, l):
                rstd(halves[h], 2 * l + 2)

            steps = {"setup": setup, "keys": keys, "scores": scores, "attn_stats": attn_stats, "ffn_stats": ffn_stats}
            for step, *at in PLAN:
                if step in steps:
                    steps[step](*at)

        @block.scalar
        def _(act):
            def setup():
                act.wait_ge(ctx_ps, 1)
                act.activation(ctxT[:, 0:512], halves[0].up[0], ACT.Copy).then_inc(ctx_sb_act, 1)

            def set_gates():
                loaded(act, "misc")
                act.activation(gx[:], gates[:, 0:LAYERS], ACT.Tanh).then_inc(gates_sb, 1)
                act.activation(gf[:], gates[:, LAYERS:], ACT.Tanh).then_inc(gates_sb, 1)

            def turn_weights(g):
                act.wait_ge(wturn_ps, g + 1)
                lo = len(W_DIRECT) + TURN_GROUPS[g][0]
                k = len(TURN_GROUPS[g])
                act.activation(wT[:, lo:lo + k, :], halves[1].up[g % 3][:, 0:k * P].rearrange("p (k m) -> p k m", k=k),
                               ACT.Copy).then_inc(wturn_sb, 1)

            def keys(h, l):
                s = halves[h]
                if l == 0:
                    act.wait_ge(vec_sb, 1)
                act.wait_ge(s.k_ps, l + 1)
                if l > 0:
                    act.wait_ge(s.kblk_sb, PAIRS * l)
                if l < 3:
                    act.activation(s.kT, s.misc, ACT.Identity, bias=cols(f"bk{l}")).then_inc(s.k_sb, 1)
                else:
                    act.activation(s.kT, s.misc, ACT.Copy).then_inc(s.k_sb, 1)

            def values(h, l):
                s = halves[h]
                act.wait_ge(s.v_ps, l + 1)
                if l == 0:
                    act.wait_ge(zeros_set, h + 1)
                for j in range(2):
                    rows = slice(64 * j, 64 * j + 64)
                    last = act.activation(s.vblk[rows, :, :, j, 0:DH],
                                          s.misc[rows, :].rearrange("p (b h d) -> p b h d", b=HB, h=HP), ACT.Copy)
                last.then_inc(s.v_sb, 1)
                if l == 0 and h == 0:
                    set_gates()

            def attn_norm(h, l):
                s = halves[h]
                act.wait_ge(s.xT_ps, 2 * l + 1)
                act.activation(s.xT[:], s.misc, ACT.Copy).then_inc(s.xT_sb, 1)

            def queries(h, l):
                s = halves[h]
                act.wait_ge(s.q_ps, l + 1)
                if l < 3:
                    act.activation(s.qT, s.misc, ACT.Identity, bias=cols(f"bq{l}")).then_inc(s.q_sb, 1)
                else:
                    act.activation(s.qT, s.misc, ACT.Copy).then_inc(s.q_sb, 1)

            def turn_hit(h, l):
                s = halves[h]
                act.wait_ge(s.hitT_ps, 1)
                act.activation(s.hitT, s.misc, ACT.Copy).then_inc(s.hitT_sb, 1)

            def fetch(h, l):
                s = halves[h]
                act.wait_ge(s.mem_ps, 1)
                act.activation(s.memT, s.misc, ACT.Copy).then_inc(s.mem_sb, 1)

            def scores(h, l, p):
                s, i = halves[h], l * PAIRS + p
                act.wait_ge(s.diff_sb, i + 1)
                act.activation(s.prob[:, i % 2], s.prob[:, i % 2], ACT.Exp, scale=SCALE).then_inc(s.prob_sb, 1)

            def turn_probs(h, l, p, r):
                s, i = halves[h], l * PAIRS + p
                act.wait_ge(s.probT_ps, 2 * i + r + 1)
                if i > 0:
                    act.wait_ge(s.av_ps, i)
                act.activation(flat(s.probT[:, 4 * r:4 * r + 4, :]), s.turn, ACT.Copy).then_inc(s.probT_sb, 1)

            def turn_attn(h, l):
                s = halves[h]
                act.wait_ge(s.oT_ps, l + 1)
                if l < 3:
                    act.activation(s.oT, s.misc, ACT.Identity, bias=cols(f"bv{l}")).then_inc(s.oT_sb, 1)
                else:
                    act.activation(s.oT, s.misc, ACT.Copy).then_inc(s.oT_sb, 1)

            def ffn_norm(h, l):
                s = halves[h]
                act.wait_ge(s.xT_ps, 2 * l + 2)
                act.activation(s.xT[:], s.up[0], ACT.Copy).then_inc(s.xT_sb, 1)

            def logits(h, l):
                s, ne = halves[h], {0: E0, 2: E2, 3: E3}[l]
                if l != 2:
                    act.wait_ge(s.logit_sb, 1 if l == 0 else 2)
                    act.activation(s.expo[:, :, 0:ne], s.logit[:, :, 0:ne], ACT.Exp).then_inc(s.expo_sb, 1)

            def turn_route(h, l):
                s, ne = halves[h], {0: E0, 2: E2, 3: E3}[l]
                if l != 3:
                    act.wait_ge(s.hotT_ps, ROUTE0[l] + 1)
                    act.activation(s.maskTb[0:ne, :], s.up[2][0:ne, :], ACT.Copy).then_inc(s.hotT_sb, 1)
                    act.activation(s.maskT[0:ne, :], s.up[2][0:ne, :], ACT.Copy).then_inc(s.hotT_sb, 1)

            def chunk(h, l, i):
                s = halves[h]
                if i >= CHUNKS[l]:
                    return
                g = CHUNK0[l] + i
                if l == 2 and i % 4 == 0:
                    e = i // 4
                    act.wait_ge(s.mask_ps, MASK0[2] + e + 1)
                    if e >= 2:
                        act.wait_ge(s.am_sb, 4 * (e - 1))
                    act.activation(s.mB[:, e % 2, :], s.up[0], ACT.Copy).then_inc(s.mask_sb, 1)
                act.wait_ge(s.gate_ps, g + 1)
                if l == 0:
                    if i >= NH:
                        act.wait_ge(s.down_ps, g - NH + 1)
                    act.activation(s.hid[:, i % NH, :], s.up[i % 2], ACT.Gelu, bias=cols("b1_0", i)).then_inc(s.act_sb, 1)
                if l == 2:
                    if i >= 2:
                        act.wait_ge(s.hid_sb, g - 1)
                    act.activation(s.th[:, i % 2, :], s.up[0], ACT.Tanh, bias=half_bg[:, i:i + 1],
                                   scale=0.5).then_inc(s.act_sb, 1)
                if l == 3:
                    if i >= 2:
                        act.wait_ge(s.u3_sb, i - 1)
                    act.activation(s.th[:, i % 2, :], s.up[0], ACT.Tanh, scale=0.5).then_inc(s.act_sb, 1)

            def mix(h, l):
                s = halves[h]
                act.wait_ge(s.mk_ps, 1)
                act.activation(s.th[:, 0, :], s.up[0], ACT.Tanh, scale=0.5).then_inc(s.relu_sb, 1)
                act.wait_ge(s.mk_ps, 2)
                act.activation(s.th[:, 1, :], s.up[1], ACT.Relu).then_inc(s.relu_sb, 1)

            def ffn_y(h, l):
                s = halves[h]
                if l != 1:
                    act.wait_ge(s.down_ps, CHUNK0[l] + CHUNKS[l])
                    if l < 3:
                        act.wait_ge(s.y_ps, ROUTE0[l] + 1)
                    act.activation(s.yT, s.y, ACT.Copy).then_inc(s.y_sb, 1)

            steps = {"setup": setup, "turn_weights": turn_weights, "keys": keys, "values": values, "attn_norm": attn_norm,
                     "queries": queries, "turn_hit": turn_hit, "fetch": fetch, "scores": scores,
                     "turn_probs": turn_probs, "turn_attn": turn_attn, "ffn_norm": ffn_norm, "logits": logits,
                     "turn_route": turn_route, "chunk": chunk, "mix": mix, "ffn_y": ffn_y}
            for step, *at in PLAN:
                if step in steps:
                    steps[step](*at)

        @block.tensor
        def _(pe):
            def turn4(dst, src, n_in=P):
                for t in range(4):
                    last = pe.transpose(dst[0:n_in, t * P:(t + 1) * P], src(t), ident[:])
                return last

            def setup():
                pe.wait_ge(ident_set, 1)
                loaded(pe, "ctx")
                turn4(halves[0].up[0], lambda t: cx[:, t, :]).then_inc(ctx_ps, 1)
                turn4(halves[0].up[1], lambda t: cx[:, 4 + t, :]).then_inc(ctx_ps, 1)
                loaded(pe, "vec")
                pe.transpose(halves[0].up[2][:, 0:NCOL], vecs[:], ident[0:NCOL, 0:NCOL]).then_inc(vec_ps, 1)

            def turn_weights(g):
                if g == 0:
                    loaded(pe, "wn")
                    pe.wait_ge(halves[1].x_attn, 1)
                if g >= 3:
                    pe.wait_ge(wturn_sb, g - 2)
                for j, k in enumerate(TURN_GROUPS[g]):
                    rows = E3 if W_TURNED[k] == "gate" else P
                    last = pe.transpose(halves[1].up[g % 3][:, j * P:j * P + rows], w_nat[0:rows, k, :],
                                        ident[0:rows, 0:rows])
                last.then_inc(wturn_ps, 1)

            def keys(h, l):
                s = halves[h]
                if l == 0:
                    loaded(pe, "w0")
                    pe.wait_ge(ctx_sb_act if h == 0 else ctx_sb_dve, 1)
                elif l == 1:
                    pe.wait_ge(wturn_sb, len(TURN_GROUPS))
                    pe.wait_ge(s.y_sb, 1)
                elif l == 2:
                    pe.wait_ge(s.y_sb, 2)
                else:
                    pe.wait_ge(s.mem_sb, 1)
                src = ctxT[:, h * TOK:(h + 1) * TOK] if l < 3 else s.memT
                pe.matmul(s.misc, W(f"Wk{l}"), src, start=True, stop=True).then_inc(s.k_ps, 1)

            def values(h, l):
                s = halves[h]
                src = ctxT[:, h * TOK:(h + 1) * TOK] if l < 3 else s.memT
                pe.wait_ge(s.k_sb, l + 1)
                w = W(f"Wv{l}").rearrange("p (h j d) -> p j h d", j=2, d=DH)
                for b in range(HB):
                    for j in range(2):
                        last = pe.matmul(s.misc[64 * j:64 * j + 64, b * 64:(b + 1) * 64], src[:, b * S:(b + 1) * S],
                                         w[:, j], start=True, stop=True)
                last.then_inc(s.v_ps, 1)

            def attn_norm(h, l):
                s = halves[h]
                pe.wait_ge(s.xn_sb, 2 * l + 1)
                if l < 3:
                    pe.wait_ge(s.v_sb, l + 1)
                turn4(s.misc, lambda t: s.xn[:, t, :]).then_inc(s.xT_ps, 1)

            def queries(h, l):
                s = halves[h]
                pe.wait_ge(s.xT_sb, 2 * l + 1)
                pe.matmul(s.misc, W(f"Wq{l}"), s.xT[:], start=True, stop=True).then_inc(s.q_ps, 1)

            def find(h, l):
                s = halves[h]
                pe.wait_ge(s.q_sb, l + 1)
                for b in range(HB):
                    last = pe.matmul(s.misc[64 * (b % 2):64 * (b % 2) + 64, (b // 2) * S:(b // 2 + 1) * S],
                                     s.qT[:, b * S:(b + 1) * S], ctxT[:, h * TOK + b * S:h * TOK + (b + 1) * S],
                                     start=True, stop=True)
                last.then_inc(s.find_ps, 1)

            def turn_hit(h, l):
                s = halves[h]
                pe.wait_ge(s.hit_sb, 1)
                turn4(s.misc, lambda t: s.hit[:, t, :]).then_inc(s.hitT_ps, 1)

            def fetch(h, l):
                s = halves[h]
                pe.wait_ge(s.hitT_sb, 1)
                for t in range(PAIRS):
                    tile = slice(t * P, (t + 1) * P)
                    last = pe.matmul(s.misc[:, tile], cx[:, h * PAIRS + t, :], s.hitT[:, tile], start=True, stop=True)
                last.then_inc(s.mem_ps, 1)

            def scores(h, l, p):
                s, i = halves[h], l * PAIRS + p
                pe.wait_ge(s.kblk_sb, i + 1)
                if p == 0:
                    pe.wait_ge(s.q_sb, l + 1)
                    if l == 0:
                        pe.wait_ge(ctx_sb_dve, 1)
                    else:
                        pe.wait_ge(s.x_ffn, l)
                else:
                    pe.wait_ge(s.diff_sb, i)
                for b in range(2):
                    for r in range(2):
                        rows = slice(64 * r, 64 * r + 64)
                        last = pe.matmul(s.score_r[64 * b:64 * b + 64, r, :],
                                         s.qT[rows, (2 * p + b) * S:(2 * p + b + 1) * S],
                                         s.kblk[rows, i % 2, :, b * S:(b + 1) * S], start=True, stop=True)
                last.then_inc(s.score_ps, 1)

            def turn_probs(h, l, p, r):
                s, i = halves[h], l * PAIRS + p
                pe.wait_ge(s.prob_sb, i + 1)
                if i + r > 0:
                    pe.wait_ge(s.probT_sb, 2 * i + r)
                elif h == 0:
                    pe.wait_ge(vec_sb, 1)
                for t in range(4):
                    hp = 4 * r + t
                    last = pe.transpose(s.turn[:, t * P:(t + 1) * P], flat(s.prob[:, i % 2, 2 * hp:2 * hp + 2, :]),
                                        ident[:])
                last.then_inc(s.probT_ps, 1)

            def attend(h, l, p):
                s, i = halves[h], l * PAIRS + p
                pe.wait_ge(s.v_sb, l + 1)
                pe.wait_ge(s.probT_sb, 2 * i + 2)
                if p > 0:
                    pe.wait_ge(s.av_sb, i)
                for hp in range(HP):
                    for b in range(2):
                        v = s.vblk[:, 2 * p + b, hp].rearrange("p j d -> p (j d)")
                        last = pe.matmul(s.misc[64 * b:64 * b + 64, hp * 2 * (DH + 1):(hp + 1) * 2 * (DH + 1)],
                                         s.probT[:, hp, 64 * b:64 * b + 64], v, start=True, stop=True)
                last.then_inc(s.av_ps, 1)

            def turn_attn(h, l):
                s = halves[h]
                pe.wait_ge(s.av_sb, PAIRS * (l + 1))
                turn4(s.misc, lambda t: s.attn_o[:, t, :]).then_inc(s.oT_ps, 1)

            def attn_out(h, l):
                s = halves[h]
                pe.wait_ge(s.oT_sb, l + 1)
                for t in range(PAIRS):
                    tile = slice(t * P, (t + 1) * P)
                    last = pe.matmul(s.misc[:, tile], s.oT[:, tile], W(f"Wo{l}"), start=True, stop=True)
                last.then_inc(s.o_ps, 1)

            def ffn_norm(h, l):
                s = halves[h]
                pe.wait_ge(s.xn_sb, 2 * l + 2)
                if l == 0 and h == 1:
                    pe.wait_ge(wturn_sb, len(TURN_GROUPS))
                turn4(s.up[0], lambda t: s.xn[:, t, :]).then_inc(s.xT_ps, 1)

            def logits(h, l):
                s, ne = halves[h], {0: E0, 2: E2, 3: E3}[l]
                w = {0: rw0[:], 2: rw2[:], 3: W("gate")[:, 0:E3]}[l]
                if l < 3:
                    loaded(pe, {0: "f0", 2: "f2"}[l])
                pe.wait_ge(s.xT_sb, 2 * l + 2)
                for t in range(PAIRS):
                    last = pe.matmul(s.up[1][:, t * ne:(t + 1) * ne], s.xT[:, t * P:(t + 1) * P], w,
                                     start=True, stop=True)
                last.then_inc(s.logit_ps, 1)

            def turn_route(h, l):
                s, ne = halves[h], {0: E0, 2: E2, 3: E3}[l]
                pe.wait_ge(s.hot_sb, ROUTE0[l] + 1)
                turn4(s.up[2], lambda t: s.onehot[:, t, 0:ne], ne).then_inc(s.hotT_ps, 1)

            def up0(s, i):
                g, e, f = i, i // 2, i % 2
                if f == 0:
                    if i == 0:
                        pe.wait_ge(s.hotT_sb, 2)
                    else:
                        pe.wait_ge(s.hid_sb, g)
                    pe.matmul(s.up[2], pick[:, e, :], s.maskTb[0:E0, :], start=True, stop=True).then_inc(s.mask_ps, 1)
                if i >= 2:
                    pe.wait_ge(s.act_sb, g - 1)
                pe.matmul(s.up[i % 2], w1_0[:, e, f * P:(f + 1) * P], s.xT[:], start=True, stop=True).then_inc(s.gate_ps, 1)

            def up2(s, i):
                g, e, c = CHUNK0[2] + i, i // 4, i % 4
                if c == 0:
                    if i == 0:
                        loaded(pe, "w12")
                        pe.wait_ge(s.hotT_sb, 4)
                    else:
                        pe.wait_ge(s.act_sb, g)
                    pe.matmul(s.up[0], pick[0:E2, e, :], s.maskTb[0:E2, :], start=True, stop=True).then_inc(s.mask_ps, 1)
                if i >= 2:
                    pe.wait_ge(s.am_sb, i - 1)
                pe.matmul(s.up[1 + i % 2], w1_2[:, e, c * P:(c + 1) * P], s.xT[:], start=True,
                          stop=True).then_inc(s.up_ps, 1)
                if c == 0:
                    pe.wait_ge(s.mask_sb, e + 1)
                else:
                    pe.wait_ge(s.act_sb, g)
                pe.matmul(s.up[0], w1_2[:, e, F2 + c * P:F2 + (c + 1) * P], s.xT[:], start=True,
                          stop=True).then_inc(s.gate_ps, 1)

            def up3(s, i):
                shared = i == C3 - 1
                if i == 0:
                    loaded(pe, "f3")
                else:
                    pe.wait_ge(s.u3_sb, i)
                w = ws[:, 0, :] if shared else flat(w1_3[:, 2 * i:2 * i + 2, :])
                pe.matmul(s.up[0], w, s.xT[:], start=True, stop=True).then_inc(s.gate_ps, 1)
                if i > 0:
                    pe.wait_ge(s.v3_sb, i)
                w = ws[:, 1, :] if shared else flat(w3_3[:, 2 * i:2 * i + 2, :])
                pe.matmul(s.up[1], w, s.xT[:], start=True, stop=True).then_inc(s.up_ps, 1)
                if not shared:
                    if i == 0:
                        pe.wait_ge(s.parts_sb, 1)
                    else:
                        pe.wait_ge(s.hid_sb, CHUNK0[3] + i)
                    pe.matmul(s.up[2], pick3[:, i, :], s.cparts[:], start=True, stop=True).then_inc(s.c3_ps, 1)

            def chunk(h, l, i):
                s = halves[h]
                if i < CHUNKS[l]:
                    {0: up0, 2: up2, 3: up3}[l](s, i)
                if i >= LAG:
                    j = i - LAG
                    if j == 0 and l < 3:
                        loaded(pe, {0: "f0b", 2: "f2b"}[l])
                        if h == 0 and l == 2:
                            pe.wait_ge(b2x_sb, 1)
                    if l == 3 and j == C3 - 1:
                        pe.wait_ge(s.v3_sb, C3)
                        w = ws[:, 2, :]
                    else:
                        pe.wait_ge(s.hid_sb, CHUNK0[l] + j + 1)
                        w = {0: w2_0, 2: w2_2, 3: w2_3}[l][:, j, :]
                    pe.matmul(s.y, w, s.hid[:, j % NH, :], start=(j == 0),
                              stop=(l == 3 and j == C3 - 1)).then_inc(s.down_ps, 1)
                    if j == CHUNKS[l] - 1 and l < 3:
                        w = b2_0 if l == 0 else b2_2x
                        pe.matmul(s.y, w[:], s.maskT[0:{0: E0, 2: E2}[l], :], start=False, stop=True).then_inc(s.y_ps, 1)

            def mix(h, l):
                s = halves[h]
                pe.wait_ge(s.mix_sb, 1)
                pe.matmul(s.up[0], W("W_r"), s.am[:, 0, :], start=True, stop=True).then_inc(s.mk_ps, 1)
                pe.wait_ge(s.mix_sb, 2)
                pe.matmul(s.up[1], W("W_k"), s.am[:, 1, :], start=True, stop=True).then_inc(s.mk_ps, 1)

            def mix_out(h, l):
                s = halves[h]
                pe.wait_ge(s.ka_sb, 1)
                pe.matmul(s.up[2], W("W_v"), s.hid[:, 1, :], start=True, stop=True).then_inc(s.mv_ps, 1)

            def ffn_out(h, l):
                s = halves[h]
                pe.wait_ge(s.y_sb, l + 1)
                turn4(s.up[0], lambda t: s.yT[:, t * P:(t + 1) * P]).then_inc(s.yb_ps, 1)

            steps = {"setup": setup, "turn_weights": turn_weights, "keys": keys, "values": values, "attn_norm": attn_norm,
                     "queries": queries, "find": find, "turn_hit": turn_hit, "fetch": fetch, "scores": scores,
                     "turn_probs": turn_probs, "attend": attend, "turn_attn": turn_attn, "attn_out": attn_out,
                     "ffn_norm": ffn_norm, "logits": logits, "turn_route": turn_route, "chunk": chunk, "mix": mix,
                     "mix_out": mix_out, "ffn_out": ffn_out}
            for step, *at in PLAN:
                if step in steps:
                    steps[step](*at)

        @block.vector
        def _(dve):
            seq = [0]

            def done(ins):
                seq[0] += 1
                ins.then_inc(dve_seq, 1)
                dve.wait_ge(dve_seq, seq[0])

            def setup():
                dve.wait_ge(ctx_ps, 2)
                dve.tensor_copy(ctxT[:, 512:1024], halves[0].up[1]).then_inc(ctx_sb_dve, 1)
                dve.wait_ge(vec_ps, 1)
                dve.tensor_copy(col[:], halves[0].up[2][:, 0:NCOL]).then_inc(vec_sb, 1)

            def late_setup():
                dve.wait_ge(vec_sb, 1)
                b1 = col[:, COL["b1_2"][0]:COL["b1_2"][0] + 2 * C2].rearrange("p (e two c) -> p e two c", e=E2, two=2)
                done(dve.tensor_scalar(half_bg[:].rearrange("p (e c) -> p e c", e=E2), b1[:, :, 1, :], 0.5, None, ALU.mult))
                o = COL["mu_r"][0]
                done(dve.tensor_scalar(anti_mu[:], col[:, o:o + 2], -1.0, 1.0, ALU.mult, ALU.add))
                dve.wait_ge(gates_sb, 2)
                dve.tensor_scalar(gf[:, 1:LAYERS], gf[:, 1:LAYERS], 0.5, None, ALU.mult).then_inc(gf_sb, 1)

            def mask_setup():
                loaded(dve, "mask")
                done(dve.tensor_scalar(add1[:], mask1[:], 0.0, None, ALU.is_equal))
                done(dve.tensor_scalar(add1[:], add1[:], LEAST, None, ALU.mult))
                done(dve.tensor_scalar(hide2[:], mask2[:], 0.0, None, ALU.is_equal))
                loaded(dve, "f2")
                dve.tensor_scalar(b2_2x[:], b2_2[:], 2.0, None, ALU.mult).then_inc(b2x_sb, 1)

            def stats(h, count):
                s, xt = halves[h], part(x, h)
                for t in range(PAIRS):
                    last = dve.bn_stats(s.stat[:, t, :], xt[:, t, :])
                done(last)
                for t in range(PAIRS):
                    last = dve.bn_aggr(s.mv[:, t, :], s.stat[:, t, :])
                done(last)
                dve.tensor_scalar(s.mv[:, :, 1], s.mv[:, :, 1], EPS, None, ALU.add).then_inc(s.var_sb, 1)
                dve.wait_ge(s.rstd_sb, count)
                for t in range(PAIRS):
                    last = dve.tensor_scalar(s.xn[:, t, :], xt[:, t, :], s.mv[:, t, 0:1], s.rs[:, t:t + 1],
                                             ALU.subtract, ALU.mult)
                last.then_inc(s.xn_sb, 1)

            def attn_stats(h, l):
                s = halves[h]
                if l == 0:
                    loaded(dve, "x")
                else:
                    dve.wait_ge(s.x_ffn, l)
                stats(h, 2 * l + 1)

            def find(h, l):
                s = halves[h]
                sc = s.misc[:, 0:PAIRS * S].rearrange("p (t m) -> p t m", t=PAIRS)
                if h == 0:
                    dve.wait_ge(const_set, 1)
                done(dve.memset(s.hit, 0.0))
                dve.wait_ge(s.find_ps, 1)
                done(dve.tensor_reduce(s.found[:, :, 0], sc, AX, ALU.max))
                done(dve.tensor_tensor(s.eqm, sc, s.found[:, :, 0:1].to_broadcast([P, PAIRS, S]), ALU.is_equal))
                done(dve.tensor_tensor(s.eqm, s.eqm, desc[:].unsqueeze(1).to_broadcast([P, PAIRS, S]), ALU.mult))
                done(dve.tensor_reduce(s.found[:, :, 1], s.eqm, AX, ALU.max))
                for j in range(2):
                    rows = slice(64 * j, 64 * j + 64)
                    last = dve.tensor_tensor(s.hit[rows, :, 64 * j:64 * j + 64],
                                             desc[rows, :].unsqueeze(1).to_broadcast([64, PAIRS, S]),
                                             s.found[rows, :, 1:2].to_broadcast([64, PAIRS, S]), ALU.is_equal)
                    if j == 0:
                        done(last)
                last.then_inc(s.hit_sb, 1)

            def scores(h, l, p):
                s, i = halves[h], l * PAIRS + p
                if h == 0 and i == 0:
                    late_setup()
                if h == 0 and l == 1 and p == 0:
                    mask_setup()
                dve.wait_ge(s.score_ps, i + 1)
                if l == 1:
                    done(dve.tensor_tensor(s.score, s.score, add1[:].unsqueeze(1).to_broadcast([P, H, S]), ALU.add))
                if l == 2:
                    done(dve.copy_predicated(s.score, hide2[:, h * PAIRS + p, :].unsqueeze(1).to_broadcast([P, H, S]),
                                             hidden_score[:].unsqueeze(2).to_broadcast([P, H, S])))
                done(dve.tensor_reduce(s.mx[:, i % 2, :], s.score, AX, ALU.max))
                if p >= 2:
                    dve.wait_ge(s.probT_ps, 2 * (i - 1))
                dve.tensor_tensor(s.prob[:, i % 2], s.score, s.mx[:, i % 2, :].unsqueeze(2).to_broadcast([P, H, S]),
                                  ALU.subtract).then_inc(s.diff_sb, 1)

            def attend(h, l, p):
                s, i = halves[h], l * PAIRS + p
                dve.wait_ge(s.av_ps, i + 1)
                o = s.misc[:, 0:H * (DH + 1)].rearrange("p (h d) -> p h d", d=DH + 1)
                done(dve.reciprocal(s.rsum[:], o[:, :, DH]))
                dve.tensor_tensor(s.attn_o[:, p, :].rearrange("p (h d) -> p h d", d=DH), o[:, :, 0:DH],
                                  s.rsum[:].unsqueeze(2).to_broadcast([P, H, DH]), ALU.mult).then_inc(s.av_sb, 1)

            def attn_out(h, l):
                s = halves[h]
                dve.wait_ge(s.o_ps, l + 1)
                if l < 3:
                    dve.wait_ge(s.xg_sb, l + 1)
                src = s.xg if l < 3 else part(x, h)
                dve.scalar_tensor_tensor(out=flat(part(x, h)), in0=s.misc, scalar=gx[:, l:l + 1], in1=flat(src),
                                         op0=ALU.mult, op1=ALU.add).then_inc(s.x_attn, 1)

            def ffn_stats(h, l):
                dve.wait_ge(halves[h].x_attn, l + 1)
                stats(h, 2 * l + 2)

            def first_of(s, ne):
                d3 = desc[:, 0:ne].unsqueeze(1).to_broadcast([P, PAIRS, ne])
                done(dve.scalar_tensor_tensor(out=s.marks[:, :, 0:ne], in0=s.logit[:, :, 0:ne], scalar=0.0, in1=d3,
                                              op0=ALU.is_equal, op1=ALU.mult))
                done(dve.tensor_reduce(s.red[:, 3, :], s.marks[:, :, 0:ne], AX, ALU.max))
                dve.tensor_tensor(s.onehot[:, :, 0:ne], d3, s.red[:, 3, :].unsqueeze(2).to_broadcast([P, PAIRS, ne]),
                                  ALU.is_equal).then_inc(s.hot_sb, 1)

            def logits(h, l):
                s, ne = halves[h], {0: E0, 2: E2, 3: E3}[l]
                if l == 0:
                    dve.wait_ge(const_set, 1)
                    dve.wait_ge(gf_sb, 1)
                dve.wait_ge(s.logit_ps, ROUTE0[l] + 1)
                lg = s.up[1][:, 0:PAIRS * ne].rearrange("p (t e) -> p t e", e=ne)
                lo = s.logit[:, :, 0:ne]
                if l == 2:
                    done(dve.tensor_tensor(lo, lg, rb_b[:].unsqueeze(1).to_broadcast([P, PAIRS, ne]), ALU.add))
                    lg = lo
                done(dve.tensor_reduce(s.red[:, 0, :], lg, AX, ALU.max))
                less_max = dve.tensor_tensor(lo, lg, s.red[:, 0, :].unsqueeze(2).to_broadcast([P, PAIRS, ne]), ALU.subtract)
                if l == 2:
                    done(less_max)
                    first_of(s, ne)
                    return
                less_max.then_inc(s.logit_sb, 1)
                dve.wait_ge(s.expo_sb, 1 if l == 0 else 2)
                ex = s.expo[:, :, 0:ne]
                done(dve.tensor_reduce(s.red[:, 1, :], ex, AX, ALU.add))
                done(dve.reciprocal(s.red[:, 2, :], s.red[:, 1, :]))
                if l == 0:
                    done(dve.tensor_scalar(s.wg[:], s.red[:, 2, :], gf[:, 0:1], None, ALU.mult))
                    first_of(s, ne)
                    return
                done(dve.tensor_tensor(ex, ex, s.red[:, 2, :].unsqueeze(2).to_broadcast([P, PAIRS, ne]), ALU.mult))
                by_group = ex.rearrange("p t (g e) -> p t g e", e=4)
                done(dve.tensor_reduce(s.grp[:, :, 0:4], by_group, AX, ALU.max))

                def take_top(width, k, src, dst):
                    for t in range(PAIRS):
                        last = dve.max(s.top[:, t, :], src[:, t, 0:width])
                    done(last)
                    done(dve.memset(s.top[:, :, k:8], -3.0))
                    for t in range(PAIRS):
                        last = dve.match_replace(dst[:, t, 0:width], s.top[:, t, :], src[:, t, 0:width], -2.0)
                    done(last)

                take_top(8, 2, s.grp, s.grp2)
                done(dve.tensor_scalar(s.keep_g[:], s.grp2[:, :, 0:4], -2.0, None, ALU.is_equal))
                done(dve.tensor_tensor(s.marks[:].rearrange("p t (g e) -> p t g e", e=4), by_group,
                                       s.keep_g[:].unsqueeze(3).to_broadcast([P, PAIRS, 4, 4]), ALU.mult))
                take_top(E3, 4, s.marks, s.logit)
                dve.scalar_tensor_tensor(out=s.onehot[:], in0=s.logit[:], scalar=-2.0, in1=ex, op0=ALU.is_equal,
                                         op1=ALU.mult).then_inc(s.hot_sb, 1)

            def turn_route(h, l):
                if l < 3:
                    return
                s = halves[h]
                dve.wait_ge(s.hotT_ps, ROUTE0[l] + 1)
                c = s.up[2][0:E3, :]
                done(dve.tensor_copy(s.cparts[0:E3, :], c))
                done(dve.tensor_tensor(s.cleft[:, 0, :], c, s.cparts[0:E3, :], ALU.subtract))
                done(dve.tensor_copy(s.cparts[32:32 + E3, :], s.cleft[:, 0, :]))
                done(dve.tensor_copy(s.maskTb[:], s.cleft[:, 0, :]))
                done(dve.tensor_tensor(s.cleft[:, 1, :], s.cleft[:, 0, :], s.maskTb[:], ALU.subtract))
                dve.tensor_copy(s.cparts[64:64 + E3, :], s.cleft[:, 1, :]).then_inc(s.parts_sb, 1)

            def chunk(h, l, i):
                s = halves[h]
                if i >= CHUNKS[l]:
                    return
                g = CHUNK0[l] + i
                hb = s.hid[:, i % NH, :]
                if l == 0:
                    dve.wait_ge(s.mask_ps, i // 2 + 1)
                    dve.wait_ge(s.act_sb, g + 1)
                    dve.tensor_tensor(hb, hb, s.up[2], ALU.mult).then_inc(s.hid_sb, 1)
                if l == 2:
                    e, c = i // 4, i % 4
                    dve.wait_ge(s.up_ps, i + 1)
                    dve.wait_ge(s.mask_sb, e + 1)
                    dve.scalar_tensor_tensor(out=s.am[:, i % 2, :], in0=s.up[1 + i % 2], scalar=cols("b1_2", 8 * e + c),
                                             in1=s.mB[:, e % 2, :], op0=ALU.add, op1=ALU.mult).then_inc(s.am_sb, 1)
                    dve.wait_ge(s.am_sb, i + 1)
                    dve.wait_ge(s.act_sb, g + 1)
                    if i >= NH:
                        dve.wait_ge(s.down_ps, g - NH + 1)
                    dve.scalar_tensor_tensor(out=hb, in0=s.th[:, i % 2, :], scalar=1.0, in1=s.am[:, i % 2, :],
                                             op0=ALU.add, op1=ALU.mult).then_inc(s.hid_sb, 1)
                if l == 3:
                    dve.wait_ge(s.act_sb, g + 1)
                    dve.scalar_tensor_tensor(out=s.am[:, i % 2, :], in0=s.th[:, i % 2, :], scalar=1.0, in1=s.up[0],
                                             op0=ALU.add, op1=ALU.mult).then_inc(s.u3_sb, 1)
                    dve.wait_ge(s.u3_sb, i + 1)
                    dve.wait_ge(s.up_ps, C2 + i + 1)
                    if i >= NH:
                        dve.wait_ge(s.down_ps, g - NH + 1)
                    dve.tensor_tensor(hb, s.am[:, i % 2, :], s.up[1], ALU.mult).then_inc(s.v3_sb, 1)
                    if i < C3 - 1:
                        dve.wait_ge(s.v3_sb, i + 1)
                        dve.wait_ge(s.c3_ps, i + 1)
                        dve.tensor_tensor(hb, hb, s.up[2], ALU.mult).then_inc(s.hid_sb, 1)

            def mix(h, l):
                s = halves[h]
                dve.wait_ge(s.xT_sb, 2 * l + 2)
                x3 = s.xT[:].rearrange("p (b s) -> p b s", s=S)
                done(dve.memset(s.xprev[:, :, 0:1], 0.0))
                done(dve.tensor_copy(s.xprev[:, :, 1:S], x3[:, :, 0:S - 1]))
                for j, mu in enumerate(("mu_r", "mu_k")):
                    done(dve.tensor_scalar(s.hid[:, 2 + j, :], s.hid[:, 0, :], anti_mu[:, j:j + 1], None, ALU.mult))
                    dve.scalar_tensor_tensor(out=s.am[:, j, :], in0=s.xT[:], scalar=cols(mu), in1=s.hid[:, 2 + j, :],
                                             op0=ALU.mult, op1=ALU.add).then_inc(s.mix_sb, 1)
                dve.wait_ge(s.relu_sb, 2)
                dve.tensor_tensor(s.hid[:, 1, :], s.th[:, 1, :], s.up[1], ALU.mult).then_inc(s.ka_sb, 1)

            def mix_out(h, l):
                s = halves[h]
                dve.wait_ge(s.mv_ps, 1)
                dve.scalar_tensor_tensor(out=s.yT, in0=s.th[:, 0, :], scalar=1.0, in1=s.up[2],
                                         op0=ALU.add, op1=ALU.mult).then_inc(s.y_sb, 1)

            def ffn_out(h, l):
                s, xh = halves[h], part(x, h)
                dve.wait_ge(s.yb_ps, l + 1)
                if l == 0:
                    for t in range(PAIRS):
                        last = dve.scalar_tensor_tensor(out=xh[:, t, :], in0=s.up[0][:, t * P:(t + 1) * P],
                                                        scalar=s.wg[:, t:t + 1], in1=xh[:, t, :],
                                                        op0=ALU.mult, op1=ALU.add)
                else:
                    last = dve.scalar_tensor_tensor(out=flat(xh), in0=s.up[0], scalar=gf[:, l:l + 1], in1=flat(xh),
                                                    op0=ALU.mult, op1=ALU.add)
                last.then_inc(s.x_ffn, 1)

            steps = {"setup": setup, "attn_stats": attn_stats, "find": find, "scores": scores, "attend": attend,
                     "attn_out": attn_out, "ffn_stats": ffn_stats, "logits": logits, "turn_route": turn_route,
                     "chunk": chunk, "mix": mix, "mix_out": mix_out, "ffn_out": ffn_out}
            for step, *at in PLAN:
                if step in steps:
                    steps[step](*at)


def kernel(**inputs):
    import numpy as _np
    import concourse.bacc as _bacc
    from concourse import mybir as _mybir
    from concourse.bass_utils import run_bass_kernel_spmd as _run

    nc = _bacc.Bacc("TRN2", target_bir_lowering=False, num_devices=1)
    arrays, aps = {}, {}
    for name in inputs:
        a = _np.ascontiguousarray(inputs[name])
        arrays[f"in_{name}_dram"] = a
        aps[name] = nc.dram_tensor(f"in_{name}_dram", a.shape, _mybir.dt.from_np(a.dtype), kind="ExternalInput").ap()
    out = nc.dram_tensor("out_0_dram", (B, S, D), F32, kind="ExternalOutput").ap()
    flamingo_kernel(nc, aps, out)
    r = _run(nc, [arrays], core_ids=[0])
    return r.results[0]["out_0_dram"]
```

```python
from contextlib import ExitStack

import concourse.bass as bass
from concourse import mybir

F32 = mybir.dt.float32
BF16 = mybir.dt.bfloat16
I32 = mybir.dt.int32
ALU = mybir.AluOpType
ACT = mybir.ActivationFunctionType
AX = mybir.AxisListType.X

P = 128
B, S, D = 16, 64, 128
H, DH = 16, 8
LAYERS = 4
HALVES = 2
HB = B // HALVES
TOK = HB * S
PAIRS = HB // 2
HG = 8
HP = H // 2
SCALE = 1.0 / float(DH) ** 0.5
EPS = 1e-5
E0, F0 = 14, 256
E2, F2 = 8, 512
E3, F3 = 16, 64
C3 = E3 * F3 // P + 1
NH = 4
LAG = 2
NE = {0: E0, 2: E2}
FW = {0: F0, 2: F2}
TILES = {l: TOK // P + NE[l] - 1 for l in NE}
PER = {0: 2, 2: 1}
STEPS = {l: -(-TILES[l] // PER[l]) for l in NE}
STEP0 = {0: 0, 2: STEPS[0]}
STEPS3 = STEPS[0] + STEPS[2]
GATES3 = STEPS[2]
GROUPS = {l: -(-TILES[l] // 4) for l in NE}
GROUP0 = {0: 0, 2: GROUPS[0]}
TURNED0 = {0: (0, 0), 2: ((GROUPS[0] + 1) // 2, GROUPS[0] // 2)}
SOON = 8
SOON_STEPS = 4
STORES = {0: (5, 3, 1), 2: (4, 4, 3)}
STORE0 = {0: 0, 2: len(STORES[0])}
MAXT = max(TILES.values())
PARTS = 80
LEAST = -3.0e38

COL = {}
for _n, _k in (("bq0", 1), ("bk0", 1), ("bv0", 1), ("bq1", 1), ("bk1", 1), ("bv1", 1), ("bq2", 1), ("bk2", 1),
               ("bv2", 1), ("mu_r", 1), ("mu_k", 1)):
    COL[_n] = (sum(v[1] for v in COL.values()), _k)
NCOL = sum(v[1] for v in COL.values())
NCOL0 = 3

W_DIRECT = ["Wq0", "Wk0", "Wv0", "Wo0"]
W_TURNED = ["Wq1", "Wk1", "Wv1", "Wo1", "W_r", "W_k", "W_v", "Wq2", "Wk2", "Wv2", "Wo2", "Wq3", "Wk3", "Wv3", "Wo3",
            "gate"]
SLOT = {n: i for i, n in enumerate(W_DIRECT + W_TURNED)}
TURN_GROUPS = [list(range(g, min(g + 4, len(W_TURNED)))) for g in range(0, len(W_TURNED), 4)]
TURNS = len(TURN_GROUPS) + 1


MASKING = 1.13
COST = {"keys": (1.37, 3.05), "values": (2.25, 0.90), "attn_stats": (0.00, 0.80), "attn_norm": (1.80, 5.56),
        "queries": (0.90, 0.82), "find": (0.90, 0.00), "turn_hit": (1.07, 7.14), "fetch": (0.37, 0.75),
        "scores": (1.80, 2.89), "second half's scores": (0.00, 1.06), "first scores": (2.48, 0.93),
        "turn_probs": (0.14, 0.17), "second turn_probs": (0.00, 0.92), "last turn_probs": (0.89, 2.24),
        "attend": (0.97, 0.30), "second attend": (0.00, 0.95), "turn_attn": (0.18, 1.40), "attn_out": (1.51, 1.40),
        "ffn_stats": (0.00, 0.39), "ffn_norm": (0.06, 1.14), "logits": (0.60, 1.31), "turn_route": (1.90, 5.39),
        "chunk": (3.38, 3.37), "first chunk": (0.54, 4.44), "ffn_y": (2.10, 2.51), "place": (2.15, 1.60),
        "scatter": (0.70, 3.79), "turn_tiles": (0.40, 0.00), "late turn_tiles": (0.40, 0.00),
        "first turn_tiles": (0.40, 9.54), "tile": (2.74, 0.00), "tile of layer 2": (4.22, 0.37),
        "edge tile": (1.28, 0.00), "gather": (0.28, 2.70), "ffn_out": (0.00, 0.00),
        "ffn_out after gather": (0.92, 5.57), "mix": (0.94, 1.88), "mix_out": (0.01, 2.51),
        "turn_weights": (0.00, 2.29)}
TILES_YIELD = 0.720

DUE = {("act", "scores"): 3.40, ("act", "scores/second"): 5.03, ("dve", "scores/second"): 0.15,
        ("act", "turn_probs"): 0.17, ("act", "tile"): -0.42, ("act", "tile/turned"): -0.19,
        ("act", "chunk"): -0.49, ("act", "attn_norm"): 0.20, ("act", "queries"): -0.15,
        ("act", "turn_tiles"): 0.25, ("act", "keys"): 0.96, ("act", "values"): -0.50, ("act", "turn_attn"): 1.03,
        ("act", "ffn_norm"): 0.42, ("act", "logits"): 3.08, ("act", "mix"): -0.69, ("act", "ffn_y"): 1.72,
        ("dve", "scores"): -0.80, ("dve", "attend"): 0.51, ("dve", "tile"): -1.07, ("dve", "tile/out"): 1.21,
        ("dve", "chunk"): -1.26, ("dve", "chunk/weigh"): -1.22, ("dve", "attn_stats"): 0.88,
        ("dve", "ffn_stats"): -0.30, ("dve", "attn_out"): -1.20, ("dve", "logits"): 0.39, ("dve", "place"): -2.26,
        ("dve", "place/tiles"): 0.80, ("dve", "turn_route"): -1.44, ("dve", "find"): 2.26,
        ("act", "turn_hit"): -0.52, ("act", "fetch"): -0.44, ("sp", "scatter"): -1.73, ("sp", "tile"): -0.98,
        ("dve", "turn_tiles"): 0.32, ("dve", "ffn_out"): 0.36, ("dve", "mix"): -2.58, ("dve", "mix_out"): -1.51,
        ("pool", "keys"): 2.24, ("pool", "scores"): -0.13, ("pool", "attn_stats"): 3.19,
        ("pool", "ffn_stats"): -1.81, ("pool", "scatter"): 2.98, ("pool", "gather"): -2.25}


def in_order(plan, engine, steps):
    due = []
    for n, (time, (name, *at)) in enumerate(plan):
        for k, part in enumerate(p for p in steps if p.split("/")[0] == name):
            masking = MASKING if engine == "act" and name == "scores" and at[1] in (1, 2) else 0.0
            due.append((time + DUE.get((engine, part), 0.0) + masking, n, k, steps[part], at))
    return [(run, at) for *_, run, at in sorted(due, key=lambda d: d[:3])]


def stream_steps(h):
    steps = []
    for l in range(LAYERS):
        steps.append(("attn_stats", h, l))
        if l == 0:
            steps += [("keys", h, l), ("values", h, l)]
        steps += [("attn_norm", h, l), ("queries", h, l)]
        if l == 3:
            steps += [("find", h, l), ("turn_hit", h, l), ("fetch", h, l), ("keys", h, l), ("values", h, l)]
        steps.append(("scores", h, l, 0))
        for p in range(PAIRS):
            if p + 1 < PAIRS:
                steps.append(("scores", h, l, p + 1))
            steps += [("turn_probs", h, l, p, 0), ("turn_probs", h, l, p, 1),
                      ("attend", h, l, p, 0), ("attend", h, l, p, 1)]
        steps += [("turn_attn", h, l), ("attn_out", h, l), ("ffn_stats", h, l)]
        if h == 1 and l == 0:
            steps += [("turn_weights", g) for g in range(TURNS)]
        steps.append(("ffn_norm", h, l))
        if l == 1:
            steps += [("mix", h, l), ("mix_out", h, l)]
        else:
            steps.append(("logits", h, l))
            if l == 3:
                steps += [("turn_route", h, l)] + [("chunk", h, l, i) for i in range(C3 + LAG)]
            else:
                steps += [("place", h, l), ("scatter", h, l)]
                steps += [("turn_tiles", h, l, g) for g in range(SOON // 4)]
                steps += [("tile", h, l, i) for i in range(SOON_STEPS)]
                steps += [("turn_tiles", h, l, g) for g in range(SOON // 4, GROUPS[l])]
                steps += [("tile", h, l, i) for i in range(SOON_STEPS, STEPS[l] + 2)]
        if l % 2:
            steps.append(("ffn_y", h, l))
        if l + 1 < 3:
            steps += [("keys", h, l + 1), ("values", h, l + 1)]
        if l in NE:
            steps.append(("gather", h, l))
        steps.append(("ffn_out", h, l))
    return steps


def make_plan():

    def cost(step):
        name, *at = step
        if name == "scores" and at[2] == 0 or name in ("chunk", "turn_tiles") and at[2] == 0:
            name = "first " + name
        if name == "turn_tiles" and at[2] == SOON // 4:
            name = "late turn_tiles"
        if step == ("scores", 1, 0, 0):
            name = "second half's scores"
        if name == "turn_probs":
            name = "second " + name if at[3] else "last " + name if at[2] == PAIRS - 1 else name
        if name == "attend" and at[3]:
            name = "second attend"
        if name == "tile":
            name = "edge tile" if at[2] in (0, STEPS[at[1]], STEPS[at[1]] + 1) else "tile of layer 2" if at[1] == 2 else name
        if name == "ffn_out" and at[1] in NE:
            name += " after gather"
        pe, latency = COST[name]
        return pe, latency + (MASKING if name in ("scores", "last turn_probs") and at[1] in (1, 2) else 0.0)

    todo = [stream_steps(h) for h in range(HALVES)]
    at = [0] * HALVES
    end = [0.0] * HALVES
    now, plan = 0.0, [(-100.0, ("setup",))]
    while any(at[h] < len(todo[h]) for h in range(HALVES)):
        best = None
        for h in range(HALVES):
            if at[h] < len(todo[h]):
                step = todo[h][at[h]]
                pe, lat = cost(step)
                start = max(now, end[h] + lat)
                late = TILES_YIELD if step[0] in ("chunk", "tile") else 0.0
                key = (start + late, -at[h] / len(todo[h]))
                if best is None or key < best[0]:
                    best = (key, h, start + pe, step)
        _, h, now, step = best
        end[h] = now
        at[h] += 1
        plan.append((now, step))
    return plan


class Half:

    def __init__(self, h, sb, bank, sem):
        def s(name):
            return sem(f"{name}{h}")

        two = bank(f"two{h}", 2)
        self.score = two[:].rearrange("p r (h k) -> p (r h) k", k=S)
        self.score_r = two
        third = bank(f"third{h}", 1)
        self.turn = third[:, 0, :]
        self.misc = self.y = bank(f"fourth{h}", 1)[:, 0, :]
        self.up = [two[:, 0, :], two[:, 1, :], third[:, 0, :]]
        big = sb(f"big{h}", [P, 5 * 1024])
        self.kblk = big[:, 0:2048].rearrange("p (k h t) -> p k h t", k=2, h=HG)
        self.am = big[:, 0:1024].rearrange("p (k t) -> p k t", k=2)
        self.th = big[:, 1024:2048].rearrange("p (k t) -> p k t", k=2)
        self.prob = big[:, 2048:4096].rearrange("p (k h s) -> p k h s", k=2, h=H)
        self.hid = big[:, 2048:4096].rearrange("p (k t) -> p k t", k=NH)
        self.xprev = self.hid[:, 0, :].rearrange("p (b s) -> p b s", s=S)
        self.probT = big[:, 4096:5120].rearrange("p (h t) -> p h t", h=HP)
        n = MAXT * P
        self.xsT = big[:, 0:n]
        self.xs = big[:, n:2 * n].rearrange("p (j d) -> p j d", d=D)
        self.ys = self.xs
        mid = sb(f"mid{h}", [P, 5, TOK])
        self.qT, self.kT, self.xg, self.attn_o, self.oT = (mid[:, i, :] for i in range(5))
        self.xg = self.xg.rearrange("p (t d) -> p t d", d=D)
        self.attn_o = self.attn_o.rearrange("p (t d) -> p t d", d=D)
        self.yT, self.cleft = mid[:, 4, :], mid[0:E3, 2:4, :]
        self.hidn = [mid[:, 0, :], mid[:, 2, :]]
        self.hidT = [mid[:, 3, :], mid[:, 4, :]]
        th1 = sb(f"th1_{h}", [P, TOK])
        self.tht = [big[:, 2 * n:2 * n + TOK], th1[:]]
        self.hit = self.attn_o
        self.eqm = mid[:, 2, 0:PAIRS * S].rearrange("p (t s) -> p t s", s=S)
        self.memT = self.oT
        self.xn = sb(f"xn{h}", [P, PAIRS, D])
        self.hitT = self.xn[:].rearrange("p t d -> p (t d)")
        self.xT = sb(f"xT{h}", [P, TOK])
        self.ytok = self.xn
        self.above = sb(f"above{h}", [P, E0, 4])
        self.ntile = sb(f"ntile{h}", [P, E0])
        self.tri_n = sb(f"tri_n{h}", [P, E0, E0])
        self.first = sb(f"first{h}", [P, E0])
        self.place = sb(f"place{h}", [P, PAIRS, E0])
        self.place_i = sb(f"place_i{h}", [P, PAIRS], I32)
        self.begun = sb(f"begun{h}", [P, MAXT, E0])
        self.tile_e = sb(f"tile_e{h}", [P, MAXT])
        self.tile_ei = sb(f"tile_ei{h}", [P, MAXT], I32)
        self.tile_row = sb(f"tile_row{h}", [PARTS, MAXT, P], BF16)
        self.vblk = sb(f"vblk{h}", [P, HB, HP, 2, DH + 1])
        self.stat = sb(f"stat{h}", [P, PAIRS, 6])
        self.mv = sb(f"mv{h}", [P, PAIRS, 2])
        self.rs = sb(f"rs{h}", [P, PAIRS])
        self.mx = sb(f"mx{h}", [P, 2, H])
        self.rsum = sb(f"rsum{h}", [P, H])
        self.found = sb(f"found{h}", [P, PAIRS, 2])
        self.logit = sb(f"logit{h}", [P, PAIRS, E3])
        self.expo = sb(f"expo{h}", [P, PAIRS, E3])
        self.marks = sb(f"marks{h}", [P, PAIRS, E3])
        self.onehot = sb(f"onehot{h}", [P, PAIRS, E3], BF16)
        self.weight = sb(f"weight{h}", [P, PAIRS, E3])
        self.red = sb(f"red{h}", [P, 4, PAIRS])
        self.wg = sb(f"wg{h}", [P, PAIRS])
        self.grp = sb(f"grp{h}", [P, PAIRS, 8])
        self.grp2 = sb(f"grp2{h}", [P, PAIRS, 8])
        self.top = sb(f"top{h}", [P, PAIRS, 8])
        self.keep_g = sb(f"keep_g{h}", [P, PAIRS, 4])
        self.maskTb = sb(f"maskTb{h}", [E3, TOK], BF16)
        self.cparts = sb(f"cparts{h}", [80, TOK], BF16)
        self.var_sb, self.rstd_sb, self.xn_sb, self.xT_ps, self.xT_sb = map(s, ("var", "rstd", "xn", "xT_ps", "xT_sb"))
        self.x_attn, self.x_ffn = s("x_attn"), s("x_ffn")
        self.xg_sb, self.q_ps, self.q_sb, self.k_ps, self.k_sb = map(s, ("xg_sb", "q_ps", "q_sb", "k_ps", "k_sb"))
        self.kblk_sb, self.v_ps, self.v_sb = map(s, ("kblk_sb", "v_ps", "v_sb"))
        self.memory_ps, self.memory_sb, self.hit_sb = map(s, ("memory_ps", "memory_sb", "hit_sb"))
        self.score_ps, self.diff_sb, self.prob_sb = map(s, ("score_ps", "diff_sb", "prob_sb"))
        self.probT_ps, self.probT_sb, self.av_ps, self.av_sb = map(s, ("probT_ps", "probT_sb", "av_ps", "av_sb"))
        self.oT_ps, self.oT_sb, self.o_ps = map(s, ("oT_ps", "oT_sb", "o_ps"))
        self.logit_ps, self.logit_sb, self.expo_sb, self.hot_sb = map(s, ("logit_ps", "logit_sb", "expo_sb", "hot_sb"))
        self.route_ps, self.parts_sb, self.up_ps, self.gate_ps = map(s, ("route_ps", "parts_sb", "up_ps", "gate_ps"))
        self.act_sb, self.hid_sb, self.down_ps = map(s, ("act_sb", "hid_sb", "down_ps"))
        self.place_sb, self.row_sb = s("place_sb"), s("row_sb")
        self.scattered, self.xs_soon, self.xs_late = map(s, ("scattered", "xs_soon", "xs_late"))
        self.ys_stored, self.gathered = s("ys_stored"), s("gathered")
        self.xsT_ps, self.xsT_dve, self.xsT_act = map(s, ("xsT_ps", "xsT_dve", "xsT_act"))
        self.hidT_ps, self.hidT_sb, self.ys_sb = map(s, ("hidT_ps", "hidT_sb", "ys_sb"))
        self.u3_sb, self.v3_sb, self.c3_ps = map(s, ("u3_sb", "v3_sb", "c3_ps"))
        self.mix_sb, self.mix_ps, self.relu_sb, self.ka_sb = map(s, ("mix_sb", "mix_ps", "relu_sb", "ka_sb"))
        self.y_sb, self.yb_ps = s("y_sb"), s("yb_ps")


ROUTE0 = {0: 0, 2: 1, 3: 2}


def flamingo_kernel(nc: bass.Bass, A: dict, out: bass.AP, x_rows: list, y_rows: list):
    PLAN = make_plan()
    sorted_x, sorted_y = ([r.rearrange("(j p) d -> p j d", p=P) for r in rows] for rows in (x_rows, y_rows))
    with ExitStack() as ctx:
        def sb(name, shape, dt=F32):
            return ctx.enter_context(nc.sbuf_tensor(name, shape, dt))

        def bank(name, k):
            return ctx.enter_context(nc.psum_tensor(name, [P, k, 512], F32))

        def sem(name):
            return ctx.enter_context(nc.semaphore(name))

        halves = [Half(h, sb, bank, sem) for h in range(HALVES)]

        x = sb("x", [P, 2 * PAIRS, D])
        cx = sb("cx", [P, 2 * PAIRS, D])
        ctxT = sb("ctxT", [P, B * S])
        vecs0 = sb("vecs0", [NCOL0, P])
        vecs = sb("vecs", [NCOL - NCOL0, P])
        col = sb("col", [P, NCOL])
        anti_mu = sb("anti_mu", [P, 2])
        wT = sb("wT", [P, len(SLOT), P])
        bo_b = sb("bo_b", [P, 3, D])
        gbo = sb("gbo", [P, 3, D])
        rb_b = sb("rb_b", [P, E2])
        gates = sb("gates", [P, 2 * LAYERS])
        gx = sb("gx", [P, LAYERS])
        gf = sb("gf", [P, LAYERS])
        mask1 = sb("mask1", [P, S], I32)
        mask2 = sb("mask2", [P, 2 * PAIRS, S], I32)
        add1 = sb("add1", [P, S])
        hide2 = sb("hide2", [P, 2 * PAIRS, S], I32)
        hidden_score = sb("hidden_score", [P, 1])
        ident = sb("ident", [P, P])
        head_of = sb("head_of", [P, HG])
        desc = sb("desc", [P, S])
        ones = sb("ones", [P, P], BF16)
        before = sb("before", [P, P], BF16)
        tile_at = sb("tile_at", [P, MAXT])
        tri = sb("tri", [P, E0, E0])
        part_row = sb("part_row", [PARTS, 1])
        pick3 = sb("pick3", [80, C3 - 1, P], BF16)
        half_pow = sb("half_pow", [P, PAIRS])
        regA = sb("regA", [P, E0 * F0 * 2])
        w1_0 = regA[:, 0:E0 * F0].rearrange("p (e f) -> p e f", e=E0)
        w2_0 = regA[:, E0 * F0:2 * E0 * F0].rearrange("p (c d) -> p c d", d=D)
        o3 = E2 * F2
        w2_2 = regA[:, 0:o3].rearrange("p (c d) -> p c d", d=D)
        w1_3 = regA[:, o3:o3 + E3 * F3].rearrange("p (e f) -> p e f", e=E3)
        w3_3 = regA[:, o3 + E3 * F3:o3 + 2 * E3 * F3].rearrange("p (e f) -> p e f", e=E3)
        w2_3 = regA[:, o3 + 2 * E3 * F3:o3 + 3 * E3 * F3].rearrange("p (c d) -> p c d", d=D)
        ws = sb("ws", [P, 3, P])
        regB = sb("regB", [P, E2 * 2 * F2])
        w_nat = regB[:, 0:len(W_TURNED) * P].rearrange("p (k m) -> p k m", m=P)
        w1_2 = regB[:].rearrange("p (e f) -> p e f", e=E2)
        rw0 = sb("rw0", [P, E0])
        rw2 = sb("rw2", [P, E2])
        o2 = len(W_TURNED) * P
        bias0 = regB[0:E0, o2:o2 + F0 + D]
        o2 += F0 + D
        bias2 = regB[0:E2, o2:o2 + 2 * F2 + D]
        bias_p = {0: sb("bias_p0", [PARTS, F0 + D], BF16), 2: sb("bias_p2", [PARTS, 2 * F2 + D], BF16)}
        bias_mid = sb("bias_mid", [E0, 2 * F2 + D], BF16)

        ld = {n: sem("ld_" + n) for n in ("x", "ctx", "vec0", "vec", "w0", "misc", "f0", "f0b", "wn", "bias", "mask", "f2", "w12", "f2b",
                                          "f3")}
        stored = sem("stored")
        ident_set, const_set, zeros_set, pool_seq = map(sem, ("ident_set", "const_set", "zeros_set", "pool_seq"))
        vec_ps, vec_sb, ctx_ps, ctx_sb_act, ctx_sb_dve = map(sem, ("vec_ps", "vec_sb", "ctx_ps", "ctx_sb_act", "ctx_sb_dve"))
        wturn_ps, wturn_sb = sem("wturn_ps"), sem("wturn_sb")
        gates_sb, gf_sb, dve_seq = map(sem, ("gates_sb", "gf_sb", "dve_seq"))
        bias_sb, xs_zero, padded, filled = map(sem, ("bias_sb", "xs_zero", "padded", "filled"))

        def part(t, h):
            return t[:, h * PAIRS:(h + 1) * PAIRS]

        def flat(ap):
            return ap.rearrange("p a b -> p (a b)")

        def cols(name, i=0):
            o = COL[name][0] + i
            return col[:, o:o + 1]

        def W(name):
            return wT[:, SLOT[name], :]

        loads, group_size = [], {}

        def load(group, dst, src):
            group_size[group] = group_size.get(group, 0) + 1
            loads.append((group, dst, src))

        def row(v):
            return v.rearrange("(a n) -> a n", a=1)

        xf = A["x"].rearrange("b s d -> (b s) d").rearrange("(t p) d -> p t d", p=P)
        cf = A["ctx_1024"].rearrange("b s d -> (b s) d").rearrange("(t p) d -> p t d", p=P)
        load("ctx", cx[:], cf)
        load("x", x[:], xf)
        for nm, src in (("Wk0", "L0_xattn_Wk"), ("Wv0", "L0_xattn_Wv"), ("Wq0", "L0_xattn_Wq"), ("Wo0", "L0_xattn_Wo")):
            load("w0", wT[:, SLOT[nm], :], A[src])
        for nm, src in (("bq0", "L0_xattn_bq"), ("bk0", "L0_xattn_bk"), ("bv0", "L0_xattn_bv"),
                        ("bq1", "L1_xattn_bq"), ("bk1", "L1_xattn_bk"), ("bv1", "L1_xattn_bv"),
                        ("bq2", "L2_xattn_bq"), ("bk2", "L2_xattn_bk"), ("bv2", "L2_xattn_bv"),
                        ("mu_r", "L1_ffn_mu_r"), ("mu_k", "L1_ffn_mu_k")):
            o = COL[nm][0]
            if o < NCOL0:
                load("vec0", vecs0[o:o + 1, :], row(A[src]))
            else:
                load("vec", vecs[o - NCOL0:o - NCOL0 + 1, :], row(A[src]))
        load("misc", gates[:, 0:LAYERS], A["g_xattn"].partition_broadcast(P))
        load("misc", gates[:, LAYERS:], A["g_ffn"].partition_broadcast(P))
        for l in range(3):
            load("misc", bo_b[:, l, :], A[f"L{l}_xattn_bo"].partition_broadcast(P))
        load("misc", rb_b[:], A["L2_ffn_router_b"].partition_broadcast(P))
        for nm, src in (("Wq1", "L1_xattn_Wq"), ("Wk1", "L1_xattn_Wk"), ("Wv1", "L1_xattn_Wv"), ("Wo1", "L1_xattn_Wo"),
                        ("W_r", "L1_ffn_W_r"), ("W_k", "L1_ffn_W_k"), ("W_v", "L1_ffn_W_v"),
                        ("Wq2", "L2_xattn_Wq"), ("Wk2", "L2_xattn_Wk"), ("Wv2", "L2_xattn_Wv"), ("Wo2", "L2_xattn_Wo"),
                        ("Wq3", "L3_xattn_Wq"), ("Wo3", "L3_xattn_Wc")):
            load("wn", w_nat[:, W_TURNED.index(nm), :], A[src])
        for j, nm in enumerate(("Wk3", "Wv3")):
            for hd in range(H):
                load("wn", w_nat[hd * DH:(hd + 1) * DH, W_TURNED.index(nm), :],
                     A["L3_xattn_Wkv"][j * DH:(j + 1) * DH, :])
        load("wn", w_nat[0:E3, W_TURNED.index("gate"), :], A["L3_ffn_gate_w"])
        load("f0", rw0[:], A["L0_ffn_router_w"])
        load("f0", w1_0, A["L0_ffn_w1"].rearrange("e d f -> d e f"))
        load("bias", bias0[:, 0:F0], A["L0_ffn_b1"])
        load("bias", bias0[:, F0:], A["L0_ffn_b2"])
        load("bias", bias2[:, 0:2 * F2], A["L2_ffn_b1"])
        load("bias", bias2[:, 2 * F2:], A["L2_ffn_b2"])
        load("f0b", w2_0, A["L0_ffn_w2"].rearrange("e (c p) d -> p (e c) d", p=P))
        for j in range(2):
            load("mask", mask1[j * S:(j + 1) * S, :], A["mask_SxS2_if1"])
        load("mask", mask2[:], A["mask_BxSxS2_ik1"].rearrange("b q k -> (b q) k").rearrange("(t p) k -> p t k", p=P))
        load("f2", rw2[:], A["L2_ffn_router_w"])
        for j, nm in enumerate(("L3_ffn_ws1", "L3_ffn_ws3", "L3_ffn_ws2")):
            load("f2", ws[:, j, :], A[nm])
        load("w12", w1_2, A["L2_ffn_w1"].rearrange("e d f -> d e f"))
        load("f2b", w2_2, A["L2_ffn_w2"].rearrange("e (c p) d -> p (e c) d", p=P))
        load("f3", w1_3, A["L3_ffn_w1"].rearrange("e d f -> d e f"))
        load("f3", w3_3, A["L3_ffn_w3"].rearrange("e d f -> d e f"))
        load("f3", w2_3, A["L3_ffn_w2"].rearrange("(c two) f d -> (two f) c d", two=2))
        out_t = out.rearrange("b s d -> (b s) d").rearrange("(t p) d -> p t d", p=P)

        def loaded(eng, group):
            eng.wait_ge(ld[group], 16 * group_size[group])

        block = ctx.enter_context(nc.Block())

        @block.sync
        def _(sync):
            def load_groups(names):
                for group, dst, src in loads:
                    if group in names:
                        sync.dma_start(dst, src).then_inc(ld[group], 16)

            def setup():
                load_groups(("ctx", "x", "w0", "vec0", "misc"))
                sync.wait_ge(xs_zero, HALVES)
                for s, dram in zip(halves, sorted_x):
                    sync.dma_start(dram, s.xs).then_inc(padded, 16)
                load_groups(("vec", "wn", "f0", "bias", "f0b", "mask", "f2"))

            def turn_weights(g):
                if g + 1 == len(TURN_GROUPS):
                    sync.wait_ge(wturn_ps, len(TURN_GROUPS))
                    sync.wait_ge(bias_sb, 2)
                    load_groups(("w12",))

            def scatter(h, l):
                s = halves[h]
                sync.wait_ge(s.scattered, 16 * PAIRS * (ROUTE0[l] + 1))
                sync.dma_start(s.xs[:, 0:SOON, :], sorted_x[h][:, 0:SOON, :]).then_inc(s.xs_soon, 16)
                late = slice(SOON, TILES[l])
                sync.dma_start(s.xs[:, late, :], sorted_x[h][:, late, :]).then_inc(s.xs_late, 16)

            def tile(h, l, i):
                s, done_steps = halves[h], i - 1
                ends = [sum(STORES[l][:k + 1]) for k in range(len(STORES[l]))]
                if done_steps in ends:
                    first = (done_steps - STORES[l][ends.index(done_steps)]) * PER[l]
                    tiles = slice(first, min(done_steps * PER[l], TILES[l]))
                    sync.wait_ge(s.ys_sb, STEP0[l] + done_steps)
                    sync.dma_start(sorted_y[h][:, tiles, :], s.ys[:, tiles, :]).then_inc(s.ys_stored, 16)

            layer0_left = [0]

            def gather(h, l):
                if l == 0:
                    layer0_left[0] += 1
                    if layer0_left[0] == HALVES:
                        for s in halves:
                            sync.wait_ge(s.down_ps, STEPS[0])
                        load_groups(("f2b", "f3"))

            steps = {"setup": setup, "turn_weights": turn_weights, "scatter": scatter, "tile": tile, "gather": gather}
            for run, at in in_order(PLAN, "sp", steps):
                run(*at)
            for h, s in enumerate(halves):
                sync.wait_ge(s.x_ffn, LAYERS)
                sync.dma_start(out_t[:, h * PAIRS:(h + 1) * PAIRS, :], part(x, h)).then_inc(stored, 16)
            sync.wait_ge(stored, 16 * HALVES)

        @block.gpsimd
        def _(pool):
            seq = [0]

            def done(ins):
                seq[0] += 1
                ins.then_inc(pool_seq, 1)
                pool.wait_ge(pool_seq, seq[0])

            def setup():
                done(pool.memset(ident[:], 0.0))
                pool.affine_select(out=ident[:], in_=ident[:], compare_op=ALU.not_equal, fill=1.0, base=0,
                                   pattern=[[-1, P]], channel_multiplier=1).then_inc(ident_set, 1)
                for s in halves:
                    pool.memset(s.xs, 0.0).then_inc(xs_zero, 1)
                pool.wait_ge(xs_zero, HALVES)
                done(pool.memset(head_of[:], 1.0))
                for r in range(2):
                    rows = head_of[64 * r:64 * r + 64, :]
                    done(pool.affine_select(out=rows, in_=rows, compare_op=ALU.is_ge, fill=0.0, base=0,
                                            pattern=[[-DH, HG]], channel_multiplier=1))
                    done(pool.affine_select(out=rows, in_=rows, compare_op=ALU.is_ge, fill=0.0, base=DH - 1,
                                            pattern=[[DH, HG]], channel_multiplier=-1))
                done(pool.memset(half_pow[:], -0.5))

            def setup_routing():
                pool.wait_ge(filled, 1)
                done(pool.affine_select(out=before[:], in_=before[:], compare_op=ALU.is_ge, fill=0.0, base=-1,
                                        pattern=[[1, P]], channel_multiplier=-1))
                done(pool.affine_select(out=tri[:], in_=tri[:], compare_op=ALU.is_ge, fill=0.0, base=-1,
                                        pattern=[[1, E0], [-1, E0]], channel_multiplier=0))
                done(pool.iota(tile_at[:], pattern=[[P, MAXT]], base=0, channel_multiplier=0,
                               allow_small_or_imprecise_dtypes=True))
                for lo in range(0, PARTS, 32):
                    hi = min(lo + 32, PARTS)
                    done(pool.iota(part_row[lo:hi, :], pattern=[[0, 1]], base=0, channel_multiplier=1,
                                   allow_small_or_imprecise_dtypes=True))
                for k in range(3):
                    rows = pick3[32 * k:32 * k + E3, :, :].rearrange("p c (two f) -> p c two f", two=2)
                    done(pool.affine_select(out=rows, in_=rows, compare_op=ALU.not_equal, fill=1.0, base=0,
                                            pattern=[[-2, C3 - 1], [-1, 2], [0, F3]], channel_multiplier=1))
                pool.iota(desc[:], pattern=[[-1, S]], base=S, channel_multiplier=0,
                          allow_small_or_imprecise_dtypes=True).then_inc(const_set, 1)
                pool.wait_ge(const_set, 1)

            def key_block(s, l, p):
                i = l * PAIRS + p
                if i >= 2:
                    pool.wait_ge(s.score_ps, 2 * (i - 1))
                pool.tensor_tensor(s.kblk[:, i % 2], s.kT[:, p * P:(p + 1) * P].unsqueeze(1).to_broadcast([P, HG, P]),
                                   head_of[:].unsqueeze(2).to_broadcast([P, HG, P]), ALU.mult).then_inc(s.kblk_sb, 1)

            def keys(h, l):
                s = halves[h]
                pool.wait_ge(s.k_sb, l + 1)
                for p in range(2):
                    key_block(s, l, p)

            def scores(h, l, p):
                if p + 2 < PAIRS:
                    key_block(halves[h], l, p + 2)
                if p == 1 and l < 3:
                    s = halves[h]
                    if h == 0 and l == 0:
                        loaded(pool, "misc")
                        pool.wait_ge(gates_sb, 1)
                        for m in range(3):
                            done(pool.tensor_scalar(gbo[:, m, :], bo_b[:, m, :], gx[:, m:m + 1], None, ALU.mult))
                    pool.tensor_tensor(s.xg, part(x, h), gbo[:, l, :].unsqueeze(1).to_broadcast([P, PAIRS, D]),
                                       ALU.add).then_inc(s.xg_sb, 1)
                if h == 0 and l == 0 and p == 1:
                    setup_routing()

            def rstd(s, count):
                pool.wait_ge(s.var_sb, count)
                pool.tensor_tensor(s.rs[:], s.mv[:, :, 1], half_pow[:], ALU.pow).then_inc(s.rstd_sb, 1)

            def attn_stats(h, l):
                s = halves[h]
                rstd(s, 2 * l + 1)

            def ffn_stats(h, l):
                rstd(halves[h], 2 * l + 2)

            def scatter(h, l):
                s = halves[h]
                pool.wait_ge(s.place_sb, ROUTE0[l] + 1)
                pool.wait_ge(s.xn_sb, (2 * l + 2) * PAIRS // 2)
                if l == 0:
                    pool.wait_ge(padded, 16 * HALVES)
                for t in range(PAIRS):
                    pool.indirect_dma_start(x_rows[h], bass.IndirectOffsetOnAxis(ap=s.place_i[:, t:t + 1], axis=0),
                                            s.xn[:, t, :], None).then_inc(s.scattered, 16)

            def gather(h, l):
                s = halves[h]
                pool.wait_ge(s.ys_stored, 16 * (STORE0[l] + len(STORES[l])))
                for t in range(PAIRS):
                    pool.indirect_dma_start(s.ytok[:, t, :], None, y_rows[h],
                                            bass.IndirectOffsetOnAxis(ap=s.place_i[:, t:t + 1], axis=0)
                                            ).then_inc(s.gathered, 16)

            steps = {"setup": setup, "keys": keys, "scores": scores, "attn_stats": attn_stats, "ffn_stats": ffn_stats,
                     "scatter": scatter, "gather": gather}
            for run, at in in_order(PLAN, "pool", steps):
                run(*at)

        @block.scalar
        def _(act):
            def setup():
                act.wait_ge(ctx_ps, 1)
                act.activation(ctxT[:, 0:512], halves[0].up[0], ACT.Copy).then_inc(ctx_sb_act, 1)

            def set_gates():
                loaded(act, "misc")
                act.activation(gx[:], gates[:, 0:LAYERS], ACT.Tanh).then_inc(gates_sb, 1)
                act.activation(gf[:], gates[:, LAYERS:], ACT.Tanh).then_inc(gates_sb, 1)

            def turn_weights(g):
                act.wait_ge(wturn_ps, g + 1)
                if g == TURNS - 1:
                    act.activation(col[:, NCOL0:], halves[1].up[g % 3][:, 0:NCOL - NCOL0], ACT.Copy).then_inc(wturn_sb, 1)
                    return
                lo = len(W_DIRECT) + TURN_GROUPS[g][0]
                k = len(TURN_GROUPS[g])
                act.activation(wT[:, lo:lo + k, :], halves[1].up[g % 3][:, 0:k * P].rearrange("p (k m) -> p k m", k=k),
                               ACT.Copy).then_inc(wturn_sb, 1)

            def keys(h, l):
                s = halves[h]
                if h == 0 and l == 0:
                    act.wait_ge(vec_ps, 1)
                    act.activation(col[:, 0:NCOL0], s.up[2][:, 0:NCOL0], ACT.Copy).then_inc(vec_sb, 1)
                    act.wait_ge(vec_sb, 1)
                act.wait_ge(s.k_ps, l + 1)
                if l > 0:
                    act.wait_ge(s.kblk_sb, PAIRS * l)
                if l < 3:
                    act.activation(s.kT, s.misc, ACT.Identity, bias=cols(f"bk{l}")).then_inc(s.k_sb, 1)
                else:
                    act.activation(s.kT, s.misc, ACT.Copy).then_inc(s.k_sb, 1)

            def values(h, l):
                s = halves[h]
                act.wait_ge(s.v_ps, l + 1)
                if l == 0:
                    act.wait_ge(zeros_set, h + 1)
                for b in range(2):
                    tokens = s.misc[64 * b:64 * b + 64, :].rearrange("p (t h j d) -> p t h j d", t=PAIRS, j=2, d=DH)
                    for j in range(2):
                        dst = s.vblk[64 * j:64 * j + 64].rearrange("p (t b) h j d -> p t b h j d", b=2)
                        last = act.activation(dst[:, :, b, :, j, 0:DH], tokens[:, :, :, j, :], ACT.Copy)
                last.then_inc(s.v_sb, 1)
                if l == 0 and h == 0:
                    set_gates()

            def attn_norm(h, l):
                s = halves[h]
                act.wait_ge(s.xT_ps, 2 * l + 1)
                act.activation(s.xT[:], s.misc, ACT.Copy).then_inc(s.xT_sb, 1)

            def queries(h, l):
                s = halves[h]
                act.wait_ge(s.q_ps, l + 1)
                if l < 3:
                    act.activation(s.qT, s.misc, ACT.Identity, bias=cols(f"bq{l}")).then_inc(s.q_sb, 1)
                else:
                    act.activation(s.qT, s.misc, ACT.Copy).then_inc(s.q_sb, 1)

            def exponent(s, i, r):
                act.wait_ge(s.diff_sb, 2 * i + r + 1)
                pr = s.prob[:, i % 2, r * HG:(r + 1) * HG, :]
                act.activation(pr, pr, ACT.Exp, scale=SCALE).then_inc(s.prob_sb, 1)

            def turn_hit(h, l):
                s = halves[h]
                act.wait_ge(s.memory_ps, 2)
                act.activation(s.hitT, s.misc, ACT.Copy).then_inc(s.memory_sb, 1)

            def fetch(h, l):
                s = halves[h]
                act.wait_ge(s.memory_ps, 3)
                act.activation(s.memT, s.misc, ACT.Copy).then_inc(s.memory_sb, 1)

            def scores(h, l, p):
                s, i = halves[h], l * PAIRS + p
                exponent(s, i, 0)

            def scores_second(h, l, p):
                exponent(halves[h], l * PAIRS + p, 1)

            def turn_probs(h, l, p, r):
                s, i = halves[h], l * PAIRS + p
                act.wait_ge(s.probT_ps, 2 * i + r + 1)
                if i > 0:
                    act.wait_ge(s.av_ps, i)
                act.activation(flat(s.probT[:, 4 * r:4 * r + 4, :]), s.turn, ACT.Copy).then_inc(s.probT_sb, 1)

            def turn_attn(h, l):
                s = halves[h]
                act.wait_ge(s.oT_ps, l + 1)
                if l < 3:
                    act.activation(s.oT, s.misc, ACT.Identity, bias=cols(f"bv{l}")).then_inc(s.oT_sb, 1)
                else:
                    act.activation(s.oT, s.misc, ACT.Copy).then_inc(s.oT_sb, 1)

            def ffn_norm(h, l):
                s = halves[h]
                act.wait_ge(s.xT_ps, 2 * l + 2)
                act.activation(s.xT[:], s.up[0], ACT.Copy).then_inc(s.xT_sb, 1)

            def logits(h, l):
                s, ne = halves[h], {0: E0, 2: E2, 3: E3}[l]
                if l != 2:
                    act.wait_ge(s.logit_sb, 1 if l == 0 else 2)
                    act.activation(s.expo[:, :, 0:ne], s.logit[:, :, 0:ne], ACT.Exp).then_inc(s.expo_sb, 1)

            def turn_tiles(h, l, g):
                s, lo = halves[h], 4 * g * P
                if g % 2:
                    n = min(4 * P, TILES[l] * P - lo)
                    act.wait_ge(s.xsT_ps, GROUP0[l] + g + 1)
                    act.activation(s.xsT[:, lo:lo + n], s.up[g % 3][:, 0:n], ACT.Copy).then_inc(s.xsT_act, 1)

            def tile(h, l, i):
                s, g, n = halves[h], STEP0[l] + i, STEPS[l]
                if i < n:
                    if l == 0:
                        w = min(PER[0], TILES[0] - i * PER[0]) * F0
                        act.wait_ge(s.up_ps, i + 1)
                        if i >= 2:
                            act.wait_ge(s.hidT_ps, i - 1)
                        act.activation(s.hidn[i % 2][:, 0:w], s.up[i % 2][:, 0:w], ACT.Gelu).then_inc(s.act_sb, 1)
                    else:
                        act.wait_ge(s.gate_ps, i + 1)
                        if i >= 2:
                            act.wait_ge(s.hid_sb, i - 1)
                        act.activation(s.tht[i % 2], s.up[0], ACT.Tanh, scale=0.5).then_inc(s.act_sb, 1)

            def tile_turned(h, l, i):
                s, g, n = halves[h], STEP0[l] + i, STEPS[l]
                if 1 <= i <= n:
                    w = min(PER[l], TILES[l] - (i - 1) * PER[l]) * FW[l]
                    act.wait_ge(s.hidT_ps, g)
                    if i >= 3:
                        act.wait_ge(s.down_ps, g - 2)
                    act.activation(s.hidT[(i - 1) % 2][:, 0:w], s.up[2][:, 0:w], ACT.Copy).then_inc(s.hidT_sb, 1)

            def chunk(h, l, i):
                s = halves[h]
                if i < C3:
                    act.wait_ge(s.gate_ps, GATES3 + i + 1)
                    if i >= 2:
                        act.wait_ge(s.u3_sb, i - 1)
                    act.activation(s.th[:, i % 2, :], s.up[0], ACT.Tanh, scale=0.5).then_inc(s.act_sb, 1)

            def mix(h, l):
                s = halves[h]
                act.wait_ge(s.mix_ps, 1)
                act.activation(s.th[:, 0, :], s.up[0], ACT.Tanh, scale=0.5).then_inc(s.relu_sb, 1)
                act.wait_ge(s.mix_ps, 2)
                act.activation(s.th[:, 1, :], s.up[1], ACT.Relu).then_inc(s.relu_sb, 1)

            def ffn_y(h, l):
                s = halves[h]
                if l != 1:
                    act.wait_ge(s.down_ps, STEPS3 + C3)
                    act.activation(s.yT, s.y, ACT.Copy).then_inc(s.y_sb, 1)

            steps = {"setup": setup, "turn_weights": turn_weights, "keys": keys, "values": values, "attn_norm": attn_norm,
                     "queries": queries, "turn_hit": turn_hit, "fetch": fetch, "scores": scores, "scores/second": scores_second,
                     "turn_probs": turn_probs, "turn_attn": turn_attn, "ffn_norm": ffn_norm, "logits": logits,
                     "turn_tiles": turn_tiles, "tile": tile, "tile/turned": tile_turned, "chunk": chunk, "mix": mix,
                     "ffn_y": ffn_y}
            for run, at in in_order(PLAN, "act", steps):
                run(*at)

        @block.tensor
        def _(pe):
            expert_of = {}

            def turn4(dst, src, n_in=P):
                for t in range(4):
                    last = pe.transpose(dst[0:n_in, t * P:(t + 1) * P], src(t), ident[:])
                return last

            def turn_normed(s, dst, before):
                for t in range(PAIRS):
                    if t % 2 == 0:
                        pe.wait_ge(s.xn_sb, (before * PAIRS + t) // 2 + 1)
                    last = pe.transpose(dst[:, t * P:(t + 1) * P], s.xn[:, t, :], ident[:])
                last.then_inc(s.xT_ps, 1)

            def setup():
                pe.wait_ge(ident_set, 1)
                loaded(pe, "ctx")
                turn4(halves[0].up[0], lambda t: cx[:, t, :]).then_inc(ctx_ps, 1)
                turn4(halves[0].up[1], lambda t: cx[:, 4 + t, :]).then_inc(ctx_ps, 1)
                loaded(pe, "vec0")
                pe.transpose(halves[0].up[2][:, 0:NCOL0], vecs0[:], ident[0:NCOL0, 0:NCOL0]).then_inc(vec_ps, 1)

            def turn_weights(g):
                if g == 0:
                    loaded(pe, "wn")
                    pe.wait_ge(halves[1].x_attn, 1)
                if g >= 3:
                    pe.wait_ge(wturn_sb, g - 2)
                if g == TURNS - 1:
                    n = NCOL - NCOL0
                    loaded(pe, "vec")
                    pe.transpose(halves[1].up[g % 3][:, 0:n], vecs[:], ident[0:n, 0:n]).then_inc(wturn_ps, 1)
                    return
                for j, k in enumerate(TURN_GROUPS[g]):
                    rows = E3 if W_TURNED[k] == "gate" else P
                    last = pe.transpose(halves[1].up[g % 3][:, j * P:j * P + rows], w_nat[0:rows, k, :],
                                        ident[0:rows, 0:rows])
                last.then_inc(wturn_ps, 1)

            def keys(h, l):
                s = halves[h]
                if l == 0:
                    loaded(pe, "w0")
                    pe.wait_ge(ctx_sb_act if h == 0 else ctx_sb_dve, 1)
                elif l == 1:
                    pe.wait_ge(wturn_sb, TURNS)
                    pe.wait_ge(s.ys_sb, STEPS[0])
                elif l == 2:
                    pe.wait_ge(s.y_sb, 1)
                else:
                    pe.wait_ge(s.memory_sb, 2)
                src = ctxT[:, h * TOK:(h + 1) * TOK] if l < 3 else s.memT
                pe.matmul(s.misc, W(f"Wk{l}"), src, start=True, stop=True).then_inc(s.k_ps, 1)

            def values(h, l):
                s = halves[h]
                src = ctxT[:, h * TOK:(h + 1) * TOK] if l < 3 else s.memT
                pe.wait_ge(s.k_sb, l + 1)
                for t in range(PAIRS):
                    tile = slice(t * P, (t + 1) * P)
                    last = pe.matmul(s.misc[:, tile], src[:, tile], W(f"Wv{l}"), start=True, stop=True)
                last.then_inc(s.v_ps, 1)

            def attn_norm(h, l):
                s = halves[h]
                if l < 3:
                    pe.wait_ge(s.v_sb, l + 1)
                turn_normed(s, s.misc, 2 * l)

            def queries(h, l):
                s = halves[h]
                pe.wait_ge(s.xT_sb, 2 * l + 1)
                pe.matmul(s.misc, W(f"Wq{l}"), s.xT[:], start=True, stop=True).then_inc(s.q_ps, 1)

            def find(h, l):
                s = halves[h]
                pe.wait_ge(s.q_sb, l + 1)
                for b in range(HB):
                    last = pe.matmul(s.misc[64 * (b % 2):64 * (b % 2) + 64, (b // 2) * S:(b // 2 + 1) * S],
                                     s.qT[:, b * S:(b + 1) * S], ctxT[:, h * TOK + b * S:h * TOK + (b + 1) * S],
                                     start=True, stop=True)
                last.then_inc(s.memory_ps, 1)

            def turn_hit(h, l):
                s = halves[h]
                pe.wait_ge(s.hit_sb, 1)
                turn4(s.misc, lambda t: s.hit[:, t, :]).then_inc(s.memory_ps, 1)

            def fetch(h, l):
                s = halves[h]
                pe.wait_ge(s.memory_sb, 1)
                for t in range(PAIRS):
                    tile = slice(t * P, (t + 1) * P)
                    last = pe.matmul(s.misc[:, tile], cx[:, h * PAIRS + t, :], s.hitT[:, tile], start=True, stop=True)
                last.then_inc(s.memory_ps, 1)

            def scores(h, l, p):
                s, i = halves[h], l * PAIRS + p
                pe.wait_ge(s.kblk_sb, i + 1)
                if p == 0:
                    pe.wait_ge(s.q_sb, l + 1)
                    if l == 0:
                        pe.wait_ge(ctx_sb_dve, 1)
                    else:
                        pe.wait_ge(s.x_ffn, l)
                for r in range(2):
                    rows = slice(64 * r, 64 * r + 64)
                    if p > 0:
                        pe.wait_ge(s.diff_sb, 2 * i + r - 1)
                    for b in range(2):
                        last = pe.matmul(s.score_r[64 * b:64 * b + 64, r, :],
                                         s.qT[rows, (2 * p + b) * S:(2 * p + b + 1) * S],
                                         s.kblk[rows, i % 2, :, b * S:(b + 1) * S], start=True, stop=True)
                    last.then_inc(s.score_ps, 1)

            def turn_probs(h, l, p, r):
                s, i = halves[h], l * PAIRS + p
                pe.wait_ge(s.prob_sb, 2 * i + r + 1)
                if i + r > 0:
                    pe.wait_ge(s.probT_sb, 2 * i + r)
                elif h == 0:
                    pe.wait_ge(vec_sb, 1)
                for t in range(4):
                    hp = 4 * r + t
                    last = pe.transpose(s.turn[:, t * P:(t + 1) * P], flat(s.prob[:, i % 2, 2 * hp:2 * hp + 2, :]),
                                        ident[:])
                last.then_inc(s.probT_ps, 1)

            def attend(h, l, p, r):
                s, i = halves[h], l * PAIRS + p
                if r == 0:
                    pe.wait_ge(s.v_sb, l + 1)
                    if p > 0:
                        pe.wait_ge(s.av_sb, i)
                pe.wait_ge(s.probT_sb, 2 * i + r + 1)
                for hp in range(4 * r, 4 * r + 4):
                    for b in range(2):
                        v = s.vblk[:, 2 * p + b, hp].rearrange("p j d -> p (j d)")
                        last = pe.matmul(s.misc[64 * b:64 * b + 64, hp * 2 * (DH + 1):(hp + 1) * 2 * (DH + 1)],
                                         s.probT[:, hp, 64 * b:64 * b + 64], v, start=True, stop=True)
                if r == 1:
                    last.then_inc(s.av_ps, 1)

            def turn_attn(h, l):
                s = halves[h]
                pe.wait_ge(s.av_sb, PAIRS * (l + 1))
                turn4(s.misc, lambda t: s.attn_o[:, t, :]).then_inc(s.oT_ps, 1)

            def attn_out(h, l):
                s = halves[h]
                pe.wait_ge(s.oT_sb, l + 1)
                for t in range(PAIRS):
                    tile = slice(t * P, (t + 1) * P)
                    last = pe.matmul(s.misc[:, tile], s.oT[:, tile], W(f"Wo{l}"), start=True, stop=True)
                last.then_inc(s.o_ps, 1)

            def ffn_norm(h, l):
                s = halves[h]
                if l == 0 and h == 1:
                    pe.wait_ge(wturn_sb, TURNS)
                turn_normed(s, s.up[0], 2 * l + 1)

            def logits(h, l):
                s, ne = halves[h], {0: E0, 2: E2, 3: E3}[l]
                w = {0: rw0[:], 2: rw2[:], 3: W("gate")[:, 0:E3]}[l]
                if l < 3:
                    loaded(pe, {0: "f0", 2: "f2"}[l])
                pe.wait_ge(s.xT_sb, 2 * l + 2)
                for t in range(PAIRS):
                    last = pe.matmul(s.up[1][:, t * ne:(t + 1) * ne], s.xT[:, t * P:(t + 1) * P], w,
                                     start=True, stop=True)
                last.then_inc(s.logit_ps, 1)

            def turn_route(h, l):
                s = halves[h]
                pe.wait_ge(s.hot_sb, ROUTE0[l] + 1)
                turn4(s.up[2], lambda t: s.weight[:, t, :], E3).then_inc(s.route_ps, 1)

            def place(h, l):
                s, ne = halves[h], NE[l]
                pe.wait_ge(s.hot_sb, ROUTE0[l] + 1)
                rank = s.up[2][:, 0:PAIRS * ne].rearrange("p (t e) -> p t e", e=ne)
                for t in range(PAIRS):
                    pe.matmul(rank[:, t, :], before[:], s.onehot[:, t, 0:ne], start=True, stop=(t == 0))
                    for k in range(t):
                        pe.matmul(rank[:, t, :], ones[:], s.onehot[:, k, 0:ne], start=False, stop=(k == t - 1))
                for t in range(PAIRS):
                    last = pe.matmul(s.up[2][:, 64:64 + ne], ones[:], s.onehot[:, t, 0:ne], start=(t == 0),
                                     stop=(t == PAIRS - 1))
                last.then_inc(s.route_ps, 1)

            def turn_tiles(h, l, g):
                s = halves[h]
                if g == 0:
                    pe.wait_ge(s.xs_soon, 16 * (ROUTE0[l] + 1))
                    pe.wait_ge(s.row_sb, ROUTE0[l] + 1)
                if g == SOON // 4:
                    pe.wait_ge(s.xs_late, 16 * (ROUTE0[l] + 1))
                    pe.wait_ge(s.hidT_sb, STEP0[l] + SOON_STEPS - 1)
                if g > SOON // 4:
                    pe.wait_ge(s.act_sb, STEP0[l] + SOON_STEPS)
                for t in range(4 * g, min(4 * g + 4, TILES[l])):
                    last = pe.transpose(s.up[g % 3][:, (t - 4 * g) * P:(t - 4 * g + 1) * P], s.xs[:, t, :], ident[:])
                last.then_inc(s.xsT_ps, 1)

            def tile(h, l, i):
                s, g, n = halves[h], STEP0[l] + i, STEPS[l]

                def tiles_of(i):
                    return range(i * PER[l], min((i + 1) * PER[l], TILES[l]))

                def product(dst, lhsT, w, j, bias_at):
                    pe.matmul(dst, s.tile_row[:, j, :], bias_p[l][:, bias_at:bias_at + dst.shape[-1]], start=True,
                              stop=False)
                    for k, (a, b) in enumerate(zip(lhsT, w)):
                        last = pe.matmul(dst, a, b, start=False, stop=(k == len(w) - 1))
                    return last

                def read_expert(j):
                    with pe.register(f"tile{h}_{l}_{j}") as reg:
                        pe.reg_load(reg, s.tile_ei[0:1, j:j + 1])
                        expert_of[h, j] = pe.snap(reg, min_val=0, max_val=NE[l] - 1)
                    return expert_of[h, j]

                if i in (0, SOON_STEPS):
                    groups = SOON // 4 if i == 0 else GROUPS[l]
                    pe.wait_ge(s.xsT_dve, TURNED0[l][0] + (groups + 1) // 2)
                    pe.wait_ge(s.xsT_act, TURNED0[l][1] + groups // 2)
                if i == 0:
                    if l == 2:
                        loaded(pe, "w12")
                    pe.wait_ge(bias_sb, 1 if l == 0 else 2)
                if i < n and l == 0:
                    if i >= 2:
                        pe.wait_ge(s.act_sb, i - 1)
                    for j in tiles_of(i):
                        e = read_expert(j)
                        lo = (j % PER[0]) * F0
                        last = product(s.up[i % 2][:, lo:lo + F0], [s.xsT[:, j * P:(j + 1) * P]],
                                       [flat(w1_0[:, bass.ds(e, 1), :])], j, 0)
                    last.then_inc(s.up_ps, 1)
                if i < n and l == 2:
                    e = read_expert(i)
                    xt = [s.xsT[:, i * P:(i + 1) * P]]
                    if i >= 1:
                        pe.wait_ge(s.act_sb, g)
                    product(s.up[0], xt, [flat(w1_2[:, bass.ds(e, 1), F2:2 * F2])], i, F2).then_inc(s.gate_ps, 1)
                    if i >= 1:
                        pe.wait_ge(s.hid_sb, i)
                    product(s.up[1], xt, [flat(w1_2[:, bass.ds(e, 1), 0:F2])], i, 0).then_inc(s.up_ps, 1)
                if 1 <= i <= n:
                    if l == 0:
                        pe.wait_ge(s.act_sb, g)
                    else:
                        pe.wait_ge(s.hid_sb, i)
                    if i >= 2:
                        pe.wait_ge(s.hidT_sb, g - 1)
                    for c in range(len(tiles_of(i - 1)) * FW[l] // P):
                        cs = slice(c * P, (c + 1) * P)
                        last = pe.transpose(s.up[2][:, cs], s.hidn[(i - 1) % 2][:, cs], ident[:])
                    last.then_inc(s.hidT_ps, 1)
                if i >= 2:
                    if i == 2:
                        loaded(pe, {0: "f0b", 2: "f2b"}[l])
                    pe.wait_ge(s.hidT_sb, g - 1)
                    if i >= 3:
                        pe.wait_ge(s.ys_sb, g - 2)
                    n_c = FW[l] // P
                    w2 = {0: w2_0, 2: w2_2}[l].rearrange("p (e c) d -> p e c d", e=NE[l])
                    for k, j in enumerate(tiles_of(i - 2)):
                        e = expert_of.pop((h, j))
                        hid_c = [s.hidT[i % 2][:, c * P:(c + 1) * P] for c in range(k * n_c, (k + 1) * n_c)]
                        w_c = [flat(w2[:, bass.ds(e, 1), c, :]) for c in range(n_c)]
                        last = product(s.y[:, k * P:(k + 1) * P], hid_c, w_c, j, {0: F0, 2: 2 * F2}[l])
                    last.then_inc(s.down_ps, 1)

            def up3(s, i):
                shared = i == C3 - 1
                if i == 0:
                    loaded(pe, "f3")
                else:
                    pe.wait_ge(s.u3_sb, i)
                w = ws[:, 0, :] if shared else flat(w1_3[:, 2 * i:2 * i + 2, :])
                pe.matmul(s.up[0], w, s.xT[:], start=True, stop=True).then_inc(s.gate_ps, 1)
                if i > 0:
                    pe.wait_ge(s.v3_sb, i)
                w = ws[:, 1, :] if shared else flat(w3_3[:, 2 * i:2 * i + 2, :])
                pe.matmul(s.up[1], w, s.xT[:], start=True, stop=True).then_inc(s.up_ps, 1)
                if not shared:
                    if i == 0:
                        pe.wait_ge(s.parts_sb, 1)
                    else:
                        pe.wait_ge(s.hid_sb, GATES3 + i)
                    pe.matmul(s.up[2], pick3[:, i, :], s.cparts[:], start=True, stop=True).then_inc(s.c3_ps, 1)

            def chunk(h, l, i):
                s = halves[h]
                if i < C3:
                    up3(s, i)
                if i >= LAG:
                    j = i - LAG
                    if j == C3 - 1:
                        pe.wait_ge(s.v3_sb, C3)
                        w = ws[:, 2, :]
                    else:
                        pe.wait_ge(s.hid_sb, GATES3 + j + 1)
                        w = w2_3[:, j, :]
                    pe.matmul(s.y, w, s.hid[:, j % NH, :], start=(j == 0), stop=(j == C3 - 1)).then_inc(s.down_ps, 1)

            def mix(h, l):
                s = halves[h]
                pe.wait_ge(s.mix_sb, 1)
                pe.matmul(s.up[0], W("W_r"), s.am[:, 0, :], start=True, stop=True).then_inc(s.mix_ps, 1)
                pe.wait_ge(s.mix_sb, 2)
                pe.matmul(s.up[1], W("W_k"), s.am[:, 1, :], start=True, stop=True).then_inc(s.mix_ps, 1)

            def mix_out(h, l):
                s = halves[h]
                pe.wait_ge(s.ka_sb, 1)
                pe.matmul(s.up[2], W("W_v"), s.hid[:, 1, :], start=True, stop=True).then_inc(s.mix_ps, 1)

            def ffn_out(h, l):
                s = halves[h]
                if l in NE:
                    return
                pe.wait_ge(s.y_sb, l // 2 + 1)
                turn4(s.up[0], lambda t: s.yT[:, t * P:(t + 1) * P]).then_inc(s.yb_ps, 1)

            steps = {"setup": setup, "turn_weights": turn_weights, "keys": keys, "values": values, "attn_norm": attn_norm,
                     "queries": queries, "find": find, "turn_hit": turn_hit, "fetch": fetch, "scores": scores,
                     "turn_probs": turn_probs, "attend": attend, "turn_attn": turn_attn, "attn_out": attn_out,
                     "ffn_norm": ffn_norm, "logits": logits, "turn_route": turn_route, "place": place,
                     "turn_tiles": turn_tiles, "tile": tile, "chunk": chunk, "mix": mix, "mix_out": mix_out, "ffn_out": ffn_out}
            for run, at in in_order(PLAN, "pe", steps):
                run(*at)

        @block.vector
        def _(dve):
            seq = [0]

            def done(ins):
                seq[0] += 1
                ins.then_inc(dve_seq, 1)
                dve.wait_ge(dve_seq, seq[0])

            def fill_values(h):
                s = halves[h]
                done(dve.memset(s.vblk[:], 0.0))
                done(dve.memset(s.vblk[0:64, :, :, 0, DH:DH + 1], 1.0))
                dve.memset(s.vblk[64:P, :, :, 1, DH:DH + 1], 1.0).then_inc(zeros_set, 1)

            def fill():
                dve.memset(hidden_score[:], -10000.0 / SCALE)
                for s in halves:
                    dve.memset(s.cparts[:], 0.0)
                    dve.memset(s.grp[:], -1.0)
                for l in NE:
                    dve.memset(bias_p[l][:], 0.0)
                dve.memset(ones[:], 1.0)
                dve.memset(before[:], 1.0)
                dve.memset(tri[:], float(P))
                dve.memset(pick3[:], 0.0).then_inc(filled, 1)

            def setup():
                fill_values(0)
                fill_values(1)
                dve.wait_ge(ctx_ps, 2)
                dve.tensor_copy(ctxT[:, 512:1024], halves[0].up[1]).then_inc(ctx_sb_dve, 1)

            def late_setup():
                dve.wait_ge(gates_sb, 2)
                dve.tensor_scalar(gf[:, 1:LAYERS], gf[:, 1:LAYERS], 0.5, None, ALU.mult).then_inc(gf_sb, 1)

            def mask_setup():
                dve.wait_ge(wturn_sb, TURNS)
                o = COL["mu_r"][0]
                done(dve.tensor_scalar(anti_mu[:], col[:, o:o + 2], -1.0, 1.0, ALU.mult, ALU.add))
                loaded(dve, "mask")
                done(dve.tensor_scalar(add1[:], mask1[:], 0.0, None, ALU.is_equal))
                done(dve.tensor_scalar(add1[:], add1[:], LEAST, None, ALU.mult))
                done(dve.tensor_scalar(hide2[:], mask2[:], 0.0, None, ALU.is_equal))

            def split_bias(l, src):
                p, mid, ne = bias_p[l], bias_mid[0:NE[l], 0:src.shape[-1]], NE[l]
                if l == 2:
                    done(dve.tensor_scalar(src[:, 2 * F2:], src[:, 2 * F2:], 2.0, None, ALU.mult))
                done(dve.tensor_copy(p[0:ne, :], src))
                done(dve.tensor_tensor(src, src, p[0:ne, :], ALU.subtract))
                done(dve.tensor_copy(p[32:32 + ne, :], src))
                done(dve.tensor_copy(mid, src))
                done(dve.tensor_tensor(src, src, mid, ALU.subtract))
                dve.tensor_copy(p[64:64 + ne, :], src).then_inc(bias_sb, 1)

            def stats(h, count):
                s, xt = halves[h], part(x, h)
                for t in range(PAIRS):
                    last = dve.bn_stats(s.stat[:, t, :], xt[:, t, :])
                done(last)
                for t in range(PAIRS):
                    last = dve.bn_aggr(s.mv[:, t, :], s.stat[:, t, :])
                done(last)
                dve.tensor_scalar(s.mv[:, :, 1], s.mv[:, :, 1], EPS, None, ALU.add).then_inc(s.var_sb, 1)
                dve.wait_ge(s.rstd_sb, count)
                for t in range(PAIRS):
                    last = dve.tensor_scalar(s.xn[:, t, :], xt[:, t, :], s.mv[:, t, 0:1], s.rs[:, t:t + 1],
                                             ALU.subtract, ALU.mult)
                    if t % 2:
                        last.then_inc(s.xn_sb, 1)

            def attn_stats(h, l):
                s = halves[h]
                if l == 0:
                    loaded(dve, "x")
                else:
                    dve.wait_ge(s.x_ffn, l)
                stats(h, 2 * l + 1)
                if h == 0 and l == 0:
                    fill()

            def find(h, l):
                s = halves[h]
                sc = s.misc[:, 0:PAIRS * S].rearrange("p (t m) -> p t m", t=PAIRS)
                if h == 0:
                    dve.wait_ge(const_set, 1)
                done(dve.memset(s.hit, 0.0))
                dve.wait_ge(s.memory_ps, 1)
                done(dve.tensor_reduce(s.found[:, :, 0], sc, AX, ALU.max))
                done(dve.tensor_tensor(s.eqm, sc, s.found[:, :, 0:1].to_broadcast([P, PAIRS, S]), ALU.is_equal))
                done(dve.tensor_tensor(s.eqm, s.eqm, desc[:].unsqueeze(1).to_broadcast([P, PAIRS, S]), ALU.mult))
                done(dve.tensor_reduce(s.found[:, :, 1], s.eqm, AX, ALU.max))
                for j in range(2):
                    rows = slice(64 * j, 64 * j + 64)
                    last = dve.tensor_tensor(s.hit[rows, :, 64 * j:64 * j + 64],
                                             desc[rows, :].unsqueeze(1).to_broadcast([64, PAIRS, S]),
                                             s.found[rows, :, 1:2].to_broadcast([64, PAIRS, S]), ALU.is_equal)
                    if j == 0:
                        done(last)
                last.then_inc(s.hit_sb, 1)

            def scores(h, l, p):
                s, i = halves[h], l * PAIRS + p
                if h == 0 and i == 0:
                    late_setup()
                if h == 0 and l == 0 and p == 2:
                    dve.wait_ge(const_set, 1)
                    loaded(dve, "bias")
                    split_bias(0, bias0)
                if h == 1 and l == 0 and p == 2:
                    split_bias(2, bias2)
                if h == 0 and l == 1 and p == 0:
                    mask_setup()
                less_maximum(s, h, l, p, 0)

            def scores_second(h, l, p):
                less_maximum(halves[h], h, l, p, 1)

            def less_maximum(s, h, l, p, r):
                i = l * PAIRS + p
                heads = slice(r * HG, (r + 1) * HG)
                sc, top = s.score[:, heads, :], s.mx[:, i % 2, heads]
                dve.wait_ge(s.score_ps, 2 * i + r + 1)
                if l == 1:
                    done(dve.tensor_tensor(sc, sc, add1[:].unsqueeze(1).to_broadcast([P, HG, S]), ALU.add))
                if l == 2:
                    done(dve.copy_predicated(sc, hide2[:, h * PAIRS + p, :].unsqueeze(1).to_broadcast([P, HG, S]),
                                             hidden_score[:].unsqueeze(2).to_broadcast([P, HG, S])))
                done(dve.tensor_reduce(top, sc, AX, ALU.max))
                if i == 0:
                    dve.wait_ge(padded, 16 * HALVES)
                if p >= 2:
                    dve.wait_ge(s.probT_ps, 2 * (i - 2) + r + 1)
                dve.tensor_tensor(s.prob[:, i % 2, heads, :], sc, top.unsqueeze(2).to_broadcast([P, HG, S]),
                                  ALU.subtract).then_inc(s.diff_sb, 1)

            def attend(h, l, p, r):
                if r == 0:
                    return
                s, i = halves[h], l * PAIRS + p
                dve.wait_ge(s.av_ps, i + 1)
                o = s.misc[:, 0:H * (DH + 1)].rearrange("p (h d) -> p h d", d=DH + 1)
                done(dve.reciprocal(s.rsum[:], o[:, :, DH]))
                dve.tensor_tensor(s.attn_o[:, p, :].rearrange("p (h d) -> p h d", d=DH), o[:, :, 0:DH],
                                  s.rsum[:].unsqueeze(2).to_broadcast([P, H, DH]), ALU.mult).then_inc(s.av_sb, 1)

            def attn_out(h, l):
                s = halves[h]
                dve.wait_ge(s.o_ps, l + 1)
                if l < 3:
                    dve.wait_ge(s.xg_sb, l + 1)
                src = s.xg if l < 3 else part(x, h)
                dve.scalar_tensor_tensor(out=flat(part(x, h)), in0=s.misc, scalar=gx[:, l:l + 1], in1=flat(src),
                                         op0=ALU.mult, op1=ALU.add).then_inc(s.x_attn, 1)

            def ffn_stats(h, l):
                dve.wait_ge(halves[h].x_attn, l + 1)
                stats(h, 2 * l + 2)

            def first_of(s, ne):
                d3 = desc[:, 0:ne].unsqueeze(1).to_broadcast([P, PAIRS, ne])
                done(dve.scalar_tensor_tensor(out=s.marks[:, :, 0:ne], in0=s.logit[:, :, 0:ne], scalar=0.0, in1=d3,
                                              op0=ALU.is_equal, op1=ALU.mult))
                done(dve.tensor_reduce(s.red[:, 3, :], s.marks[:, :, 0:ne], AX, ALU.max))
                dve.tensor_tensor(s.onehot[:, :, 0:ne], d3, s.red[:, 3, :].unsqueeze(2).to_broadcast([P, PAIRS, ne]),
                                  ALU.is_equal).then_inc(s.hot_sb, 1)

            def logits(h, l):
                s, ne = halves[h], {0: E0, 2: E2, 3: E3}[l]
                if l == 0:
                    dve.wait_ge(const_set, 1)
                    dve.wait_ge(gf_sb, 1)
                dve.wait_ge(s.logit_ps, ROUTE0[l] + 1)
                lg = s.up[1][:, 0:PAIRS * ne].rearrange("p (t e) -> p t e", e=ne)
                lo = s.logit[:, :, 0:ne]
                if l == 2:
                    done(dve.tensor_tensor(lo, lg, rb_b[:].unsqueeze(1).to_broadcast([P, PAIRS, ne]), ALU.add))
                    lg = lo
                done(dve.tensor_reduce(s.red[:, 0, :], lg, AX, ALU.max))
                less_max = dve.tensor_tensor(lo, lg, s.red[:, 0, :].unsqueeze(2).to_broadcast([P, PAIRS, ne]), ALU.subtract)
                if l == 2:
                    done(less_max)
                    first_of(s, ne)
                    return
                less_max.then_inc(s.logit_sb, 1)
                if l == 0:
                    dve.wait_ge(s.logit_sb, 1)
                    first_of(s, ne)
                    return
                dve.wait_ge(s.expo_sb, 2)
                ex = s.expo[:, :, 0:ne]
                done(dve.tensor_reduce(s.red[:, 1, :], ex, AX, ALU.add))
                done(dve.reciprocal(s.red[:, 2, :], s.red[:, 1, :]))
                done(dve.tensor_tensor(ex, ex, s.red[:, 2, :].unsqueeze(2).to_broadcast([P, PAIRS, ne]), ALU.mult))
                by_group = ex.rearrange("p t (g e) -> p t g e", e=4)
                done(dve.tensor_reduce(s.grp[:, :, 0:4], by_group, AX, ALU.max))

                def take_top(width, k, src, dst):
                    for t in range(PAIRS):
                        last = dve.max(s.top[:, t, :], src[:, t, 0:width])
                    done(last)
                    done(dve.memset(s.top[:, :, k:8], -3.0))
                    for t in range(PAIRS):
                        last = dve.match_replace(dst[:, t, 0:width], s.top[:, t, :], src[:, t, 0:width], -2.0)
                    done(last)

                take_top(8, 2, s.grp, s.grp2)
                done(dve.tensor_scalar(s.keep_g[:], s.grp2[:, :, 0:4], -2.0, None, ALU.is_equal))
                done(dve.tensor_tensor(s.marks[:].rearrange("p t (g e) -> p t g e", e=4), by_group,
                                       s.keep_g[:].unsqueeze(3).to_broadcast([P, PAIRS, 4, 4]), ALU.mult))
                take_top(E3, 4, s.marks, s.logit)
                dve.scalar_tensor_tensor(out=s.weight[:], in0=s.logit[:], scalar=-2.0, in1=ex, op0=ALU.is_equal,
                                         op1=ALU.mult).then_inc(s.hot_sb, 1)

            def place(h, l):
                s, ne, nt = halves[h], NE[l], TILES[l]
                dve.wait_ge(s.route_ps, ROUTE0[l] + 1)
                rank = s.up[2][:, 0:PAIRS * ne].rearrange("p (t e) -> p t e", e=ne)
                count = s.up[2][:, 64:64 + ne]
                above, ntile, first = s.above[:, 0:ne, :], s.ntile[:, 0:ne], s.first[:, 0:ne]
                done(dve.tensor_tensor(above, count.unsqueeze(2).to_broadcast([P, ne, 4]),
                                       tile_at[:, 0:4].unsqueeze(1).to_broadcast([P, ne, 4]), ALU.is_gt))
                done(dve.tensor_reduce(ntile, above, AX, ALU.add))
                tri_n = s.tri_n[:, 0:ne, 0:ne]
                done(dve.tensor_tensor(tri_n, tri[:, 0:ne, 0:ne], ntile.unsqueeze(1).to_broadcast([P, ne, ne]), ALU.mult))
                done(dve.tensor_reduce(first, tri_n, AX, ALU.add))
                at = s.place[:, :, 0:ne]
                done(dve.tensor_tensor(at, rank, first.unsqueeze(1).to_broadcast([P, PAIRS, ne]), ALU.add))
                done(dve.tensor_tensor(at, at, s.onehot[:, :, 0:ne], ALU.mult))
                done(dve.tensor_reduce(s.red[:, 0, :], at, AX, ALU.add))
                dve.tensor_copy(s.place_i[:], s.red[:, 0, :]).then_inc(s.place_sb, 1)

            def place_tiles(h, l):
                s, ne, nt = halves[h], NE[l], TILES[l]
                first = s.first[:, 0:ne]
                begun = s.begun[:, 0:nt, 0:ne]
                done(dve.tensor_tensor(begun, tile_at[:, 0:nt].unsqueeze(2).to_broadcast([P, nt, ne]),
                                       first.unsqueeze(1).to_broadcast([P, nt, ne]), ALU.is_ge))
                done(dve.tensor_reduce(s.tile_e[:, 0:nt], begun, AX, ALU.add))
                done(dve.tensor_scalar(s.tile_e[:, 0:nt], s.tile_e[:, 0:nt], -1.0, None, ALU.add))
                done(dve.tensor_copy(s.tile_ei[:, 0:nt], s.tile_e[:, 0:nt]))
                dve.tensor_scalar(s.tile_row[:, 0:nt, :], s.tile_e[0:PARTS, 0:nt].unsqueeze(2).to_broadcast([PARTS, nt, P]),
                                  part_row[:], None, ALU.is_equal).then_inc(s.row_sb, 1)
                if l == 0:
                    dve.wait_ge(s.expo_sb, 1)
                    done(dve.tensor_reduce(s.red[:, 1, :], s.expo[:, :, 0:ne], AX, ALU.add))
                    done(dve.reciprocal(s.red[:, 2, :], s.red[:, 1, :]))
                    done(dve.tensor_scalar(s.wg[:], s.red[:, 2, :], gf[:, 0:1], None, ALU.mult))

            def turn_tiles(h, l, g):
                s, lo = halves[h], 4 * g * P
                if g % 2 == 0:
                    n = min(4 * P, TILES[l] * P - lo)
                    dve.wait_ge(s.xsT_ps, GROUP0[l] + g + 1)
                    dve.tensor_copy(s.xsT[:, lo:lo + n], s.up[g % 3][:, 0:n]).then_inc(s.xsT_dve, 1)

            def tile(h, l, i):
                s, g = halves[h], STEP0[l] + i
                if l == 2 and i < STEPS[2]:
                    dve.wait_ge(s.up_ps, g + 1)
                    dve.wait_ge(s.act_sb, g + 1)
                    if i >= 2:
                        dve.wait_ge(s.hidT_ps, g - 1)
                    dve.scalar_tensor_tensor(out=s.hidn[i % 2], in0=s.tht[i % 2], scalar=1.0, in1=s.up[1],
                                             op0=ALU.add, op1=ALU.mult).then_inc(s.hid_sb, 1)

            def tile_out(h, l, i):
                s, g = halves[h], STEP0[l] + i
                if i >= 2:
                    first = (i - 2) * PER[l]
                    k = min(PER[l], TILES[l] - first)
                    dve.wait_ge(s.down_ps, g - 1)
                    dve.tensor_copy(flat(s.ys[:, first:first + k, :]), s.y[:, 0:k * P]).then_inc(s.ys_sb, 1)

            def turn_route(h, l):
                s = halves[h]
                dve.wait_ge(s.route_ps, 3)
                c = s.up[2][0:E3, :]
                done(dve.tensor_copy(s.cparts[0:E3, :], c))
                done(dve.tensor_tensor(s.cleft[:, 0, :], c, s.cparts[0:E3, :], ALU.subtract))
                done(dve.tensor_copy(s.cparts[32:32 + E3, :], s.cleft[:, 0, :]))
                done(dve.tensor_copy(s.maskTb[:], s.cleft[:, 0, :]))
                done(dve.tensor_tensor(s.cleft[:, 1, :], s.cleft[:, 0, :], s.maskTb[:], ALU.subtract))
                dve.tensor_copy(s.cparts[64:64 + E3, :], s.cleft[:, 1, :]).then_inc(s.parts_sb, 1)

            def chunk(h, l, i):
                s = halves[h]
                if i >= C3:
                    return
                hb = s.hid[:, i % NH, :]
                dve.wait_ge(s.act_sb, STEPS3 + i + 1)
                dve.scalar_tensor_tensor(out=s.am[:, i % 2, :], in0=s.th[:, i % 2, :], scalar=1.0, in1=s.up[0],
                                         op0=ALU.add, op1=ALU.mult).then_inc(s.u3_sb, 1)
                dve.wait_ge(s.u3_sb, i + 1)
                dve.wait_ge(s.up_ps, STEPS3 + i + 1)
                if i >= NH:
                    dve.wait_ge(s.down_ps, STEPS3 + i - NH + 1)
                dve.tensor_tensor(hb, s.am[:, i % 2, :], s.up[1], ALU.mult).then_inc(s.v3_sb, 1)

            def chunk_weigh(h, l, i):
                s = halves[h]
                hb = s.hid[:, i % NH, :]
                if i < C3 - 1:
                    dve.wait_ge(s.v3_sb, i + 1)
                    dve.wait_ge(s.c3_ps, i + 1)
                    dve.tensor_tensor(hb, hb, s.up[2], ALU.mult).then_inc(s.hid_sb, 1)

            def mix(h, l):
                s = halves[h]
                dve.wait_ge(s.xT_sb, 2 * l + 2)
                x3 = s.xT[:].rearrange("p (b s) -> p b s", s=S)
                done(dve.memset(s.xprev[:, :, 0:1], 0.0))
                done(dve.tensor_copy(s.xprev[:, :, 1:S], x3[:, :, 0:S - 1]))
                for j, mu in enumerate(("mu_r", "mu_k")):
                    done(dve.tensor_scalar(s.hid[:, 2 + j, :], s.hid[:, 0, :], anti_mu[:, j:j + 1], None, ALU.mult))
                    dve.scalar_tensor_tensor(out=s.am[:, j, :], in0=s.xT[:], scalar=cols(mu), in1=s.hid[:, 2 + j, :],
                                             op0=ALU.mult, op1=ALU.add).then_inc(s.mix_sb, 1)
                dve.wait_ge(s.relu_sb, 2)
                dve.tensor_tensor(s.hid[:, 1, :], s.th[:, 1, :], s.up[1], ALU.mult).then_inc(s.ka_sb, 1)

            def mix_out(h, l):
                s = halves[h]
                dve.wait_ge(s.mix_ps, 3)
                dve.scalar_tensor_tensor(out=s.yT, in0=s.th[:, 0, :], scalar=1.0, in1=s.up[2],
                                         op0=ALU.add, op1=ALU.mult).then_inc(s.y_sb, 1)

            def ffn_out(h, l):
                s, xh = halves[h], part(x, h)
                if l in NE:
                    dve.wait_ge(s.gathered, 16 * PAIRS * (ROUTE0[l] + 1))
                else:
                    dve.wait_ge(s.yb_ps, l // 2 + 1)
                if l == 0:
                    for t in range(PAIRS):
                        last = dve.scalar_tensor_tensor(out=xh[:, t, :], in0=s.ytok[:, t, :],
                                                        scalar=s.wg[:, t:t + 1], in1=xh[:, t, :],
                                                        op0=ALU.mult, op1=ALU.add)
                else:
                    y = flat(s.ytok[:]) if l == 2 else s.up[0]
                    last = dve.scalar_tensor_tensor(out=flat(xh), in0=y, scalar=gf[:, l:l + 1], in1=flat(xh),
                                                    op0=ALU.mult, op1=ALU.add)
                last.then_inc(s.x_ffn, 1)

            steps = {"setup": setup, "attn_stats": attn_stats, "find": find, "scores": scores,
                     "scores/second": scores_second, "attend": attend,
                     "attn_out": attn_out, "ffn_stats": ffn_stats, "logits": logits, "place": place, "place/tiles": place_tiles,
                     "turn_tiles": turn_tiles, "tile": tile, "tile/out": tile_out, "turn_route": turn_route,
                     "chunk": chunk, "chunk/weigh": chunk_weigh, "mix": mix, "mix_out": mix_out, "ffn_out": ffn_out}
            for run, at in in_order(PLAN, "dve", steps):
                run(*at)


def kernel(**inputs):
    import numpy as _np
    import concourse.bacc as _bacc
    from concourse import mybir as _mybir
    from concourse.bass_utils import run_bass_kernel_spmd as _run

    nc = _bacc.Bacc("TRN2", target_bir_lowering=False, num_devices=1)
    arrays, aps = {}, {}
    for name in inputs:
        a = _np.ascontiguousarray(inputs[name])
        arrays[f"in_{name}_dram"] = a
        aps[name] = nc.dram_tensor(f"in_{name}_dram", a.shape, _mybir.dt.from_np(a.dtype), kind="ExternalInput").ap()
    out = nc.dram_tensor("out_0_dram", (B, S, D), F32, kind="ExternalOutput").ap()
    rows = [[nc.dram_tensor(f"{n}{h}_dram", (MAXT * P, D), F32, kind="Internal").ap() for h in range(HALVES)]
            for n in ("x_rows", "y_rows")]
    flamingo_kernel(nc, aps, out, *rows)
    r = _run(nc, [arrays], core_ids=[0])
    return r.results[0]["out_0_dram"]
```
